# Optimizing a Trainium2 kernel written in Bass

```python
import numpy as np
import jax
import jax.numpy as jnp

def _softmax(x, axis=-1):
    return jax.nn.softmax(x, axis=axis)

def _gelu(x):
    return jax.nn.gelu(x, approximate=True)

def _silu(x):
    return jax.nn.silu(x)

def _sigmoid(x):
    return jax.nn.sigmoid(x)

def _layernorm(x, axis=-1, eps=1e-05):
    m = jnp.mean(x, axis=axis, keepdims=True)
    v = jnp.var(x, axis=axis, keepdims=True)
    return (x - m) / jnp.sqrt(v + eps)

def _scatter_add(tgt, idx, src, axis=0):
    return tgt.at[idx].add(src)

def _segment_sum(src, seg, n):
    return jax.ops.segment_sum(src, seg, n)
kernel_name = 'mk_macaron_d2_jaxref_r8_ac9f55'

def setup_inputs(seed: int=0):
    np.random.seed(seed)
    _w = jnp.asarray

    def _L0_attn_setup():
        import jax, jax.numpy as jnp
        import numpy as np
        LOG_HALF = float(np.log(0.5))

        def log_g(x):
            return jnp.where(x >= 0.0, jnp.log(jnp.maximum(x, 0.0) + 0.5), -jax.nn.softplus(-x))
        key = jax.random.key(seed)
        k1, k2, k3, k4 = jax.random.split(key, 4)
        B, T, D, E = (4, 512, 128, 192)
        x = jax.random.normal(k1, (B, T, D), dtype=jnp.float32)
        W_f = jax.random.normal(k2, (2 * E, D), dtype=jnp.float32) * 0.02
        b_f = jax.random.normal(k3, (2 * E,), dtype=jnp.float32) * 0.02
        W_down = jax.random.normal(k4, (D, E), dtype=jnp.float32) * 0.02
        return {'x': x, 'W_f': W_f, 'b_f': b_f, 'W_down': W_down}
    _L0_attn_in = _L0_attn_setup()

    def _L0_ffn_setup():
        import jax, jax.numpy as jnp
        import numpy as np
        B, S, D, F, E, TOPK = (4, 256, 128, 512, 8, 2)

        def _moe_forward(x, W_router, W_gate, W_up, W_down):
            logits = jnp.einsum('bsd,ed->bse', x, W_router)
            probs = jax.nn.softmax(logits, axis=-1)
            gates, indices = jax.lax.top_k(probs, TOPK)
            gates = gates / jnp.sum(gates, axis=-1, keepdims=True)
            weights = jnp.sum(gates[..., None] * jax.nn.one_hot(indices, E, dtype=x.dtype), axis=-2)
            weights_e = jnp.moveaxis(weights, -1, 0)

            def body(acc, params):
                wg, wu, wd, wt = params
                gate = jax.nn.silu(jnp.einsum('bsd,fd->bsf', x, wg))
                up = jnp.einsum('bsd,fd->bsf', x, wu)
                y = jnp.einsum('bsf,df->bsd', gate * up, wd)
                return (acc + wt[..., None] * y, None)
            out, _ = jax.lax.scan(body, jnp.zeros_like(x), (W_gate, W_up, W_down, weights_e))
            return out
        key = jax.random.key(seed)
        k1, k2, k3, k4, k5 = jax.random.split(key, 5)
        x = jax.random.normal(k1, (B, S, D), dtype=jnp.float32)
        W_router = jax.random.normal(k2, (E, D), dtype=jnp.float32) / np.sqrt(D)
        W_gate = jax.random.normal(k3, (E, F, D), dtype=jnp.float32) / np.sqrt(D)
        W_up = jax.random.normal(k4, (E, F, D), dtype=jnp.float32) / np.sqrt(D)
        W_down = jax.random.normal(k5, (E, D, F), dtype=jnp.float32) / np.sqrt(F)
        return {'x': x, 'W_router': W_router, 'W_gate': W_gate, 'W_up': W_up, 'W_down': W_down}
    _L0_ffn_in = _L0_ffn_setup()

    def _L1_attn_setup():
        import jax, jax.numpy as jnp
        import numpy as np
        B, S, D, H = (2, 256, 128, 16)
        HD = D // H
        MAX_BIAS = 8.0

        def _alibi_bias(T, Sk, dtype):
            slopes = (2.0 ** (-MAX_BIAS / H)) ** jnp.arange(1, H + 1, dtype=dtype)
            qpos = jnp.arange(T)[:, None]
            kpos = jnp.arange(Sk)[None, :]
            rel = -jnp.abs(kpos - qpos).astype(dtype)
            return slopes[:, None, None] * rel[None]
        key = jax.random.key(seed)
        ks = jax.random.split(key, 5)
        sc = 1.0 / np.sqrt(D)
        return {'x': jax.random.normal(ks[0], (B, S, D), jnp.float32), 'Wq': jax.random.normal(ks[1], (D, D), jnp.float32) * sc, 'bq': jnp.zeros((D,), jnp.float32), 'Wk': jax.random.normal(ks[2], (D, D), jnp.float32) * sc, 'bk': jnp.zeros((D,), jnp.float32), 'Wv': jax.random.normal(ks[3], (D, D), jnp.float32) * sc, 'bv': jnp.zeros((D,), jnp.float32), 'Wo': jax.random.normal(ks[4], (D, D), jnp.float32) * sc, 'bo': jnp.zeros((D,), jnp.float32)}
    _L1_attn_in = _L1_attn_setup()

    def _L1_ffn_setup():
        import jax, jax.numpy as jnp
        import numpy as np
        TOPK = 4
        N_GROUPS = 4
        TOPK_GROUPS = 2
        ROUTE_SCALE = 2.5

        def _gate(x2, Wg):
            T = x2.shape[0]
            E = Wg.shape[0]
            scores = x2 @ Wg.T
            s = jax.nn.sigmoid(scores)
            g = s.reshape(T, N_GROUPS, E // N_GROUPS)
            group_scores = g.max(axis=-1)
            _, gidx = jax.lax.top_k(group_scores, TOPK_GROUPS)
            group_mask = jnp.any(jax.nn.one_hot(gidx, N_GROUPS, dtype=jnp.bool_), axis=1)
            masked = jnp.where(group_mask[:, :, None], g, -jnp.inf).reshape(T, E)
            _, idx = jax.lax.top_k(masked, TOPK)
            w = jnp.take_along_axis(s, idx, axis=1)
            w = w / jnp.sum(w, axis=-1, keepdims=True)
            w = w * ROUTE_SCALE
            return (w.astype(x2.dtype), idx)
        key = jax.random.key(seed)
        ks = jax.random.split(key, 6)
        B, S, D, I, E = (2, 256, 128, 128, 16)
        scale = 0.02
        return {'x': jax.random.normal(ks[0], (B, S, D), dtype=jnp.float32), 'Wg': jax.random.normal(ks[1], (E, D), dtype=jnp.float32) * scale, 'W1': jax.random.normal(ks[2], (E, I, D), dtype=jnp.float32) * scale, 'b1': jnp.zeros((E, I), dtype=jnp.float32), 'W2': jax.random.normal(ks[3], (E, D, I), dtype=jnp.float32) * scale, 'b2': jnp.zeros((E, D), dtype=jnp.float32), 'W3': jax.random.normal(ks[4], (E, I, D), dtype=jnp.float32) * scale, 'b3': jnp.zeros((E, I), dtype=jnp.float32)}
    _L1_ffn_in = _L1_ffn_setup()
    _d = {'L0_attn_x': _L0_attn_in['x'], 'L0_attn_W_f': _L0_attn_in['W_f'], 'L0_attn_b_f': _L0_attn_in['b_f'], 'L0_attn_W_down': _L0_attn_in['W_down'], 'L0_ffn_W_router': _L0_ffn_in['W_router'], 'L0_ffn_W_gate': _L0_ffn_in['W_gate'], 'L0_ffn_W_up': _L0_ffn_in['W_up'], 'L0_ffn_W_down': _L0_ffn_in['W_down'], 'L1_attn_Wq': _L1_attn_in['Wq'], 'L1_attn_bq': _L1_attn_in['bq'], 'L1_attn_Wk': _L1_attn_in['Wk'], 'L1_attn_bk': _L1_attn_in['bk'], 'L1_attn_Wv': _L1_attn_in['Wv'], 'L1_attn_bv': _L1_attn_in['bv'], 'L1_attn_Wo': _L1_attn_in['Wo'], 'L1_attn_bo': _L1_attn_in['bo'], 'L1_ffn_Wg': _L1_ffn_in['Wg'], 'L1_ffn_W1': _L1_ffn_in['W1'], 'L1_ffn_b1': _L1_ffn_in['b1'], 'L1_ffn_W2': _L1_ffn_in['W2'], 'L1_ffn_b2': _L1_ffn_in['b2'], 'L1_ffn_W3': _L1_ffn_in['W3'], 'L1_ffn_b3': _L1_ffn_in['b3']}
    _x0 = _d['L0_attn_x']
    _d['L0_attn_x'] = jax.random.normal(jax.random.fold_in(jax.random.key(seed), 1), (8, 256, 128), dtype=_x0.dtype)
    del _x0
    return _d

def reference(L0_attn_x, L0_attn_W_f, L0_attn_b_f, L0_attn_W_down, L0_ffn_W_router, L0_ffn_W_gate, L0_ffn_W_up, L0_ffn_W_down, L1_attn_Wq, L1_attn_bq, L1_attn_Wk, L1_attn_bk, L1_attn_Wv, L1_attn_bv, L1_attn_Wo, L1_attn_bo, L1_ffn_Wg, L1_ffn_W1, L1_ffn_b1, L1_ffn_W2, L1_ffn_b2, L1_ffn_W3, L1_ffn_b3):

    def _L0_attn_ref(x, W_f, b_f, W_down):
        import jax, jax.numpy as jnp
        import numpy as np
        LOG_HALF = float(np.log(0.5))

        def log_g(x):
            return jnp.where(x >= 0.0, jnp.log(jnp.maximum(x, 0.0) + 0.5), -jax.nn.softplus(-x))
        B, T, D = x.shape
        E = W_down.shape[1]
        kz, h_x = jnp.split(jnp.einsum('btd,ed->bte', x, W_f) + b_f, 2, axis=-1)
        log_z = -jax.nn.softplus(-kz)
        log_coeffs = -jax.nn.softplus(kz)
        log_tilde_h = log_g(h_x)
        log_h0 = jnp.full((B, 1, E), LOG_HALF, dtype=x.dtype)
        log_values = jnp.concatenate([log_h0, log_tilde_h + log_z], axis=1)
        a_star = jnp.concatenate([jnp.zeros((B, 1, E), dtype=x.dtype), jnp.cumsum(log_coeffs, axis=1)], axis=1)
        log_h = a_star + jax.lax.cumlogsumexp(log_values - a_star, axis=1)
        h = jnp.exp(log_h)[:, 1:]
        return jnp.einsum('bte,de->btd', h, W_down)

    def _L0_ffn_ref(x, W_router, W_gate, W_up, W_down):
        import jax, jax.numpy as jnp
        import numpy as np
        B, S, D, F, E, TOPK = (4, 256, 128, 512, 8, 2)

        def _moe_forward(x, W_router, W_gate, W_up, W_down):
            logits = jnp.einsum('bsd,ed->bse', x, W_router)
            probs = jax.nn.softmax(logits, axis=-1)
            gates, indices = jax.lax.top_k(probs, TOPK)
            gates = gates / jnp.sum(gates, axis=-1, keepdims=True)
            weights = jnp.sum(gates[..., None] * jax.nn.one_hot(indices, E, dtype=x.dtype), axis=-2)
            weights_e = jnp.moveaxis(weights, -1, 0)

            def body(acc, params):
                wg, wu, wd, wt = params
                gate = jax.nn.silu(jnp.einsum('bsd,fd->bsf', x, wg))
                up = jnp.einsum('bsd,fd->bsf', x, wu)
                y = jnp.einsum('bsf,df->bsd', gate * up, wd)
                return (acc + wt[..., None] * y, None)
            out, _ = jax.lax.scan(body, jnp.zeros_like(x), (W_gate, W_up, W_down, weights_e))
            return out
        return _moe_forward(x, W_router, W_gate, W_up, W_down)

    def _L1_attn_ref(x, Wq, bq, Wk, bk, Wv, bv, Wo, bo):
        import jax, jax.numpy as jnp
        import numpy as np
        B, S, D, H = (2, 256, 128, 16)
        HD = D // H
        MAX_BIAS = 8.0

        def _alibi_bias(T, Sk, dtype):
            slopes = (2.0 ** (-MAX_BIAS / H)) ** jnp.arange(1, H + 1, dtype=dtype)
            qpos = jnp.arange(T)[:, None]
            kpos = jnp.arange(Sk)[None, :]
            rel = -jnp.abs(kpos - qpos).astype(dtype)
            return slopes[:, None, None] * rel[None]
        Bb, Ss, Dd = x.shape
        q = (x @ Wq + bq).reshape(Bb, Ss, H, HD)
        k = (x @ Wk + bk).reshape(Bb, Ss, H, HD)
        v = (x @ Wv + bv).reshape(Bb, Ss, H, HD)
        scores = jnp.einsum('bthd,bshd->bhts', q, k) / jnp.sqrt(jnp.asarray(HD, x.dtype))
        alibi = _alibi_bias(Ss, Ss, x.dtype)
        causal = jnp.triu(jnp.ones((Ss, Ss), bool), 1)
        scores = scores + alibi[None]
        scores = jnp.where(causal[None, None], -jnp.inf, scores)
        attn = jax.nn.softmax(scores, axis=-1)
        out = jnp.einsum('bhts,bshd->bthd', attn, v).reshape(Bb, Ss, Dd)
        return out @ Wo + bo

    def _L1_ffn_ref(x, Wg, W1, b1, W2, b2, W3, b3):
        import jax, jax.numpy as jnp
        import numpy as np
        TOPK = 4
        N_GROUPS = 4
        TOPK_GROUPS = 2
        ROUTE_SCALE = 2.5

        def _gate(x2, Wg):
            T = x2.shape[0]
            E = Wg.shape[0]
            scores = x2 @ Wg.T
            s = jax.nn.sigmoid(scores)
            g = s.reshape(T, N_GROUPS, E // N_GROUPS)
            group_scores = g.max(axis=-1)
            _, gidx = jax.lax.top_k(group_scores, TOPK_GROUPS)
            group_mask = jnp.any(jax.nn.one_hot(gidx, N_GROUPS, dtype=jnp.bool_), axis=1)
            masked = jnp.where(group_mask[:, :, None], g, -jnp.inf).reshape(T, E)
            _, idx = jax.lax.top_k(masked, TOPK)
            w = jnp.take_along_axis(s, idx, axis=1)
            w = w / jnp.sum(w, axis=-1, keepdims=True)
            w = w * ROUTE_SCALE
            return (w.astype(x2.dtype), idx)
        shape = x.shape
        D = shape[-1]
        x2 = x.reshape(-1, D)
        weights, indices = _gate(x2, Wg)
        E = Wg.shape[0]
        y = jnp.zeros_like(x2)
        for e in range(E):
            we = jnp.sum(weights * (indices == e), axis=-1)
            h = jax.nn.silu(x2 @ W1[e].T + b1[e]) * (x2 @ W3[e].T + b3[e])
            y = y + (h @ W2[e].T + b2[e]) * we[:, None]
        return y.reshape(shape)
    x = L0_attn_x
    x = x + 0.5 * _L0_ffn_ref(_layernorm(x, axis=-1), L0_ffn_W_router, L0_ffn_W_gate, L0_ffn_W_up, L0_ffn_W_down)
    x = x + _L0_attn_ref(_layernorm(x, axis=-1), L0_attn_W_f, L0_attn_b_f, L0_attn_W_down)
    x = x + 0.5 * _L0_ffn_ref(_layernorm(x, axis=-1), L0_ffn_W_router, L0_ffn_W_gate, L0_ffn_W_up, L0_ffn_W_down)
    x = x + 0.5 * _L1_ffn_ref(_layernorm(x, axis=-1), L1_ffn_Wg, L1_ffn_W1, L1_ffn_b1, L1_ffn_W2, L1_ffn_b2, L1_ffn_W3, L1_ffn_b3)
    x = x + _L1_attn_ref(_layernorm(x, axis=-1), L1_attn_Wq, L1_attn_bq, L1_attn_Wk, L1_attn_bk, L1_attn_Wv, L1_attn_bv, L1_attn_Wo, L1_attn_bo)
    x = x + 0.5 * _L1_ffn_ref(_layernorm(x, axis=-1), L1_ffn_Wg, L1_ffn_W1, L1_ffn_b1, L1_ffn_W2, L1_ffn_b2, L1_ffn_W3, L1_ffn_b3)
    return x

_drawn_inputs = setup_inputs


def setup_inputs(seed=0):
    import zlib

    import numpy as np

    out = dict(_drawn_inputs(seed))
    spreads = {'L1_attn_bq': (0.0, 0.327),
     'L1_attn_bk': (0.0, 0.8),
     'L1_attn_bv': (0.0, 0.1),
     'L1_attn_bo': (0.0, 0.1),
     'L1_ffn_b1': (0.0, 0.8),
     'L1_ffn_b2': (0.0, 0.1),
     'L1_ffn_b3': (0.0, 0.8)}
    factors = {'L0_attn_b_f': 4.542, 'L1_ffn_W1': 7.728, 'L1_ffn_W2': 7.003, 'L1_ffn_W3': 7.846}
    for name, (base, spread) in spreads.items():
        noise = np.random.default_rng([zlib.crc32(name.encode()), seed]).standard_normal(out[name].shape)
        drawn = base * np.exp(spread * noise) if base else spread * noise
        out[name] = jnp.asarray(drawn.astype(out[name].dtype))
    for name, factor in factors.items():
        out[name] = (out[name] * factor).astype(out[name].dtype)
    return out
```

```python
from contextlib import ExitStack

import numpy as np
import concourse.bass as bass
import concourse.mybir as mybir

P = 128
TOK = 2048
SEQ = 256
CH = 4
CT = TOK // CH
TI = CT // P
NB = CT // SEQ
D = 128
E0, F0, FB = 8, 512, 4
E1 = 16
GR = 4
H, HD = 16, 8
HG = 4
EH = 192
MROW = 28
SCALE = 1.0 / float(np.sqrt(np.float32(HD)))
EPS = 1e-5
S0N, S1N = E0 * FB, E1
LAG = 3

C_ID, C_IOTA, C_TRI, C_MLQ, C_MLK, C_POW, C_EPS = 0, 128, 144, 160, 161, 162, 166
C_MASK1, C_MASK2, C_END = 170, 298, 426

JOBS = [("F1", c) for c in range(CH)] + [("F2", c) for c in range(CH)] \
     + [("G1", c) for c in range(CH)] + [("G2", c) for c in range(CH)]


def job_of(stage, c):
    return JOBS.index((stage, c))


def first_step(j):
    return S0N * min(j, 8) + S1N * max(j - 8, 0)


def steps(j):
    return S0N if j < 8 else S1N


def norm_pieces(stage, c):
    return [(n, stage, c) for n in ("ln_stats", "ln_rstd", "ln_scale", "ln_transpose", "ln_split")]


def route_pieces(stage, c):
    kind = "f" if stage[0] == "F" else "g"
    return norm_pieces(stage, c) + [("route_logits", stage, c), (f"route_{kind}1", stage, c),
                                    (f"route_{kind}2", stage, c), ("route_transpose", stage, c)]


def side_pieces(j):
    out = []
    if j < 3:
        out += route_pieces("F1", j + 1)
    if j == 0:
        return out
    stage, c = JOBS[j - 1]
    out += [("post_transpose", j - 1, 0), ("post_add", j - 1, 0)]
    if stage == "F1":
        out += norm_pieces("A", c)
        out += [("rec_project", c, 0), ("rec_gates", c, 0), ("rec_project", c, 1), ("rec_gates", c, 1),
                ("rec_down", c, 0), ("rec_add", c, 0)]
        out += route_pieces("F2", c)
    elif stage == "F2":
        out += route_pieces("G1", c)
    elif stage == "G1":
        out += norm_pieces("B", c)
        out += [("att_qk", c, i) for i in range(2 * HG)]
        for b in range(NB):
            out += [("att_v", c, b)]
            for g in range(HG):
                u = HG * b + g
                out += [("att_keys", c, u)]
                out += [("att_max", c, u, p) for p in range(3)] + [("att_shift", c, u)]
                out += [("att_exp", c, u, p) for p in range(3)] + [("att_pv", c, u)]
            for t in range(SEQ // P):
                out += [("att_gather", c, b, t), ("att_turn", c, b, t), ("att_out", c, b, t)]
        out += route_pieces("G2", c)
    return out


NORMS = [("F1", 0)] + [(p[1], p[2]) for j in range(len(JOBS)) for p in side_pieces(j) if p[0] == "ln_stats"]
ROUTES = [x for x in NORMS if x[0] in ("F1", "F2", "G1", "G2")]


def build(nc, x_d, const_d, wf_d, wg_d, ws_d, wa_d, wfd_d, wo_d, bf_d, b13_d, b2_d, aug_d, bv_d, bo_d, out_d):
    f32, f32r, bf16, u32 = mybir.dt.float32, mybir.dt.float32r, mybir.dt.bfloat16, mybir.dt.uint32
    ALU, ACT, AX = mybir.AluOpType, mybir.ActivationFunctionType, mybir.AxisListType
    ctx = ExitStack()
    with ctx:
        def sb(name, shape, dt=f32):
            return ctx.enter_context(nc.sbuf_tensor(name, shape, dt))

        def ps(name):
            return ctx.enter_context(nc.psum_tensor(name, [P, 512], f32))

        def sem(name):
            return ctx.enter_context(nc.semaphore(name))

        x = sb("x", [P, CH * TI, D])
        w_hi = sb("w_hi", [P, E0, 3 * F0], f32r)
        w_lo = sb("w_lo", [P, E0, 3 * F0], f32r)
        ws_hi = sb("ws_hi", [P, 536], f32r)
        ws_lo = sb("ws_lo", [P, 536], f32r)
        arena = sb("arena", [P, 2, 1536])
        n_hi = sb("n_hi", [P, TOK], f32r)
        n_lo = sb("n_lo", [P, TOK], f32r)
        a_hi = sb("a_hi", [P, CT], f32r)
        a_lo = sb("a_lo", [P, CT], f32r)
        nrm = sb("nrm", [P, TI, D])
        gate = sb("gate", [P, 3, CT])
        hid = sb("hid", [P, 3, CT])
        h_hi = sb("h_hi", [P, 4, CT], f32r)
        h_lo = sb("h_lo", [P, 4, CT], f32r)
        wbc = sb("wbc", [P, 4, CT])
        y_fm = sb("y_fm", [P, CT])
        wT = sb("wT", [E1, CT])
        wTm = sb("wTm", [E1, CT])
        vpad = sb("vpad", [P, SEQ // P, H, 32])
        k_one = sb("k_one", [P, 2, 4, SEQ], f32r)
        const = sb("const", [P, C_END])
        ident_b = sb("ident_b", [P, P], bf16)
        mask1_b = sb("mask1_b", [P, P], bf16)
        mask2_b = sb("mask2_b", [P, P], bf16)
        wfd = sb("wfd", [P, 2, D])
        wo = sb("wo", [P, D])
        bf = sb("bf", [P, 4])
        bf_neg = sb("bf_neg", [P, 4])
        bf_half = sb("bf_half", [P, 4])
        b13 = sb("b13", [P, 2, E1])
        b2 = sb("b2", [E1, D])
        bv = sb("bv", [P, D])
        bo = sb("bo", [1, D])
        ones_row = sb("ones_row", [1, P])
        stats = sb("stats", [P, TI, 6])
        mv = sb("mv", [P, TI, 2])
        rstd = sb("rstd", [P, TI])
        mpad = sb("mpad", [P, SEQ // P, P])
        rden = sb("rden", [P, H])
        o_tm = sb("o_tm", [P, H, HD])
        o_fm = sb("o_fm", [P, P])
        lg = sb("lg", [P, TI, E1])
        sc = sb("sc", [P, TI, E1])
        top = sb("top", [P, TI, 8])
        topi = sb("topi", [P, TI, 8], u32)
        topf = sb("topf", [P, TI, 8])
        hot = sb("hot", [P, TI, E1, 4])
        gmax = sb("gmax", [P, TI, GR])
        gcmp = sb("gcmp", [P, TI, GR, GR])
        gcmq = sb("gcmq", [P, TI, GR, GR])
        gsel = sb("gsel", [P, TI, GR])
        gsel1 = sb("gsel1", [P, TI, GR])
        wtm = sb("wtm", [P, TI, E1])
        gap = sb("gap", [P, TI])
        egap = sb("egap", [P, TI])
        gk = sb("gk", [P, TI, 2])
        den = sb("den", [P, TI])

        rec = arena[:, :, :].rearrange("p a n -> p (a n)")
        r_a, r_z, r_g = (rec[:, i * CT:(i + 1) * CT] for i in range(3))
        r_h = [rec[:, (3 + k) * CT:(4 + k) * CT] for k in range(2)]
        prob = rec[:, 0:3 * CT]
        o_pad = rec[:, 3 * CT:5 * CT].rearrange("p (g t) -> p g t", g=HG)
        wh = w_hi[:, 4:8, :].rearrange("p a n -> p (a n)")
        wl = w_lo[:, 4:8, :].rearrange("p a n -> p (a n)")
        q_r = wh[:, 0:2048].rearrange("p (g t) -> p g t", g=HG)
        k_r = wh[:, 2048:4096].rearrange("p (g t) -> p g t", g=HG)
        wa_hi, wa_lo = wh[:, 4096:4096 + 1152], wl[:, 4096:4096 + 1152]
        qs_r = wh[:, 5248:5248 + 512].rearrange("p (i t) -> p i t", i=2)
        qk_hi = wl[:, 0:1024].rearrange("p (i t) -> p i t", i=2)
        aug_hi, aug_lo, pos_r = wl[0:2, 1024:2048], wl[0:2, 2048:3072], wl[0:2, 3072:3584]

        ident = const[:, C_ID:C_ID + P]
        w_scr = nc.dram_tensor("w_scr", (len(JOBS), E1, CT), f32, kind="Internal").ap()

        pg = [ps(f"pg{i}") for i in range(2)]
        pu = [ps(f"pu{i}") for i in range(2)]
        pacc = ps("pacc")
        pa, pb, pc = ps("pa"), ps("pb"), ps("pc")

        consts_in, smalls_in, x_in = sem("consts_in"), sem("smalls_in"), [sem(f"x_in{i}") for i in range(CH)]
        staged = [sem(f"staged{i}") for i in range(2)]
        w_split = sem("w_split")
        ws_split = sem("ws_split")
        setup_dve = sem("setup_dve")
        dve_chain, pool_chain = sem("dve_chain"), sem("pool_chain")
        gate_mm, up_mm, down_mm = sem("gate_mm"), sem("up_mm"), sem("down_mm")
        silu_done, weighted, hid_done, hi_done, lo_done = (
            sem(n) for n in ("silu_done", "weighted", "hid_done", "hi_done", "lo_done"))
        wbc_in = [sem(f"wbc_in{i}") for i in range(4)]
        wTm_in, b2_mm = sem("wTm_in"), sem("b2_mm")
        y_out, y_turned, x_added = sem("y_out"), sem("y_turned"), sem("x_added")
        ln_mv, ln_rs, ln_nrm, ln_T, ln_hi, ln_lo = (
            sem(n) for n in ("ln_mv", "ln_rs", "ln_nrm", "ln_T", "ln_hi", "ln_lo"))
        lg_mm, lg_read, lg_act, act_exp, w_tm, wT_mm, wT_out, w_stored = (
            sem(n) for n in ("lg_mm", "lg_read", "lg_act", "act_exp", "w_tm", "wT_mm", "wT_out", "w_stored"))
        rec_mm, rec_sig, rec_h, rec_y, rec_x = (sem(n) for n in ("rec_mm", "rec_sig", "rec_h", "rec_y", "rec_x"))
        qk_mm, qk_rd, qk_res = sem("qk_mm"), sem("qk_rd"), sem("qk_res")
        v_mm, v_out = sem("v_mm"), sem("v_out")
        k_zero, k_apart = sem("k_zero"), sem("k_apart")
        s1_mm, s1_max, m_T, q_shift, s2_mm, s2_exp, pv_mm, pv_out = (
            sem(n) for n in ("s1_mm", "s1_max", "m_T", "q_shift", "s2_mm", "s2_exp", "pv_mm", "pv_out"))
        o_T, o_nrm, o_T2, o_T2out, att_y, att_x = (
            sem(n) for n in ("o_T", "o_nrm", "o_T2", "o_T2out", "att_y", "att_x"))
        stored = sem("stored")

        block = ctx.enter_context(nc.Block())

        smalls = [(wfd[:, :, :], wfd_d), (wo[:, :], wo_d), (bf[:, :], bf_d), (b13[:, :, :], b13_d), (b2[:, :], b2_d),
                  (bv[:, :], bv_d.to_broadcast([P, D])), (bo[:, :], bo_d)]

        def nth_norm(stage, c):
            return NORMS.index((stage, c)) + 1

        def nth_route(stage, c):
            return ROUTES.index((stage, c)) + 1

        def norm_target(stage, c):
            if stage in ("A", "B"):
                return a_hi[:, :], a_lo[:, :]
            return n_hi[:, c * CT:(c + 1) * CT], n_lo[:, c * CT:(c + 1) * CT]

        def x_ready(eng, stage, c):
            if stage == "F1":
                eng.wait_ge(x_in[c], 16)
            elif stage == "F2":
                eng.wait_ge(rec_x, c + 1)
            elif stage == "G2":
                eng.wait_ge(att_x, 4 * (c + 1))
            else:
                eng.wait_ge(x_added, {"A": 0, "G1": 4, "B": 8}[stage] + c + 1)

        def place(j):
            pieces = side_pieces(j)
            skip = 3 * (LAG + 1) if j else 0
            at = {}
            for k, piece in enumerate(pieces):
                at.setdefault(skip + k * (3 * steps(j) - skip) // len(pieces), []).append(piece)
            return at

        placed = [place(j) for j in range(len(JOBS))]

        def pieces_at(j, i, subs):
            return [piece for s in subs for piece in placed[j].get(3 * i + s, [])]

        @block.tensor
        def _(pe):
            def mm3(out, lh, ll, rh, rl, start=True, stop=True):
                nc.tensor.matmul(out, lh, rh, start=start, stop=False)
                nc.tensor.matmul(out, lh, rl, start=False, stop=False)
                return nc.tensor.matmul(out, ll, rh, start=False, stop=stop)

            reader = {"pa": None, "pb": None, "pc": None}

            def take(bank):
                if reader[bank] is not None:
                    pe.wait_ge(*reader[bank])

            def ln_transpose(stage, c):
                n = nth_norm(stage, c)
                pe.wait_ge(ln_nrm, n)
                take("pa")
                for t in range(TI):
                    last = nc.tensor.transpose(pa[:, t * P:(t + 1) * P], nrm[:, t, :], ident)
                last.then_inc(ln_T, 1)
                reader["pa"] = (ln_lo, n)

            def route_logits(stage, c):
                n = nth_norm(stage, c)
                e, off = (E0, 512) if stage[0] == "F" else (E1, 520)
                pe.wait_ge(ln_hi, n)
                pe.wait_ge(ln_lo, n)
                take("pb")
                for t in range(TI):
                    s = slice(c * CT + t * P, c * CT + (t + 1) * P)
                    last = mm3(pb[:, t * e:(t + 1) * e], n_hi[:, s], n_lo[:, s], ws_hi[:, off:off + e], ws_lo[:, off:off + e])
                last.then_inc(lg_mm, 1)
                reader["pb"] = (lg_read, nth_route(stage, c))

            def route_transpose(stage, c):
                n = nth_route(stage, c)
                e = E0 if stage[0] == "F" else E1
                pe.wait_ge(w_tm, n)
                take("pb")
                for t in range(TI):
                    last = nc.tensor.transpose(pb[0:e, t * P:(t + 1) * P], wtm[:, t, 0:e], ident)
                last.then_inc(wT_mm, 1)
                reader["pb"] = (wT_out, n)

            def post_transpose(j, _):
                pe.wait_ge(y_out, j + 1)
                take("pc")
                for t in range(TI):
                    last = nc.tensor.transpose(pc[:, t * P:(t + 1) * P], y_fm[:, t * P:(t + 1) * P], ident)
                last.then_inc(y_turned, 1)
                reader["pc"] = (x_added, j + 1)

            def rec_project(c, k):
                pe.wait_ge(ln_hi, nth_norm("A", c))
                pe.wait_ge(ln_lo, nth_norm("A", c))
                for i, (name, bank) in enumerate((("pa", pa), ("pb", pb))):
                    take(name)
                    o = (2 * k + i) * P
                    last = mm3(bank[:, :], ws_hi[:, o:o + P], ws_lo[:, o:o + P], a_hi[:, :], a_lo[:, :])
                    reader[name] = (rec_sig, 3 * (2 * c + k) + 2) if i == 0 else (rec_h, 2 * c + k + 1)
                last.then_inc(rec_mm, 1)

            def rec_down(c, _):
                pe.wait_ge(rec_h, 2 * (c + 1))
                take("pc")
                for t in range(TI):
                    s = slice(t * P, (t + 1) * P)
                    nc.tensor.matmul(pc[:, s], r_h[0][:, s], wfd[:, 0, :], start=True, stop=False)
                    last = nc.tensor.matmul(pc[:, s], r_h[1][0:EH - P, s], wfd[0:EH - P, 1, :], start=False, stop=True)
                last.then_inc(rec_y, 1)
                reader["pc"] = (rec_x, c + 1)

            def att_qk(c, i):
                if i == 0:
                    pe.wait_ge(ln_hi, nth_norm("B", c))
                    pe.wait_ge(ln_lo, nth_norm("B", c))
                    pe.wait_ge(w_split, E0 + 6)
                g, what = i // 2, i % 2
                name, bank = (("pa", pa), ("pb", pb))[what]
                take(name)
                o = (what * HG + g) * P
                mm3(bank[:, :], wa_hi[:, o:o + P], wa_lo[:, o:o + P], a_hi[:, :], a_lo[:, :], stop=False)
                nc.tensor.matmul(bank[:, :], aug_hi[:, o:o + P], pos_r, start=False, stop=False)
                nc.tensor.matmul(bank[:, :], aug_lo[:, o:o + P], pos_r, start=False, stop=True).then_inc(qk_mm, 1)
                reader[name] = (qk_res, 8 * c + i + 1)

            def att_v(c, b):
                take("pc")
                for t in range(SEQ // P):
                    s = slice(b * SEQ + t * P, b * SEQ + (t + 1) * P)
                    last = mm3(pc[:, t * P:(t + 1) * P], a_hi[:, s], a_lo[:, s], wa_hi[:, 1024:1152], wa_lo[:, 1024:1152])
                last.then_inc(v_mm, 1)
                reader["pc"] = (v_out, 2 * c + b + 1)

            def att_max(c, u, p):
                b, g = divmod(u, HG)
                nth = 3 * (8 * c + u) + p
                name, bank = (("pa", pa), ("pb", pb))[nth % 2]
                if p == 0:
                    pe.wait_ge(k_apart, 2 * (8 * c + u + 1))
                take(name)
                heads = range(4) if p == 0 else range(2 * p - 2, 2 * p)
                w = P if p == 0 else SEQ
                for i, h in enumerate(heads):
                    t0 = b * SEQ + (0 if p == 0 else P)
                    nc.tensor.matmul(bank[:, i * w:(i + 1) * w], q_r[:, g, t0:t0 + P],
                                     k_one[:, u % 2, h, 0:w], start=True, stop=False)
                    last = nc.tensor.matmul(bank[:, (i + 1) * w - P:(i + 1) * w], ident_b[:, :], mask1_b[:, :],
                                            start=False, stop=True)
                last.then_inc(s1_mm, 1)
                reader[name] = (s1_max, nth + 1)

            def att_shift(c, u):
                pe.wait_ge(s1_max, 3 * (8 * c + u + 1))
                take("pc")
                for t in range(SEQ // P):
                    last = nc.tensor.transpose(pc[:, t * P:(t + 1) * P], mpad[:, t, :], ident)
                last.then_inc(m_T, 1)
                reader["pc"] = (q_shift, 8 * c + u + 1)

            def att_exp(c, u, p):
                b, g = divmod(u, HG)
                nth = 3 * (8 * c + u) + p
                name, bank = (("pa", pa), ("pb", pb))[(nth + 1) % 2]
                if p == 0:
                    pe.wait_ge(q_shift, 8 * c + u + 1)
                take(name)
                heads = range(4) if p == 2 else range(2 * p, 2 * p + 2)
                w = P if p == 2 else SEQ
                for i, h in enumerate(heads):
                    s0 = P if p == 2 else 0
                    nc.tensor.matmul(bank[:, i * w:(i + 1) * w], k_one[:, u % 2, h, s0:s0 + P],
                                     qs_r[:, u % 2, SEQ - w:SEQ], start=True, stop=False)
                    last = nc.tensor.matmul(bank[:, i * w:i * w + P], ident_b[:, :], mask2_b[:, :],
                                            start=False, stop=True)
                last.then_inc(s2_mm, 1)
                reader[name] = (s2_exp, nth + 1)

            def att_pv(c, u):
                b, g = divmod(u, HG)
                pe.wait_ge(s2_exp, 3 * (8 * c + u + 1))
                if g == 0:
                    pe.wait_ge(v_out, 2 * c + b + 1)
                take("pc")
                for h in range(4):
                    o = pc[32 * h:32 * h + 32, 0:SEQ]
                    hh = 4 * g + h
                    nc.tensor.matmul(o, vpad[:, 0, hh, :], prob[:, h * SEQ:(h + 1) * SEQ], start=True, stop=False)
                    last = nc.tensor.matmul(pc[32 * h:32 * h + 32, P:SEQ], vpad[:, 1, hh, :],
                                            prob[:, 4 * SEQ + h * P:4 * SEQ + (h + 1) * P], start=False, stop=True)
                last.then_inc(pv_mm, 1)
                reader["pc"] = (pv_out, 8 * c + u + 1)

            def att_gather(c, b, t):
                k = 2 * (2 * c + b) + t
                pe.wait_ge(pv_out, 4 * (2 * c + b + 1))
                take("pc")
                for g in range(HG):
                    last = nc.tensor.transpose(pc[:, g * P:(g + 1) * P], o_pad[:, g, t * P:(t + 1) * P], ident)
                last.then_inc(o_T, 1)
                reader["pc"] = (o_nrm, k + 1)

            def att_turn(c, b, t):
                k = 2 * (2 * c + b) + t
                take("pc")
                nc.tensor.transpose(pc[:, 0:P], o_tm[:, :, :].rearrange("p h d -> p (h d)"), ident).then_inc(o_T2, 1)
                reader["pc"] = (o_T2out, k + 1)

            def att_out(c, b, t):
                k = 2 * (2 * c + b) + t
                take("pc")
                nc.tensor.matmul(pc[:, 0:P], o_fm[:, :], wo[:, :], start=True, stop=False)
                nc.tensor.matmul(pc[:, 0:P], ones_row[:, :], bo[:, :], start=False, stop=True).then_inc(att_y, 1)
                reader["pc"] = (att_x, k + 1)

            mine = dict(ln_transpose=ln_transpose, route_logits=route_logits, route_transpose=route_transpose,
                        post_transpose=post_transpose, rec_project=rec_project, rec_down=rec_down, att_qk=att_qk,
                        att_v=att_v, att_max=att_max, att_shift=att_shift, att_exp=att_exp, att_pv=att_pv,
                        att_gather=att_gather, att_turn=att_turn, att_out=att_out)

            def run(j, i, sub):
                for name, *args in pieces_at(j, i, [sub]):
                    if name in mine:
                        mine[name](*args)

            def weights(j, i):
                if j < 8:
                    e, f = divmod(i, FB)
                    part = lambda w, k: w[:, e, k * F0 + f * P:k * F0 + (f + 1) * P]
                    return [(part(w_hi, k), part(w_lo, k)) for k in range(3)], e + 1
                q, r = divmod(i, 4)
                part = lambda w, k: w[:, q, r * 3 * P + k * P:r * 3 * P + (k + 1) * P]
                return [(part(w_hi, k), part(w_lo, k)) for k in range(3)], E0 + q + 1

            def down(n):
                j = n // S0N if n < 8 * S0N else 8 + (n - 8 * S0N) // S1N
                i = n - first_step(j)
                if i == 0 and j:
                    pe.wait_ge(y_out, j)
                first = i == 0
                if first and j >= 8:
                    pe.wait_ge(wTm_in, 16 * (j - 7))
                    nc.tensor.matmul(pacc[:, :], b2[:, :], wTm[:, :], start=True, stop=False).then_inc(b2_mm, 1)
                    first = False
                w, _ = weights(j, i)
                pe.wait_ge(lo_done, n + 1)
                mm3(pacc[:, :], w[2][0], w[2][1], h_hi[:, n % 4, :], h_lo[:, n % 4, :], start=first,
                    stop=i == steps(j) - 1).then_inc(down_mm, 1)

            pe.wait_ge(consts_in, 16)
            pe.wait_ge(ws_split, 1)
            pe.wait_ge(setup_dve, 1)
            for name, *args in route_pieces("F1", 0):
                if name in mine:
                    mine[name](*args)
            for j in range(len(JOBS)):
                c = JOBS[j][1]
                s = slice(c * CT, (c + 1) * CT)
                pe.wait_ge(ln_lo, nth_norm(*JOBS[j]))
                for i in range(steps(j)):
                    n = first_step(j) + i
                    w, split = weights(j, i)
                    pe.wait_ge(w_split, split)
                    if n >= 2:
                        pe.wait_ge(silu_done, n - 1)
                    mm3(pg[n % 2][:, :], *w[0], n_hi[:, s], n_lo[:, s]).then_inc(gate_mm, 1)
                    run(j, i, 0)
                    if n >= 2:
                        pe.wait_ge(hid_done, n - 1)
                    mm3(pu[n % 2][:, :], *w[1], n_hi[:, s], n_lo[:, s]).then_inc(up_mm, 1)
                    run(j, i, 1)
                    if n >= LAG:
                        down(n - LAG)
                    run(j, i, 2)
            total = first_step(len(JOBS))
            for n in range(total - LAG, total):
                down(n)
            post_transpose(len(JOBS) - 1, 0)

        @block.scalar
        def _(act):
            def ln_split(stage, c):
                n = nth_norm(stage, c)
                act.wait_ge(ln_T, n)
                nc.scalar.activation(norm_target(stage, c)[0], pa[:, :], ACT.Copy).then_inc(ln_hi, 1)

            def route_f1(stage, c):
                act.wait_ge(lg_act, nth_route(stage, c))
                nc.scalar.activation(egap[:, :], gap[:, :], ACT.Exp).then_inc(act_exp, 1)

            def route_g1(stage, c):
                act.wait_ge(lg_mm, nth_route(stage, c))
                nc.scalar.activation(lg[:, :, :], pb[:, 0:TI * E1].rearrange("p (t e) -> p t e", t=TI), ACT.Exp,
                                     scale=-1.0).then_inc(lg_read, 1)

            def route_transpose(stage, c):
                n = nth_route(stage, c)
                e = E0 if stage[0] == "F" else E1
                act.wait_ge(wT_mm, n)
                if n > 1:
                    act.wait_ge(w_stored, 16 * (n - 1))
                nc.scalar.activation(wT[0:e, :], pb[0:e, :], ACT.Copy).then_inc(wT_out, 1)
                act.wait_ge(wT_out, n)
                act.dma_start(w_scr[job_of(stage, c), 0:e, :], wT[0:e, :]).then_inc(w_stored, 16)

            def rec_gates(c, k):
                m = 2 * c + k
                act.wait_ge(rec_mm, m + 1)
                if m:
                    act.wait_ge(rec_h, m)
                else:
                    act.wait_ge(w_split, E0)
                nc.scalar.activation(r_a, pa[:, :], ACT.Sigmoid, bias=bf_neg[:, 2 * k:2 * k + 1],
                                     scale=-1.0).then_inc(rec_sig, 1)
                nc.scalar.activation(r_z, pa[:, :], ACT.Sigmoid, bias=bf[:, 2 * k:2 * k + 1]).then_inc(rec_sig, 1)
                nc.scalar.activation(r_g, pb[:, :], ACT.Sigmoid, bias=bf[:, 2 * k + 1:2 * k + 2]).then_inc(rec_sig, 1)

            def att_qk(c, i):
                g, what = i // 2, i % 2
                act.wait_ge(qk_mm, 8 * c + i + 1)
                nth = 8 * c + i
                if nth >= 2:
                    act.wait_ge(qk_res, nth - 1)
                nc.scalar.activation(qk_hi[:, i % 2, :], (pa, pb)[what][:, :], ACT.Copy).then_inc(qk_rd, 1)

            def att_keys(c, u):
                b, g = divmod(u, HG)
                act.wait_ge(qk_res, 8 * c + 2 * g + 2)
                act.wait_ge(k_zero, 1)
                if 8 * c + u >= 2:
                    act.wait_ge(s2_mm, 3 * (8 * c + u - 1))
                for h in (0, 1):
                    r = slice(32 * h, 32 * h + 32)
                    last = nc.scalar.activation(k_one[r, u % 2, h, :], k_r[r, g, b * SEQ:(b + 1) * SEQ].bitcast(f32), ACT.Copy)
                last.then_inc(k_apart, 1)

            def att_exp(c, u, p):
                nth = 3 * (8 * c + u) + p
                bank = (pa, pb)[(nth + 1) % 2]
                act.wait_ge(s2_mm, nth + 1)
                if p == 0 and 8 * c + u:
                    act.wait_ge(pv_mm, 8 * c + u)
                nc.scalar.activation(prob[:, p * CT:(p + 1) * CT], bank[:, :], ACT.Exp, scale=SCALE).then_inc(s2_exp, 1)

            def att_pv(c, u):
                g = u % HG
                act.wait_ge(pv_mm, 8 * c + u + 1)
                if g == 0 and 8 * c + u:
                    act.wait_ge(o_T, 2 * ((8 * c + u) // HG))
                nc.scalar.activation(o_pad[:, g, :], pc[:, 0:SEQ], ACT.Copy).then_inc(pv_out, 1)

            def att_turn(c, b, t):
                k = 2 * (2 * c + b) + t
                act.wait_ge(o_T2, k + 1)
                if k:
                    act.wait_ge(att_y, k)
                nc.scalar.activation(o_fm[:, :], pc[:, 0:P], ACT.Copy).then_inc(o_T2out, 1)

            mine = dict(ln_split=ln_split, route_f1=route_f1, route_g1=route_g1, route_transpose=route_transpose,
                        rec_gates=rec_gates, att_qk=att_qk, att_keys=att_keys, att_exp=att_exp, att_pv=att_pv, att_turn=att_turn)

            def round_hidden(n):
                act.wait_ge(hid_done, n + 1)
                if n >= 4:
                    act.wait_ge(down_mm, n - 3)
                nc.scalar.activation(h_hi[:, n % 4, :], hid[:, n % 3, :], ACT.Copy).then_inc(hi_done, 1)

            def take_sum(j):
                act.wait_ge(down_mm, first_step(j + 1))
                if j:
                    act.wait_ge(y_turned, j)
                nc.scalar.activation(y_fm[:, :], pacc[:, :], ACT.Copy).then_inc(y_out, 1)

            act.wait_ge(smalls_in, 16 * len(smalls))
            for name, *args in route_pieces("F1", 0):
                if name in mine:
                    mine[name](*args)
            for j in range(len(JOBS)):
                for i in range(steps(j)):
                    n = first_step(j) + i
                    if j and i == LAG:
                        take_sum(j - 1)
                    act.wait_ge(gate_mm, n + 1)
                    if n >= 3:
                        act.wait_ge(hid_done, n - 2)
                    bias = b13[:, 0, i:i + 1] if j >= 8 else 0.0
                    nc.scalar.activation(gate[:, n % 3, :], pg[n % 2][:, :], ACT.Silu, bias=bias).then_inc(silu_done, 1)
                    for name, *args in pieces_at(j, i, (0, 1, 2)):
                        if name in mine:
                            mine[name](*args)
                    if n:
                        round_hidden(n - 1)
            round_hidden(first_step(len(JOBS)) - 1)
            take_sum(len(JOBS) - 1)

        @block.gpsimd
        def _(pool):
            chain = [0]

            def link(ins):
                chain[0] += 1
                ins.then_inc(pool_chain, 1)
                pool.wait_ge(pool_chain, chain[0])

            def ln_rstd(stage, c):
                n = nth_norm(stage, c)
                pool.wait_ge(ln_mv, n)
                link(nc.gpsimd.tensor_tensor(rstd[:, :], mv[:, :, 1], const[:, C_EPS:C_EPS + TI], ALU.add))
                nc.gpsimd.tensor_tensor(rstd[:, :], rstd[:, :], const[:, C_POW:C_POW + TI], ALU.pow).then_inc(ln_rs, 1)

            mine = dict(ln_rstd=ln_rstd)
            pool.wait_ge(consts_in, 16)
            for name, *args in route_pieces("F1", 0):
                if name in mine:
                    mine[name](*args)
            for j in range(len(JOBS)):
                for i in range(steps(j)):
                    n = first_step(j) + i
                    pool.wait_ge(silu_done, n + 1)
                    if j < 8:
                        load = n // FB
                    else:
                        load = 8 * E0 + (n - 8 * S0N)
                    pool.wait_ge(wbc_in[load % 4], 16 * (load // 4 + 1))
                    nc.gpsimd.tensor_tensor(gate[:, n % 3, :], gate[:, n % 3, :], wbc[:, load % 4, :],
                                            ALU.mult).then_inc(weighted, 1)
                    for name, *args in pieces_at(j, i, (0, 1, 2)):
                        if name in mine:
                            mine[name](*args)

        @block.vector
        def _(dve):
            chain = [0]

            def link(ins):
                chain[0] += 1
                ins.then_inc(dve_chain, 1)
                dve.wait_ge(dve_chain, chain[0])

            tt, ts = nc.vector.tensor_tensor, nc.vector.tensor_scalar

            def ln_stats(stage, c):
                n = nth_norm(stage, c)
                x_ready(dve, stage, c)
                if n > 1:
                    dve.wait_ge(ln_rs, n - 1)
                for t in range(TI):
                    last = nc.vector.bn_stats(stats[:, t, :], x[:, c * TI + t, :])
                link(last)
                for t in range(TI):
                    last = nc.vector.bn_aggr(mv[:, t, :], stats[:, t, :])
                last.then_inc(ln_mv, 1)

            def ln_scale(stage, c):
                n = nth_norm(stage, c)
                dve.wait_ge(ln_rs, n)
                dve.wait_ge(ln_mv, n)
                if n > 1:
                    dve.wait_ge(ln_T, n - 1)
                for t in range(TI):
                    last = ts(nrm[:, t, :], x[:, c * TI + t, :], mv[:, t, 0:1], rstd[:, t:t + 1], ALU.subtract, ALU.mult)
                last.then_inc(ln_nrm, 1)

            def ln_split(stage, c):
                n = nth_norm(stage, c)
                dve.wait_ge(ln_hi, n)
                hi, lo = norm_target(stage, c)
                tt(lo, pa[:, :], hi.bitcast(f32), ALU.subtract).then_inc(ln_lo, 1)

            def top_of(values, e):
                for t in range(TI):
                    last = nc.vector.max(top[:, t, :], values[:, t, 0:e])
                link(last)
                for t in range(TI):
                    last = nc.vector.max_index(topi[:, t, :], top[:, t, :], values[:, t, 0:e])
                link(last)
                link(nc.vector.tensor_copy(topf[:, :, :], topi[:, :, :]))

            def places(e, k):
                iota = const[:, C_IOTA:C_IOTA + e].unsqueeze(1).unsqueeze(3).to_broadcast([P, TI, e, k])
                want = topf[:, :, 0:k].unsqueeze(2).to_broadcast([P, TI, e, k])
                link(tt(hot[:, :, 0:e, 0:k], iota, want, ALU.is_equal))

            def route_f1(stage, c):
                n = nth_route(stage, c)
                dve.wait_ge(lg_mm, n)
                nc.vector.tensor_copy(lg[:, :, 0:E0], pb[:, 0:TI * E0].rearrange("p (t e) -> p t e", t=TI)).then_inc(lg_read, 1)
                dve.wait_ge(lg_read, n)
                top_of(lg, E0)
                tt(gap[:, :], top[:, :, 1], top[:, :, 0], ALU.subtract).then_inc(lg_act, 1)
                places(E0, 2)

            def route_f2(stage, c):
                n = nth_route(stage, c)
                dve.wait_ge(act_exp, n)
                link(ts(den[:, :], egap[:, :], 1.0, None, ALU.add))
                link(nc.vector.reciprocal(gk[:, :, 0], den[:, :]))
                link(tt(gk[:, :, 1], gk[:, :, 0], egap[:, :], ALU.mult))
                link(tt(hot[:, :, 0:E0, 0:2], hot[:, :, 0:E0, 0:2],
                        gk[:, :, :].unsqueeze(2).to_broadcast([P, TI, E0, 2]), ALU.mult))
                if n > 1:
                    dve.wait_ge(wT_mm, n - 1)
                nc.vector.tensor_reduce(wtm[:, :, 0:E0], hot[:, :, 0:E0, 0:2], AX.X, ALU.add).then_inc(w_tm, 1)

            def route_g1(stage, c):
                n = nth_route(stage, c)
                dve.wait_ge(lg_read, n)
                link(ts(lg[:, :, :], lg[:, :, :], 1.0, None, ALU.add))
                link(nc.vector.reciprocal(sc[:, :, :], lg[:, :, :]))
                s4 = sc[:, :, :].rearrange("p t (g e) -> p t g e", g=GR)
                link(nc.vector.tensor_reduce(gmax[:, :, :], s4, AX.X, ALU.max))
                other = gmax[:, :, :].unsqueeze(2).to_broadcast([P, TI, GR, GR])
                own = gmax[:, :, :].unsqueeze(3).to_broadcast([P, TI, GR, GR])
                before = const[:, C_TRI:C_TRI + GR * GR].rearrange("p (a b) -> p a b", a=GR).unsqueeze(1) \
                    .to_broadcast([P, TI, GR, GR])
                link(tt(gcmp[:, :, :, :], other, own, ALU.is_gt))
                link(tt(gcmq[:, :, :, :], other, own, ALU.is_equal))
                link(tt(gcmq[:, :, :, :], gcmq[:, :, :, :], before, ALU.mult))
                link(tt(gcmp[:, :, :, :], gcmp[:, :, :, :], gcmq[:, :, :, :], ALU.add))
                link(nc.vector.tensor_reduce(gsel[:, :, :], gcmp[:, :, :, :], AX.X, ALU.add))
                link(ts(gsel[:, :, :], gsel[:, :, :], 1.5, None, ALU.is_lt))
                link(ts(gsel1[:, :, :], gsel[:, :, :], 1.0, None, ALU.subtract))
                m4 = lg[:, :, :].rearrange("p t (g e) -> p t g e", g=GR)
                link(tt(m4, s4, gsel[:, :, :].unsqueeze(3).to_broadcast([P, TI, GR, 4]), ALU.mult))
                link(tt(m4, m4, gsel1[:, :, :].unsqueeze(3).to_broadcast([P, TI, GR, 4]), ALU.add))

            def route_g2(stage, c):
                n = nth_route(stage, c)
                top_of(lg, E1)
                places(E1, 4)
                link(nc.vector.tensor_reduce(lg[:, :, :], hot[:, :, :, :], AX.X, ALU.add))
                link(tt(sc[:, :, :], sc[:, :, :], lg[:, :, :], ALU.mult))
                link(nc.vector.tensor_reduce(den[:, :], sc[:, :, :], AX.X, ALU.add))
                link(nc.vector.reciprocal(gap[:, :], den[:, :]))
                link(ts(gap[:, :], gap[:, :], 2.5, None, ALU.mult))
                dve.wait_ge(wT_mm, n - 1)
                tt(wtm[:, :, :], sc[:, :, :], gap[:, :].unsqueeze(2).to_broadcast([P, TI, E1]), ALU.mult).then_inc(w_tm, 1)

            def post_add(j, _):
                c = JOBS[j][1]
                dve.wait_ge(y_turned, j + 1)
                xs = x[:, c * TI:(c + 1) * TI, :].rearrange("p t d -> p (t d)")
                nc.vector.scalar_tensor_tensor(xs, pc[:, :], 0.5, xs, ALU.mult, ALU.add).then_inc(x_added, 1)

            def rec_gates(c, k):
                m = 2 * c + k
                dve.wait_ge(rec_sig, 3 * (m + 1))
                link(nc.vector.scalar_tensor_tensor(r_g, pb[:, :], bf_half[:, 2 * k + 1:2 * k + 2], r_g, ALU.add, ALU.max))
                link(tt(r_g, r_g, r_z, ALU.mult))
                if c:
                    dve.wait_ge(rec_y, c)
                for b in range(NB):
                    s = slice(b * SEQ, (b + 1) * SEQ)
                    last = nc.vector.tensor_tensor_scan(r_h[k][:, s], r_a[:, s], r_g[:, s], 0.5, ALU.mult, ALU.add)
                last.then_inc(rec_h, 1)

            def rec_add(c, _):
                dve.wait_ge(rec_y, c + 1)
                xs = x[:, c * TI:(c + 1) * TI, :].rearrange("p t d -> p (t d)")
                tt(xs, pc[:, :], xs, ALU.add).then_inc(rec_x, 1)

            def att_qk(c, i):
                g, what = i // 2, i % 2
                dve.wait_ge(qk_rd, 8 * c + i + 1)
                if c:
                    dve.wait_ge(pv_mm, 8 * c)
                ml = const[:, (C_MLQ, C_MLK)[what]:(C_MLQ, C_MLK)[what] + 1]
                nc.vector.scalar_tensor_tensor((q_r, k_r)[what][:, g, :], qk_hi[:, i % 2, :].bitcast(f32), ml,
                                               (pa, pb)[what][:, :], ALU.mult, ALU.add).then_inc(qk_res, 1)

            def att_v(c, b):
                dve.wait_ge(v_mm, 2 * c + b + 1)
                if 2 * c + b:
                    dve.wait_ge(pv_mm, 4 * (2 * c + b))
                for t in range(SEQ // P):
                    last = tt(vpad[:, t, :, 0:HD], pc[:, t * P:(t + 1) * P].rearrange("p (h d) -> p h d", h=H),
                              bv[:, :].rearrange("p (h d) -> p h d", h=H), ALU.add)
                last.then_inc(v_out, 1)

            def att_keys(c, u):
                b, g = divmod(u, HG)
                dve.wait_ge(qk_res, 8 * c + 2 * g + 2)
                dve.wait_ge(k_zero, 1)
                if 8 * c + u >= 2:
                    dve.wait_ge(s2_mm, 3 * (8 * c + u - 1))
                for h in (2, 3):
                    r = slice(32 * h, 32 * h + 32)
                    last = nc.vector.tensor_copy(k_one[r, u % 2, h, :], k_r[r, g, b * SEQ:(b + 1) * SEQ])
                last.then_inc(k_apart, 1)

            def att_max(c, u, p):
                nth = 3 * (8 * c + u) + p
                bank = (pa, pb)[nth % 2]
                dve.wait_ge(s1_mm, nth + 1)
                if p == 0 and 8 * c + u:
                    dve.wait_ge(m_T, 8 * c + u)
                k, w = (4, P) if p == 0 else (2, SEQ)
                h0 = 0 if p < 2 else 2
                out = mpad[:, min(p, 1), :].rearrange("p (h r) -> p h r", r=32)[:, h0:h0 + k, MROW]
                nc.vector.tensor_reduce(out, bank[:, :].rearrange("p (h w) -> p h w", w=w), AX.X, ALU.max,
                                        negate=True).then_inc(s1_max, 1)

            def att_shift(c, u):
                b, g = divmod(u, HG)
                dve.wait_ge(m_T, 8 * c + u + 1)
                if 8 * c + u >= 2:
                    dve.wait_ge(s2_mm, 3 * (8 * c + u - 1))
                tt(qs_r[:, u % 2, :], pc[:, 0:SEQ], q_r[:, g, b * SEQ:(b + 1) * SEQ].bitcast(f32), ALU.add).then_inc(q_shift, 1)

            def att_gather(c, b, t):
                k = 2 * (2 * c + b) + t
                dve.wait_ge(o_T, k + 1)
                heads = pc[:, :].rearrange("p (h r) -> p h r", r=32)
                link(nc.vector.reciprocal(rden[:, :], heads[:, :, HD]))
                if k:
                    dve.wait_ge(o_T2, k)
                tt(o_tm[:, :, :], heads[:, :, 0:HD], rden[:, :].unsqueeze(2).to_broadcast([P, H, HD]), ALU.mult).then_inc(o_nrm, 1)

            def att_out(c, b, t):
                k = 2 * (2 * c + b) + t
                dve.wait_ge(att_y, k + 1)
                xs = x[:, c * TI + 2 * b + t, :]
                tt(xs, pc[:, 0:P], xs, ALU.add).then_inc(att_x, 1)

            mine = dict(ln_stats=ln_stats, ln_scale=ln_scale, ln_split=ln_split, route_f1=route_f1, route_f2=route_f2,
                        route_g1=route_g1, route_g2=route_g2, post_add=post_add, rec_gates=rec_gates, rec_add=rec_add,
                        att_qk=att_qk, att_v=att_v, att_keys=att_keys, att_max=att_max, att_shift=att_shift,
                        att_gather=att_gather, att_out=att_out)

            def run(j, i, subs):
                for name, *args in pieces_at(j, i, subs):
                    if name in mine:
                        mine[name](*args)

            def split_block(k, hi, lo, width):
                dve.wait_ge(staged[k % 2], 16 * (k // 2 + 1))
                src = arena[:, k % 2, 0:width]
                link(nc.vector.tensor_copy(hi, src))
                tt(lo, src, hi.bitcast(f32), ALU.subtract).then_inc(w_split, 1)

            dve.wait_ge(consts_in, 16)
            dve.wait_ge(smalls_in, 16 * len(smalls))
            nc.vector.tensor_copy(ident_b[:, :], ident)
            nc.vector.tensor_copy(mask1_b[:, :], const[:, C_MASK1:C_MASK1 + P])
            nc.vector.tensor_copy(mask2_b[:, :], const[:, C_MASK2:C_MASK2 + P])
            ts(bf_neg[:, :], bf[:, :], -1.0, None, ALU.mult)
            ts(bf_half[:, :], bf[:, :], 0.5, None, ALU.add)
            nc.vector.memset(vpad[:, :, :, :], 0.0)
            nc.vector.memset(mpad[:, :, :], 0.0)
            nc.vector.memset(k_one[:, :, :, :].bitcast(f32), 0.0).then_inc(k_zero, 1)
            link(nc.vector.memset(ones_row[:, :], 1.0))
            nc.vector.memset(vpad[:, :, :, HD:HD + 1], 1.0).then_inc(setup_dve, 1)
            dve.wait_ge(staged[0], 16)
            link(nc.vector.tensor_copy(ws_hi[:, :], arena[:, 0, 0:536]))
            tt(ws_lo[:, :], arena[:, 0, 0:536], ws_hi[:, :].bitcast(f32), ALU.subtract).then_inc(ws_split, 1)
            for name, *args in route_pieces("F1", 0):
                if name in mine:
                    mine[name](*args)

            def more_weights(j, i):
                if j == 0 and i % FB == 0 and i // FB + 1 < E0:
                    e = i // FB + 1
                    split_block(e + 1, w_hi[:, e, :], w_lo[:, e, :], 3 * F0)
                if j == 7 and i in (8, 12, 16, 20):
                    q = i // 4 - 2
                    dve.wait_ge(down_mm, first_step(7) + FB * (q + 1))
                    split_block(E0 + 1 + q, w_hi[:, q, :], w_lo[:, q, :], 3 * F0)
                if j == 8 and i == 4:
                    dve.wait_ge(down_mm, first_step(8))
                    split_block(E0 + 5, wa_hi, wa_lo, 1152)
                if j == 8 and i == 8:
                    dve.wait_ge(staged[E0 % 2], 16 * ((E0 + 6) // 2 + 1))
                    src = arena[0:2, E0 % 2, :]
                    nc.vector.tensor_copy(pos_r, src[:, 1024:1536])
                    link(nc.vector.tensor_copy(aug_hi, src[:, 0:1024]))
                    tt(aug_lo, src[:, 0:1024], aug_hi.bitcast(f32), ALU.subtract).then_inc(w_split, 1)

            split_block(1, w_hi[:, 0, :], w_lo[:, 0, :], 3 * F0)
            for j in range(len(JOBS)):
                for i in range(steps(j)):
                    n = first_step(j) + i
                    run(j, i, (0,))
                    dve.wait_ge(weighted, n + 1)
                    dve.wait_ge(up_mm, n + 1)
                    if n >= 3:
                        dve.wait_ge(lo_done, n - 2)
                    if j < 8:
                        tt(hid[:, n % 3, :], pu[n % 2][:, :], gate[:, n % 3, :], ALU.mult).then_inc(hid_done, 1)
                    else:
                        nc.vector.scalar_tensor_tensor(hid[:, n % 3, :], pu[n % 2][:, :], b13[:, 1, i:i + 1],
                                                       gate[:, n % 3, :], ALU.add, ALU.mult).then_inc(hid_done, 1)
                    run(j, i, (1, 2))
                    if n:
                        m = n - 1
                        dve.wait_ge(hi_done, m + 1)
                        tt(h_lo[:, m % 4, :], hid[:, m % 3, :], h_hi[:, m % 4, :].bitcast(f32), ALU.subtract).then_inc(lo_done, 1)
                    more_weights(j, i)
            m = first_step(len(JOBS)) - 1
            dve.wait_ge(hi_done, m + 1)
            tt(h_lo[:, m % 4, :], hid[:, m % 3, :], h_hi[:, m % 4, :].bitcast(f32), ALU.subtract).then_inc(lo_done, 1)
            post_add(len(JOBS) - 1, 0)

        @block.sync
        def _(sp):
            def load_x(c):
                sp.dma_start(x[:, c * TI:(c + 1) * TI, :],
                             x_d[c * CT:(c + 1) * CT, :].rearrange("(t p) d -> p t d", p=P)).then_inc(x_in[c], 16)

            def stage(k):
                if k == 2:
                    sp.wait_ge(ws_split, 1)
                if k >= 3:
                    sp.wait_ge(w_split, k - 2)
                if k == E0 + 1:
                    sp.wait_ge(rec_y, CH)
                src = ws_d if k == 0 else wf_d[k - 1] if k <= E0 else wg_d[k - E0 - 1] if k < E0 + 5 \
                    else wa_d if k == E0 + 5 else aug_d
                sp.dma_start(arena[0:src.shape[0], k % 2, 0:src.shape[1]], src).then_inc(staged[k % 2], 16)

            def store(j):
                c = JOBS[j][1]
                sp.wait_ge(x_added, j + 1)
                sp.dma_start(out_d[c * CT:(c + 1) * CT, :].rearrange("(t p) d -> p t d", p=P),
                             x[:, c * TI:(c + 1) * TI, :]).then_inc(stored, 16)

            sp.dma_start(const[:, :], const_d).then_inc(consts_in, 16)
            load_x(0)
            stage(0)
            for dst, src in smalls:
                sp.dma_start(dst, src).then_inc(smalls_in, 16)
            stage(1)
            stage(2)
            for c in range(1, CH):
                load_x(c)
            load = 0
            for j in range(len(JOBS)):
                sp.wait_ge(w_stored, 16 * nth_route(*JOBS[j]))
                if j >= 8:
                    if j > 8:
                        sp.wait_ge(b2_mm, j - 8)
                    sp.dma_start(wTm[:, :], w_scr[j]).then_inc(wTm_in, 16)
                for e in range(E0 if j < 8 else E1):
                    if load >= 4:
                        old = load - 4
                        done = FB * (old + 1) if old < 8 * E0 else 8 * S0N + old - 8 * E0 + 1
                        sp.wait_ge(weighted, done)
                    sp.dma_start(wbc[:, load % 4, :], w_scr[j, e:e + 1, :].to_broadcast([P, CT])).then_inc(wbc_in[load % 4], 16)
                    load += 1
                    if j == 0 and e + 3 <= E0:
                        stage(e + 3)
                    if j == 7 and e in (0, 1):
                        stage(E0 + 1 + e)
                    if j == 7 and e in (4, 5):
                        stage(E0 - 1 + e)
                    if j == 8 and e in (0, 1):
                        stage(E0 + 5 + e)
                if j >= 13:
                    store(j - 1)
            store(len(JOBS) - 1)
            sp.wait_ge(stored, 16 * CH)


def _constants():
    c = np.zeros((P, C_END), np.float32)
    c[:, C_ID:C_ID + P] = np.eye(P)
    c[:, C_IOTA:C_IOTA + E1] = np.arange(E1)
    c[:, C_TRI:C_TRI + GR * GR] = np.tril(np.ones((GR, GR)), -1).reshape(-1)
    r = np.arange(P) % 32
    c[:, C_MLQ] = -((r >= 2 * HD) & (r < 3 * HD) | (r == 25) | (r == 27)).astype(np.float32)
    c[:, C_MLK] = -((r >= HD) & (r < 2 * HD)).astype(np.float32)
    c[:, C_POW:C_POW + TI] = -0.5
    c[:, C_EPS:C_EPS + TI] = EPS
    upper = np.triu(np.full((P, P), -1e30, np.float32), 1)
    c[:, C_MASK1:C_MASK1 + P] = upper
    c[:, C_MASK2:C_MASK2 + P] = upper.T
    return c


def _by_head(w):
    lead = w.shape[:-1]
    out = np.zeros(lead + (HG, 4, 4, HD), np.float32)
    out[..., 0:3, :] = w.reshape(lead + (HG, 4, 1, HD))
    return out.reshape(lead + (HG * P,))


def _added_rows(bq, bk):
    aug = np.zeros((2, 2, HG, 4, 32), np.float32)
    aug[0, 0] = _by_head(bq).reshape(HG, 4, 32)
    aug[0, 1] = _by_head(bk).reshape(HG, 4, 32)
    slope = (np.float32(2.0 ** (-8.0 / H)) ** np.arange(1, H + 1, dtype=np.float32)).reshape(HG, 4)
    slope = slope * np.sqrt(np.float32(HD))
    aug[0, 0, :, :, 24] = aug[0, 0, :, :, 25] = slope
    aug[1, 1, :, :, 24:26] = 1.0
    aug[1, 0, :, :, 26] = aug[1, 0, :, :, 27] = -slope
    aug[0, 1, :, :, 26:MROW + 1] = 1.0
    return aug.reshape(2, -1)


def kernel(**inputs):
    import concourse.bacc as bacc
    from concourse.bass_utils import run_bass_kernel_spmd

    i = {k: np.asarray(v) for k, v in inputs.items()}
    wf = np.zeros((E0, P, 3, F0), np.float32)
    wf[:, :, 0] = i["L0_ffn_W_gate"].transpose(0, 2, 1)
    wf[:, :, 1] = i["L0_ffn_W_up"].transpose(0, 2, 1)
    wf[:, :, 2] = i["L0_ffn_W_down"].reshape(E0, D, FB, P).transpose(0, 3, 2, 1).reshape(E0, P, F0)
    wg = np.stack([i["L1_ffn_W1"].transpose(0, 2, 1), i["L1_ffn_W3"].transpose(0, 2, 1),
                   i["L1_ffn_W2"].transpose(0, 2, 1)], 2)
    wg = wg.reshape(4, 4, P, 3 * P).transpose(0, 2, 1, 3)
    wz = np.zeros((P, 4, P), np.float32)
    bf = np.zeros((P, 4), np.float32)
    wfT, b_f = i["L0_attn_W_f"].T, i["L0_attn_b_f"]
    wfd = np.zeros((P, 2, D), np.float32)
    for k, (a, b) in enumerate(((0, P), (P, EH))):
        wz[:, 2 * k, 0:b - a], wz[:, 2 * k + 1, 0:b - a] = wfT[:, a:b], wfT[:, EH + a:EH + b]
        bf[0:b - a, 2 * k], bf[0:b - a, 2 * k + 1] = b_f[a:b], b_f[EH + a:EH + b]
        wfd[0:b - a, k] = i["L0_attn_W_down"].T[a:b]
    ws = np.concatenate([wz.reshape(P, 4 * P), i["L0_ffn_W_router"].T, i["L1_ffn_Wg"].T], 1)
    wa = np.concatenate([_by_head(i["L1_attn_Wq"]), _by_head(i["L1_attn_Wk"]), i["L1_attn_Wv"]], 1)
    pos = np.stack([np.ones(CT, np.float32), np.tile(np.arange(SEQ, dtype=np.float32), NB)])
    arrays = dict(
        x=i["L0_attn_x"].reshape(TOK, D), const=_constants(), wf=wf.reshape(E0, P, 3 * F0),
        wg=wg.reshape(4, P, 12 * P), ws=ws, wa=wa, wfd=wfd, wo=i["L1_attn_Wo"], bf=bf,
        b13=np.stack([i["L1_ffn_b1"].T, i["L1_ffn_b3"].T], 1), b2=i["L1_ffn_b2"],
        aug=np.concatenate([_added_rows(i["L1_attn_bq"], i["L1_attn_bk"]), pos], 1),
        bv=i["L1_attn_bv"].reshape(1, D), bo=i["L1_attn_bo"].reshape(1, D))
    nc = bacc.Bacc("TRN2", target_bir_lowering=False, num_devices=1)
    feed, args = {}, []
    for name, a in arrays.items():
        feed[f"in_{name}"] = np.ascontiguousarray(a)
        args.append(nc.dram_tensor(f"in_{name}", a.shape, mybir.dt.from_np(a.dtype), kind="ExternalInput").ap())
    args.append(nc.dram_tensor("out_x", (TOK, D), mybir.dt.float32, kind="ExternalOutput").ap())
    build(nc, *args)
    r = run_bass_kernel_spmd(nc, [feed], core_ids=[0])
    return r.results[0]["out_x"].reshape(TOK // SEQ, SEQ, D)
```

```python
from contextlib import ExitStack

import numpy as np
import concourse.bass as bass
import concourse.mybir as mybir

P = 128
TOK = 2048
SEQ = 256
CH = 4
CT = TOK // CH
TI = CT // P
NB = CT // SEQ
D = 128
E0, F0, FB = 8, 512, 4
E1 = 16
GR = 4
H, HD = 16, 8
HG = 4
EH = 192
MROW = 28
UNITS = NB * HG
SCALE = 1.0 / float(np.sqrt(np.float32(HD)))
EPS = 1e-5
S0N, S1N = E0 * FB, E1
LAG = 4

C_ID, C_IOTA, C_TRI, C_MLQ, C_MLK, C_POW, C_EPS = 0, 128, 144, 160, 161, 162, 166
C_MASK1, C_MASK2, C_END = 170, 298, 426

JOBS = [("F1", c) for c in range(CH)] + [("F2", c) for c in range(CH)] \
     + [("G1", c) for c in range(CH)] + [("G2", c) for c in range(CH)]


def job_of(stage, c):
    return JOBS.index((stage, c))


def first_step(j):
    return S0N * min(j, 8) + S1N * max(j - 8, 0)


def steps(j):
    return S0N if j < 8 else S1N


def norm_pieces(stage, c):
    return [(n, stage, c) for n in ("ln_stats", "ln_rstd", "ln_scale", "ln_transpose", "ln_hi", "ln_lo")]


def weigh_pieces(stage, c):
    names = ["route_logits"]
    names += ["f_top", "f_gap", "f_places", "f_gates"] if stage[0] == "F" else \
        ["g_exp", "g_sigmoid", "g_groups", "g_choose", "g_top", "g_places", "g_weights"]
    return [(n, stage, c) for n in names + ["route_transpose", "route_out"]]


def route_pieces(stage, c):
    return norm_pieces(stage, c) + weigh_pieces(stage, c)


def attention_pieces(c):
    units = NB * HG
    out = []
    for i in range(2 * HG):
        out += [("att_qk", c, i)] + ([("att_qk_hi", c, i - 1), ("att_qk_split", c, i - 1)] if i else [])
    out += [("att_v", c, 0), ("att_qk_hi", c, 2 * HG - 1), ("att_qk_split", c, 2 * HG - 1), ("att_v_out", c, 0)]
    out += [("att_keys", c, 0)]
    for p in range(3):
        out += [("att_max", c, 0, p), ("att_max_out", c, 0, p)]
    out += [("att_keys", c, 1), ("att_shift", c, 0), ("att_shift_out", c, 0)]
    tail = []
    for u in range(units):
        exp = lambda p: [("att_exp", c, u, p)]
        exp_out = lambda p: [("att_exp_out", c, u, p)]
        top = lambda p: [("att_max", c, u + 1, p)] * (u + 1 < units)
        top_out = lambda p: [("att_max_out", c, u + 1, p)] * (u + 1 < units)
        body = exp(0) + top(0) + exp_out(0) + top_out(0) + exp(1) + top(1) + exp_out(1) + top_out(1) + top(2) \
            + exp(2) + top_out(2) + exp_out(2) + [("att_keys", c, u + 2)] * (u + 2 < units) \
            + [("att_shift", c, u + 1), ("att_shift_out", c, u + 1)] * (u + 1 < units)
        if tail:
            mixed = []
            for k, piece in enumerate(body):
                mixed.append(piece)
                mixed += tail[k * len(tail) // len(body):(k + 1) * len(tail) // len(body)]
            body, tail = mixed, []
        out += body + [("att_pv", c, u), ("att_pv_out", c, u)]
        if (u + 1) % HG == 0:
            b = u // HG
            if b + 1 < NB:
                out += [("att_v", c, b + 1), ("att_v_out", c, b + 1)]
            for t in range(SEQ // P):
                tail += [(n, c, b, t) for n in ("att_gather", "att_norm", "att_turn", "att_turn_out", "att_out", "att_add")]
    return out + tail


def lanes(j):
    done = (LAG + 1) / steps(j)
    post = [("post_transpose", j - 1, 0), ("post_add", j - 1, 0)]
    if j == 0:
        return [(0, 1, route_pieces("F1", 1) + route_pieces("F1", 2))]
    if j <= 4:
        c = j - 1
        early = ("F1", 3) if j == 1 else ("F2", j - 2)
        rec = [(n, c, k) for k in range(2) for n in ("rec_project", "rec_gates", "rec_input", "rec_scan")]
        return [(0, done, norm_pieces(*early)), (done, 1, weigh_pieces(*early)),
                (done, 1, post + norm_pieces("A", c) + rec + [("rec_down", c, 0), ("rec_add", c, 0)])]
    if j == 5:
        return [(0, .45, route_pieces("F2", 3)), (done, .45, post), (.45, 1, route_pieces("G1", 0))]
    if j <= 8:
        return [(done, 1, post + route_pieces("G1", j - 5))]
    if j == 9:
        return [(done, 1, post + norm_pieces("B", 0))]
    if j <= 13:
        c = j - 10
        out = [(0, 1, attention_pieces(c)), (done, done + .05, post)]
        if c:
            out += [(done + .05, .6, norm_pieces("G2", c - 1)), (.6, 1, weigh_pieces("G2", c - 1))]
        if c < CH - 1:
            out += [(.6, 1, norm_pieces("B", c + 1))]
        return out
    if j == 14:
        return [(0, .9, route_pieces("G2", 3)), (done, .9, post)]
    return [(done, 1, post)]


FILLS = dict(ln_transpose="a", route_logits="b", route_transpose="b", post_transpose="c", rec_project="ab",
             rec_down="c", att_qk="ab", att_v="c", att_max="ag", att_shift="bu", att_exp="bu", att_pv="c",
             att_gather="c", att_turn="c", att_out="c")
FREES = dict(ln_lo="a", f_top="b", g_exp="b", route_out="b", post_add="c", rec_input="ab", rec_add="c",
             att_qk_split="ab", att_v_out="c", att_max_out="ag", att_shift_out="bu", att_exp_out="bu", att_pv_out="c",
             att_norm="c", att_turn_out="c", att_add="c")


def attends(j):
    return any(p[0] == "att_exp" for _, _, pieces in lanes(j) for p in pieces)


def nth_part(c, u, p):
    return 3 * (UNITS * c + u) + p


def banks(table, piece):
    found = table.get(piece[0], "")
    if found and piece[0] in ("att_qk", "att_qk_split"):
        return found[piece[2] % 2]
    if found and piece[0] in ("att_max", "att_max_out", "att_exp", "att_exp_out"):
        return found[nth_part(*piece[1:]) % 2]
    if found and piece[0] in ("att_shift", "att_shift_out"):
        return found[nth_part(*piece[1:], 0) % 2]
    return found


def place(j):
    total = 3 * steps(j)
    queues = [[(total * (a + (b - a) * k / len(pieces)), piece) for k, piece in enumerate(pieces)]
              for a, b, pieces in lanes(j)]
    held, out, now = {}, {}, 0.0
    while any(queues):
        free = [(q[0][0], n) for n, q in enumerate(queues)
                if q and all(held.get(x, n) == n for x in banks(FILLS, q[0][1]))]
        where, n = min(free)
        piece = queues[n].pop(0)[1]
        now = max(now, where)
        held.update((x, n) for x in banks(FILLS, piece))
        for x in banks(FREES, piece):
            held.pop(x, None)
        out.setdefault(min(int(now), total - 1), []).append(piece)
    return out


PLACED = [place(j) for j in range(len(JOBS))]
NORMS = [("F1", 0)] + [(p[1], p[2]) for at in PLACED for g in sorted(at) for p in at[g] if p[0] == "ln_stats"]
ROUTES = [x for x in NORMS if x[0] in ("F1", "F2", "G1", "G2")]


def build(nc, x_d, const_d, wf_d, wg_d, ws_d, wa_d, wfd_d, wo_d, bf_d, b13_d, b2_d, aug_d, bv_d, bo_d, out_d):
    f32, f32r, bf16, u32 = mybir.dt.float32, mybir.dt.float32r, mybir.dt.bfloat16, mybir.dt.uint32
    ALU, ACT, AX = mybir.AluOpType, mybir.ActivationFunctionType, mybir.AxisListType
    ctx = ExitStack()
    with ctx:
        def sb(name, shape, dt=f32):
            return ctx.enter_context(nc.sbuf_tensor(name, shape, dt))

        def ps(name):
            return ctx.enter_context(nc.psum_tensor(name, [P, 512], f32))

        def sem(name):
            return ctx.enter_context(nc.semaphore(name))

        x = sb("x", [P, CH * TI, D])
        w_hi = sb("w_hi", [P, E0, 3 * F0], f32r)
        w_lo = sb("w_lo", [P, E0, 3 * F0], f32r)
        ws_hi = sb("ws_hi", [P, 536], f32r)
        ws_lo = sb("ws_lo", [P, 536], f32r)
        arena = sb("arena", [P, 2, 1536])
        n_hi = sb("n_hi", [P, TOK], f32r)
        n_lo = sb("n_lo", [P, TOK], f32r)
        a_hi = sb("a_hi", [P, CT], f32r)
        a_lo = sb("a_lo", [P, CT], f32r)
        nrm = sb("nrm", [P, TI, D])
        gate = sb("gate", [P, 2, CT])
        hid = sb("hid", [P, 4, CT])
        h_hi = sb("h_hi", [P, 4, CT], f32r)
        h_lo = sb("h_lo", [P, 4, CT], f32r)
        wbc = sb("wbc", [P, 4, CT])
        y_fm = sb("y_fm", [P, CT])
        wT = sb("wT", [E1, CT])
        wTm = sb("wTm", [E1, CT])
        vpad = sb("vpad", [P, SEQ // P, H, 32])
        k_one = sb("k_one", [P, 2, 4, SEQ], f32r)
        const = sb("const", [P, C_END])
        ident_b = sb("ident_b", [P, P], bf16)
        mask1_b = sb("mask1_b", [P, P], bf16)
        mask2_b = sb("mask2_b", [P, P], bf16)
        wfd = sb("wfd", [P, 2, D])
        wo = sb("wo", [P, D])
        bf = sb("bf", [P, 4])
        bf_neg = sb("bf_neg", [P, 4])
        bf_half = sb("bf_half", [P, 4])
        b13 = sb("b13", [P, 2, E1])
        b1_half = sb("b1_half", [P, E1])
        b2 = sb("b2", [E1, D])
        bv = sb("bv", [P, D])
        bo = sb("bo", [1, D])
        ones_row = sb("ones_row", [1, P])
        stats = sb("stats", [P, TI, 6])
        mv = sb("mv", [P, TI, 2])
        rstd = sb("rstd", [P, TI])
        mpad = sb("mpad", [P, SEQ // P, P])
        rden = sb("rden", [P, H])
        o_tm = sb("o_tm", [P, H, HD])
        o_fm = sb("o_fm", [P, P])
        lg = sb("lg", [P, TI, E1])
        sc = sb("sc", [P, TI, E1])
        top = sb("top", [P, TI, 8])
        topi = sb("topi", [P, TI, 8], u32)
        topf = sb("topf", [P, TI, 8])
        hot = sb("hot", [P, TI, E1, 4])
        gmax = sb("gmax", [P, TI, GR])
        gcmp = sb("gcmp", [P, TI, GR, GR])
        gcmq = sb("gcmq", [P, TI, GR, GR])
        gsel = sb("gsel", [P, TI, GR])
        gsel1 = sb("gsel1", [P, TI, GR])
        wtm = sb("wtm", [P, TI, E1])
        gap = sb("gap", [P, TI])
        egap = sb("egap", [P, TI])
        gk = sb("gk", [P, TI, 2])
        den = sb("den", [P, TI])

        rec = arena[:, :, :].rearrange("p a n -> p (a n)")
        r_a, r_z, r_g = (rec[:, i * CT:(i + 1) * CT] for i in range(3))
        r_h = [rec[:, (3 + k) * CT:(4 + k) * CT] for k in range(2)]
        prob = rec[:, 0:3 * CT]
        o_pad = rec[:, 3 * CT:5 * CT].rearrange("p (g t) -> p g t", g=HG)
        wh = w_hi[:, 4:8, :].rearrange("p a n -> p (a n)")
        wl = w_lo[:, 4:8, :].rearrange("p a n -> p (a n)")
        q_r = wh[:, 0:2048].rearrange("p (g t) -> p g t", g=HG)
        k_r = wh[:, 2048:4096].rearrange("p (g t) -> p g t", g=HG)
        wa_hi, wa_lo = wh[:, 4096:4096 + 1152], wl[:, 4096:4096 + 1152]
        qs_r = wh[:, 5248:5248 + 512].rearrange("p (i t) -> p i t", i=2)
        qk_hi = wl[:, 0:1024].rearrange("p (i t) -> p i t", i=2)
        aug_hi, aug_lo, pos_r = wl[0:2, 1024:2048], wl[0:2, 2048:3072], wl[0:2, 3072:3584]

        ident = const[:, C_ID:C_ID + P]
        w_scr = nc.dram_tensor("w_scr", (len(JOBS), E1, CT), f32, kind="Internal").ap()

        pg = [ps(f"pg{i}") for i in range(2)]
        pu = [ps(f"pu{i}") for i in range(2)]
        pacc = ps("pacc")
        pa, pb, pc = ps("pa"), ps("pb"), ps("pc")

        consts_in, smalls_in, x_in = sem("consts_in"), sem("smalls_in"), [sem(f"x_in{i}") for i in range(CH)]
        staged = [sem(f"staged{i}") for i in range(2)]
        w_split = sem("w_split")
        ws_split = sem("ws_split")
        setup_dve = sem("setup_dve")
        dve_chain, pool_chain = sem("dve_chain"), sem("pool_chain")
        gate_mm, up_mm, down_mm = sem("gate_mm"), sem("up_mm"), sem("down_mm")
        silu_done, weighted, hid_done, hi_done, lo_done = (
            sem(n) for n in ("silu_done", "weighted", "hid_done", "hi_done", "lo_done"))
        wbc_in = [sem(f"wbc_in{i}") for i in range(4)]
        wTm_in, b2_mm = sem("wTm_in"), sem("b2_mm")
        y_out, y_turned, x_added = sem("y_out"), sem("y_turned"), sem("x_added")
        ln_mv, ln_rs, ln_nrm, ln_T, ln_hi, ln_lo = (
            sem(n) for n in ("ln_mv", "ln_rs", "ln_nrm", "ln_T", "ln_hi", "ln_lo"))
        lg_mm, lg_read, lg_act, act_exp, w_tm, wT_mm, wT_out, w_stored = (
            sem(n) for n in ("lg_mm", "lg_read", "lg_act", "act_exp", "w_tm", "wT_mm", "wT_out", "w_stored"))
        rec_mm, rec_sig, rec_read, rec_h, rec_y, rec_x = (sem(n) for n in ("rec_mm", "rec_sig", "rec_read", "rec_h", "rec_y", "rec_x"))
        qk_mm, qk_rd, qk_res = sem("qk_mm"), sem("qk_rd"), sem("qk_res")
        v_mm, v_out = sem("v_mm"), sem("v_out")
        k_zero, k_apart1, k_apart2 = sem("k_zero"), sem("k_apart1"), sem("k_apart2")
        s1_mm, s1_max, m_T, q_shift, s2_mm, s2_exp, pv_mm, pv_out = (
            sem(n) for n in ("s1_mm", "s1_max", "m_T", "q_shift", "s2_mm", "s2_exp", "pv_mm", "pv_out"))
        o_T, o_nrm, o_T2, o_T2out, att_y, att_x = (
            sem(n) for n in ("o_T", "o_nrm", "o_T2", "o_T2out", "att_y", "att_x"))
        stored = sem("stored")

        block = ctx.enter_context(nc.Block())

        smalls = [(wfd[:, :, :], wfd_d), (wo[:, :], wo_d), (bf[:, :], bf_d), (b13[:, :, :], b13_d), (b2[:, :], b2_d),
                  (bv[:, :], bv_d.to_broadcast([P, D])), (bo[:, :], bo_d)]

        def nth_norm(stage, c):
            return NORMS.index((stage, c)) + 1

        def nth_route(stage, c):
            return ROUTES.index((stage, c)) + 1

        def norm_target(stage, c):
            if stage in ("A", "B"):
                return a_hi[:, :], a_lo[:, :]
            return n_hi[:, c * CT:(c + 1) * CT], n_lo[:, c * CT:(c + 1) * CT]

        def x_ready(eng, stage, c):
            if stage == "F1":
                eng.wait_ge(x_in[c], 16)
            elif stage == "F2":
                eng.wait_ge(rec_x, c + 1)
            elif stage == "G2":
                eng.wait_ge(att_x, 4 * (c + 1))
            else:
                eng.wait_ge(x_added, {"A": 0, "G1": 4, "B": 8}[stage] + c + 1)

        def pieces_at(j, i, subs):
            return [piece for s in subs for piece in PLACED[j].get(3 * i + s, [])]

        @block.tensor
        def _(pe):
            def mm3(out, lh, ll, rh, rl, start=True, stop=True):
                nc.tensor.matmul(out, lh, rh, start=start, stop=False)
                nc.tensor.matmul(out, lh, rl, start=False, stop=False)
                return nc.tensor.matmul(out, ll, rh, start=False, stop=stop)

            reader = {bank: None for bank in ("pa", "pb", "pc", "pg0", "pg1", "pu0", "pu1")}

            def take(bank):
                if reader[bank] is not None:
                    pe.wait_ge(*reader[bank])

            def ln_transpose(stage, c):
                n = nth_norm(stage, c)
                pe.wait_ge(ln_nrm, n)
                take("pa")
                for t in range(TI):
                    last = nc.tensor.transpose(pa[:, t * P:(t + 1) * P], nrm[:, t, :], ident)
                last.then_inc(ln_T, 1)
                reader["pa"] = (ln_lo, n)

            def route_logits(stage, c):
                n = nth_norm(stage, c)
                e, off = (E0, 512) if stage[0] == "F" else (E1, 520)
                pe.wait_ge(ln_hi, n)
                pe.wait_ge(ln_lo, n)
                take("pb")
                for t in range(TI):
                    s = slice(c * CT + t * P, c * CT + (t + 1) * P)
                    last = mm3(pb[:, t * e:(t + 1) * e], n_hi[:, s], n_lo[:, s], ws_hi[:, off:off + e], ws_lo[:, off:off + e])
                last.then_inc(lg_mm, 1)
                reader["pb"] = (lg_read, nth_route(stage, c))

            def route_transpose(stage, c):
                n = nth_route(stage, c)
                e = E0 if stage[0] == "F" else E1
                pe.wait_ge(w_tm, n)
                take("pb")
                for t in range(TI):
                    last = nc.tensor.transpose(pb[0:e, t * P:(t + 1) * P], wtm[:, t, 0:e], ident)
                last.then_inc(wT_mm, 1)
                reader["pb"] = (wT_out, n)

            def post_transpose(j, _):
                pe.wait_ge(y_out, j + 1)
                take("pc")
                for t in range(TI):
                    last = nc.tensor.transpose(pc[:, t * P:(t + 1) * P], y_fm[:, t * P:(t + 1) * P], ident)
                last.then_inc(y_turned, 1)
                reader["pc"] = (x_added, j + 1)

            def rec_project(c, k):
                pe.wait_ge(ln_hi, nth_norm("A", c))
                pe.wait_ge(ln_lo, nth_norm("A", c))
                for i, (name, bank) in enumerate((("pa", pa), ("pb", pb))):
                    take(name)
                    o = (2 * k + i) * P
                    last = mm3(bank[:, :], ws_hi[:, o:o + P], ws_lo[:, o:o + P], a_hi[:, :], a_lo[:, :])
                    reader[name] = (rec_sig, 3 * (2 * c + k) + 2) if i == 0 else (rec_read, 2 * c + k + 1)
                last.then_inc(rec_mm, 1)

            def rec_down(c, _):
                pe.wait_ge(rec_h, 2 * (c + 1))
                take("pc")
                for t in range(TI):
                    s = slice(t * P, (t + 1) * P)
                    nc.tensor.matmul(pc[:, s], r_h[0][:, s], wfd[:, 0, :], start=True, stop=False)
                    last = nc.tensor.matmul(pc[:, s], r_h[1][0:EH - P, s], wfd[0:EH - P, 1, :], start=False, stop=True)
                last.then_inc(rec_y, 1)
                reader["pc"] = (rec_x, c + 1)

            def att_qk(c, i):
                if i == 0:
                    pe.wait_ge(ln_hi, nth_norm("B", c))
                    pe.wait_ge(ln_lo, nth_norm("B", c))
                    pe.wait_ge(w_split, E0 + 6)
                g, what = i // 2, i % 2
                name, bank = (("pa", pa), ("pb", pb))[what]
                take(name)
                o = (what * HG + g) * P
                mm3(bank[:, :], wa_hi[:, o:o + P], wa_lo[:, o:o + P], a_hi[:, :], a_lo[:, :], stop=False)
                nc.tensor.matmul(bank[:, :], aug_hi[:, o:o + P], pos_r, start=False, stop=False)
                nc.tensor.matmul(bank[:, :], aug_lo[:, o:o + P], pos_r, start=False, stop=True).then_inc(qk_mm, 1)
                reader[name] = (qk_res, 8 * c + i + 1)

            def att_v(c, b):
                take("pc")
                for t in range(SEQ // P):
                    s = slice(b * SEQ + t * P, b * SEQ + (t + 1) * P)
                    last = mm3(pc[:, t * P:(t + 1) * P], a_hi[:, s], a_lo[:, s], wa_hi[:, 1024:1152], wa_lo[:, 1024:1152])
                last.then_inc(v_mm, 1)
                reader["pc"] = (v_out, 2 * c + b + 1)

            def att_max(c, u, p):
                b, g = divmod(u, HG)
                nth = nth_part(c, u, p)
                name, bank = (("pa", pa), ("pg1", pg[1]))[nth % 2]
                if p == 0:
                    pe.wait_ge(k_apart1, 8 * c + u + 1)
                    pe.wait_ge(k_apart2, 8 * c + u + 1)
                take(name)
                heads = range(4) if p == 0 else range(2 * p - 2, 2 * p)
                w = P if p == 0 else SEQ
                for i, h in enumerate(heads):
                    t0 = b * SEQ + (0 if p == 0 else P)
                    nc.tensor.matmul(bank[:, i * w:(i + 1) * w], q_r[:, g, t0:t0 + P],
                                     k_one[:, u % 2, h, 0:w], start=True, stop=False)
                    last = nc.tensor.matmul(bank[:, (i + 1) * w - P:(i + 1) * w], ident_b[:, :], mask1_b[:, :],
                                            start=False, stop=True)
                last.then_inc(s1_mm, 1)
                reader[name] = (s1_max, nth + 1)

            def att_shift(c, u):
                pe.wait_ge(s1_max, 3 * (8 * c + u + 1))
                name, bank = (("pb", pb), ("pu1", pu[1]))[nth_part(c, u, 0) % 2]
                take(name)
                for t in range(SEQ // P):
                    last = nc.tensor.transpose(bank[:, t * P:(t + 1) * P], mpad[:, t, :], ident)
                last.then_inc(m_T, 1)
                reader[name] = (q_shift, 8 * c + u + 1)

            def att_exp(c, u, p):
                b, g = divmod(u, HG)
                nth = nth_part(c, u, p)
                name, bank = (("pb", pb), ("pu1", pu[1]))[nth % 2]
                if p == 0:
                    pe.wait_ge(q_shift, 8 * c + u + 1)
                take(name)
                heads = range(4) if p == 2 else range(2 * p, 2 * p + 2)
                w = P if p == 2 else SEQ
                for i, h in enumerate(heads):
                    s0 = P if p == 2 else 0
                    nc.tensor.matmul(bank[:, i * w:(i + 1) * w], k_one[:, u % 2, h, s0:s0 + P],
                                     qs_r[:, u % 2, SEQ - w:SEQ], start=True, stop=False)
                    last = nc.tensor.matmul(bank[:, i * w:i * w + P], ident_b[:, :], mask2_b[:, :],
                                            start=False, stop=True)
                last.then_inc(s2_mm, 1)
                reader[name] = (s2_exp, nth + 1)

            def att_pv(c, u):
                b, g = divmod(u, HG)
                pe.wait_ge(s2_exp, 3 * (8 * c + u + 1))
                if g == 0:
                    pe.wait_ge(v_out, 2 * c + b + 1)
                take("pc")
                for h in range(4):
                    o = pc[32 * h:32 * h + 32, 0:SEQ]
                    hh = 4 * g + h
                    nc.tensor.matmul(o, vpad[:, 0, hh, :], prob[:, h * SEQ:(h + 1) * SEQ], start=True, stop=False)
                    last = nc.tensor.matmul(pc[32 * h:32 * h + 32, P:SEQ], vpad[:, 1, hh, :],
                                            prob[:, 4 * SEQ + h * P:4 * SEQ + (h + 1) * P], start=False, stop=True)
                last.then_inc(pv_mm, 1)
                reader["pc"] = (pv_out, 8 * c + u + 1)

            def att_gather(c, b, t):
                k = 2 * (2 * c + b) + t
                pe.wait_ge(pv_out, 4 * (2 * c + b + 1))
                take("pc")
                for g in range(HG):
                    last = nc.tensor.transpose(pc[:, g * P:(g + 1) * P], o_pad[:, g, t * P:(t + 1) * P], ident)
                last.then_inc(o_T, 1)
                reader["pc"] = (o_nrm, k + 1)

            def att_turn(c, b, t):
                k = 2 * (2 * c + b) + t
                take("pc")
                nc.tensor.transpose(pc[:, 0:P], o_tm[:, :, :].rearrange("p h d -> p (h d)"), ident).then_inc(o_T2, 1)
                reader["pc"] = (o_T2out, k + 1)

            def att_out(c, b, t):
                k = 2 * (2 * c + b) + t
                take("pc")
                nc.tensor.matmul(pc[:, 0:P], o_fm[:, :], wo[:, :], start=True, stop=False)
                nc.tensor.matmul(pc[:, 0:P], ones_row[:, :], bo[:, :], start=False, stop=True).then_inc(att_y, 1)
                reader["pc"] = (att_x, k + 1)

            mine = dict(ln_transpose=ln_transpose, route_logits=route_logits, route_transpose=route_transpose,
                        post_transpose=post_transpose, rec_project=rec_project, rec_down=rec_down, att_qk=att_qk,
                        att_v=att_v, att_max=att_max, att_shift=att_shift, att_exp=att_exp, att_pv=att_pv,
                        att_gather=att_gather, att_turn=att_turn, att_out=att_out)

            def run(j, i, sub):
                for name, *args in pieces_at(j, i, [sub]):
                    if name in mine:
                        mine[name](*args)

            def weights(j, i):
                if j < 8:
                    e, f = divmod(i, FB)
                    part = lambda w, k: w[:, e, k * F0 + f * P:k * F0 + (f + 1) * P]
                    return [(part(w_hi, k), part(w_lo, k)) for k in range(3)], e + 1
                q, r = divmod(i, 4)
                part = lambda w, k: w[:, q, r * 3 * P + k * P:r * 3 * P + (k + 1) * P]
                return [(part(w_hi, k), part(w_lo, k)) for k in range(3)], E0 + q + 1

            def down(n):
                j = n // S0N if n < 8 * S0N else 8 + (n - 8 * S0N) // S1N
                i = n - first_step(j)
                if i == 0 and j:
                    pe.wait_ge(y_out, j)
                first = i == 0
                if first and j >= 8:
                    pe.wait_ge(wTm_in, 16 * (j - 7))
                    nc.tensor.matmul(pacc[:, :], b2[:, :], wTm[:, :], start=True, stop=False).then_inc(b2_mm, 1)
                    first = False
                w, _ = weights(j, i)
                pe.wait_ge(lo_done, n + 1)
                mm3(pacc[:, :], w[2][0], w[2][1], h_hi[:, n % 4, :], h_lo[:, n % 4, :], start=first,
                    stop=i == steps(j) - 1).then_inc(down_mm, 1)

            pe.wait_ge(consts_in, 16)
            pe.wait_ge(ws_split, 1)
            pe.wait_ge(setup_dve, 1)
            for name, *args in route_pieces("F1", 0):
                if name in mine:
                    mine[name](*args)
            for j in range(len(JOBS)):
                c = JOBS[j][1]
                s = slice(c * CT, (c + 1) * CT)
                pe.wait_ge(ln_lo, nth_norm(*JOBS[j]))
                for i in range(steps(j)):
                    n = first_step(j) + i
                    w, split = weights(j, i)
                    pe.wait_ge(w_split, split)
                    k = 0 if attends(j) else n % 2
                    take(f"pg{k}")
                    mm3(pg[k][:, :], *w[0], n_hi[:, s], n_lo[:, s]).then_inc(gate_mm, 1)
                    reader[f"pg{k}"] = (hid_done, n + 1) if attends(j) else (silu_done, n + 1)
                    run(j, i, 0)
                    take(f"pu{k}")
                    mm3(pu[k][:, :], *w[1], n_hi[:, s], n_lo[:, s]).then_inc(up_mm, 1)
                    reader[f"pu{k}"] = (hid_done, n + 1)
                    run(j, i, 1)
                    if n >= LAG:
                        down(n - LAG)
                    run(j, i, 2)
            total = first_step(len(JOBS))
            for n in range(total - LAG, total):
                down(n)
            post_transpose(len(JOBS) - 1, 0)

        @block.scalar
        def _(act):
            def ln_hi_part(stage, c):
                n = nth_norm(stage, c)
                act.wait_ge(ln_T, n)
                nc.scalar.activation(norm_target(stage, c)[0], pa[:, :], ACT.Copy).then_inc(ln_hi, 1)

            def f_gap(stage, c):
                act.wait_ge(lg_act, nth_route(stage, c))
                nc.scalar.activation(egap[:, :], gap[:, :], ACT.Exp).then_inc(act_exp, 1)

            def g_exp(stage, c):
                act.wait_ge(lg_mm, nth_route(stage, c))
                nc.scalar.activation(lg[:, :, :], pb[:, 0:TI * E1].rearrange("p (t e) -> p t e", t=TI), ACT.Exp,
                                     scale=-1.0).then_inc(lg_read, 1)

            def route_out(stage, c):
                n = nth_route(stage, c)
                e = E0 if stage[0] == "F" else E1
                act.wait_ge(wT_mm, n)
                if n > 1:
                    act.wait_ge(w_stored, 16 * (n - 1))
                nc.scalar.activation(wT[0:e, :], pb[0:e, :], ACT.Copy).then_inc(wT_out, 1)
                act.wait_ge(wT_out, n)
                act.dma_start(w_scr[job_of(stage, c), 0:e, :], wT[0:e, :]).then_inc(w_stored, 16)

            def rec_gates(c, k):
                m = 2 * c + k
                act.wait_ge(rec_mm, m + 1)
                if m:
                    act.wait_ge(rec_h, m)
                else:
                    act.wait_ge(w_split, E0)
                nc.scalar.activation(r_a, pa[:, :], ACT.Sigmoid, bias=bf_neg[:, 2 * k:2 * k + 1],
                                     scale=-1.0).then_inc(rec_sig, 1)
                nc.scalar.activation(r_z, pa[:, :], ACT.Sigmoid, bias=bf[:, 2 * k:2 * k + 1]).then_inc(rec_sig, 1)
                nc.scalar.activation(r_g, pb[:, :], ACT.Sigmoid, bias=bf[:, 2 * k + 1:2 * k + 2]).then_inc(rec_sig, 1)

            def att_qk_hi(c, i):
                g, what = i // 2, i % 2
                act.wait_ge(qk_mm, 8 * c + i + 1)
                nth = 8 * c + i
                if nth >= 2:
                    act.wait_ge(qk_res, nth - 1)
                nc.scalar.activation(qk_hi[:, i % 2, :], (pa, pb)[what][:, :], ACT.Copy).then_inc(qk_rd, 1)

            def att_keys(c, u):
                b, g = divmod(u, HG)
                act.wait_ge(qk_res, 8 * c + 2 * g + 2)
                act.wait_ge(k_zero, 1)
                if 8 * c + u >= 2:
                    act.wait_ge(s2_mm, 3 * (8 * c + u - 1))
                for h in (0, 1):
                    r = slice(32 * h, 32 * h + 32)
                    last = nc.scalar.activation(k_one[r, u % 2, h, :], k_r[r, g, b * SEQ:(b + 1) * SEQ].bitcast(f32), ACT.Copy)
                last.then_inc(k_apart1, 1)

            def att_exp_out(c, u, p):
                nth = nth_part(c, u, p)
                bank = (pb, pu[1])[nth % 2]
                act.wait_ge(s2_mm, nth + 1)
                if p == 0 and 8 * c + u:
                    act.wait_ge(pv_mm, 8 * c + u)
                nc.scalar.activation(prob[:, p * CT:(p + 1) * CT], bank[:, :], ACT.Exp, scale=SCALE).then_inc(s2_exp, 1)

            def att_pv_out(c, u):
                g = u % HG
                act.wait_ge(pv_mm, 8 * c + u + 1)
                if g == 0 and 8 * c + u:
                    act.wait_ge(o_T, 2 * ((8 * c + u) // HG))
                nc.scalar.activation(o_pad[:, g, :], pc[:, 0:SEQ], ACT.Copy).then_inc(pv_out, 1)

            def att_turn_out(c, b, t):
                k = 2 * (2 * c + b) + t
                act.wait_ge(o_T2, k + 1)
                if k:
                    act.wait_ge(att_y, k)
                nc.scalar.activation(o_fm[:, :], pc[:, 0:P], ACT.Copy).then_inc(o_T2out, 1)

            mine = dict(ln_hi=ln_hi_part, f_gap=f_gap, g_exp=g_exp, route_out=route_out, rec_gates=rec_gates,
                        att_qk_hi=att_qk_hi, att_keys=att_keys, att_exp_out=att_exp_out, att_pv_out=att_pv_out,
                        att_turn_out=att_turn_out)

            def round_hidden(n):
                act.wait_ge(weighted, n + 1)
                if n >= 4:
                    act.wait_ge(down_mm, n - 3)
                nc.scalar.activation(h_hi[:, n % 4, :], hid[:, n % 4, :], ACT.Copy).then_inc(hi_done, 1)

            def take_sum(j):
                act.wait_ge(down_mm, first_step(j + 1))
                if j:
                    act.wait_ge(y_turned, j)
                nc.scalar.activation(y_fm[:, :], pacc[:, :], ACT.Copy).then_inc(y_out, 1)

            act.wait_ge(smalls_in, 16 * len(smalls))
            for name, *args in route_pieces("F1", 0):
                if name in mine:
                    mine[name](*args)
            for j in range(len(JOBS)):
                for i in range(steps(j)):
                    n = first_step(j) + i
                    if j and i == LAG:
                        take_sum(j - 1)
                    act.wait_ge(gate_mm, n + 1)
                    if n >= 2:
                        act.wait_ge(hid_done, n - 1)
                    bias = b13[:, 0, i:i + 1] if j >= 8 else 0.0
                    if attends(j):
                        nc.scalar.activation(gate[:, n % 2, :], pg[0][:, :], ACT.Tanh, bias=b1_half[:, i:i + 1],
                                             scale=0.5).then_inc(silu_done, 1)
                    else:
                        nc.scalar.activation(gate[:, n % 2, :], pg[n % 2][:, :], ACT.Silu, bias=bias).then_inc(silu_done, 1)
                    for name, *args in pieces_at(j, i, (0, 1, 2)):
                        if name in mine:
                            mine[name](*args)
                    if n >= 2:
                        round_hidden(n - 2)
            round_hidden(first_step(len(JOBS)) - 2)
            round_hidden(first_step(len(JOBS)) - 1)
            take_sum(len(JOBS) - 1)

        @block.gpsimd
        def _(pool):
            chain = [0]

            def link(ins):
                chain[0] += 1
                ins.then_inc(pool_chain, 1)
                pool.wait_ge(pool_chain, chain[0])

            def ln_rstd(stage, c):
                n = nth_norm(stage, c)
                pool.wait_ge(ln_mv, n)
                link(nc.gpsimd.tensor_tensor(rstd[:, :], mv[:, :, 1], const[:, C_EPS:C_EPS + TI], ALU.add))
                nc.gpsimd.tensor_tensor(rstd[:, :], rstd[:, :], const[:, C_POW:C_POW + TI], ALU.pow).then_inc(ln_rs, 1)

            mine = dict(ln_rstd=ln_rstd)

            def run(j, i, subs):
                for name, *args in pieces_at(j, i, subs):
                    if name in mine:
                        mine[name](*args)

            pool.wait_ge(consts_in, 16)
            for name, *args in route_pieces("F1", 0):
                if name in mine:
                    mine[name](*args)
            for j in range(len(JOBS)):
                for i in range(steps(j)):
                    n = first_step(j) + i
                    run(j, i, (0,))
                    pool.wait_ge(hid_done, n + 1)
                    if j < 8:
                        load = n // FB
                    else:
                        load = 8 * E0 + (n - 8 * S0N)
                    pool.wait_ge(wbc_in[load % 4], 16 * (load // 4 + 1))
                    nc.gpsimd.tensor_tensor(hid[:, n % 4, :], hid[:, n % 4, :], wbc[:, load % 4, :],
                                            ALU.mult).then_inc(weighted, 1)
                    run(j, i, (1, 2))

        @block.vector
        def _(dve):
            chain = [0]

            def link(ins):
                chain[0] += 1
                ins.then_inc(dve_chain, 1)
                dve.wait_ge(dve_chain, chain[0])

            tt, ts = nc.vector.tensor_tensor, nc.vector.tensor_scalar

            def ln_stats(stage, c):
                n = nth_norm(stage, c)
                x_ready(dve, stage, c)
                if n > 1:
                    dve.wait_ge(ln_rs, n - 1)
                for t in range(TI):
                    last = nc.vector.bn_stats(stats[:, t, :], x[:, c * TI + t, :])
                link(last)
                for t in range(TI):
                    last = nc.vector.bn_aggr(mv[:, t, :], stats[:, t, :])
                last.then_inc(ln_mv, 1)

            def ln_scale(stage, c):
                n = nth_norm(stage, c)
                dve.wait_ge(ln_rs, n)
                dve.wait_ge(ln_mv, n)
                if n > 1:
                    dve.wait_ge(ln_T, n - 1)
                for t in range(TI):
                    last = ts(nrm[:, t, :], x[:, c * TI + t, :], mv[:, t, 0:1], rstd[:, t:t + 1], ALU.subtract, ALU.mult)
                last.then_inc(ln_nrm, 1)

            def ln_lo_part(stage, c):
                n = nth_norm(stage, c)
                dve.wait_ge(ln_hi, n)
                hi, lo = norm_target(stage, c)
                tt(lo, pa[:, :], hi.bitcast(f32), ALU.subtract).then_inc(ln_lo, 1)

            def top_of(values, e):
                for t in range(TI):
                    last = nc.vector.max(top[:, t, :], values[:, t, 0:e])
                link(last)
                for t in range(TI):
                    last = nc.vector.max_index(topi[:, t, :], top[:, t, :], values[:, t, 0:e])
                link(last)
                link(nc.vector.tensor_copy(topf[:, :, :], topi[:, :, :]))

            def places(e, k):
                iota = const[:, C_IOTA:C_IOTA + e].unsqueeze(1).unsqueeze(3).to_broadcast([P, TI, e, k])
                want = topf[:, :, 0:k].unsqueeze(2).to_broadcast([P, TI, e, k])
                link(tt(hot[:, :, 0:e, 0:k], iota, want, ALU.is_equal))

            def f_top(stage, c):
                n = nth_route(stage, c)
                dve.wait_ge(lg_mm, n)
                nc.vector.tensor_copy(lg[:, :, 0:E0], pb[:, 0:TI * E0].rearrange("p (t e) -> p t e", t=TI)).then_inc(lg_read, 1)
                dve.wait_ge(lg_read, n)
                top_of(lg, E0)
                tt(gap[:, :], top[:, :, 1], top[:, :, 0], ALU.subtract).then_inc(lg_act, 1)

            def f_places(stage, c):
                places(E0, 2)

            def f_gates(stage, c):
                n = nth_route(stage, c)
                dve.wait_ge(act_exp, n)
                link(ts(den[:, :], egap[:, :], 1.0, None, ALU.add))
                link(nc.vector.reciprocal(gk[:, :, 0], den[:, :]))
                link(tt(gk[:, :, 1], gk[:, :, 0], egap[:, :], ALU.mult))
                link(tt(hot[:, :, 0:E0, 0:2], hot[:, :, 0:E0, 0:2],
                        gk[:, :, :].unsqueeze(2).to_broadcast([P, TI, E0, 2]), ALU.mult))
                if n > 1:
                    dve.wait_ge(wT_mm, n - 1)
                nc.vector.tensor_reduce(wtm[:, :, 0:E0], hot[:, :, 0:E0, 0:2], AX.X, ALU.add).then_inc(w_tm, 1)

            def g_sigmoid(stage, c):
                n = nth_route(stage, c)
                dve.wait_ge(lg_read, n)
                link(ts(lg[:, :, :], lg[:, :, :], 1.0, None, ALU.add))
                link(nc.vector.reciprocal(sc[:, :, :], lg[:, :, :]))

            s4 = sc[:, :, :].rearrange("p t (g e) -> p t g e", g=GR)
            m4 = lg[:, :, :].rearrange("p t (g e) -> p t g e", g=GR)

            def g_groups(stage, c):
                link(nc.vector.tensor_reduce(gmax[:, :, :], s4, AX.X, ALU.max))
                other = gmax[:, :, :].unsqueeze(2).to_broadcast([P, TI, GR, GR])
                own = gmax[:, :, :].unsqueeze(3).to_broadcast([P, TI, GR, GR])
                before = const[:, C_TRI:C_TRI + GR * GR].rearrange("p (a b) -> p a b", a=GR).unsqueeze(1) \
                    .to_broadcast([P, TI, GR, GR])
                link(tt(gcmp[:, :, :, :], other, own, ALU.is_gt))
                link(tt(gcmq[:, :, :, :], other, own, ALU.is_equal))
                link(tt(gcmq[:, :, :, :], gcmq[:, :, :, :], before, ALU.mult))
                link(tt(gcmp[:, :, :, :], gcmp[:, :, :, :], gcmq[:, :, :, :], ALU.add))

            def g_choose(stage, c):
                link(nc.vector.tensor_reduce(gsel[:, :, :], gcmp[:, :, :, :], AX.X, ALU.add))
                link(ts(gsel[:, :, :], gsel[:, :, :], 1.5, None, ALU.is_lt))
                link(ts(gsel1[:, :, :], gsel[:, :, :], 1.0, None, ALU.subtract))
                link(tt(m4, s4, gsel[:, :, :].unsqueeze(3).to_broadcast([P, TI, GR, 4]), ALU.mult))
                link(tt(m4, m4, gsel1[:, :, :].unsqueeze(3).to_broadcast([P, TI, GR, 4]), ALU.add))

            def g_top(stage, c):
                top_of(lg, E1)

            def g_places(stage, c):
                places(E1, 4)

            def g_weights(stage, c):
                n = nth_route(stage, c)
                link(nc.vector.tensor_reduce(lg[:, :, :], hot[:, :, :, :], AX.X, ALU.add))
                link(tt(sc[:, :, :], sc[:, :, :], lg[:, :, :], ALU.mult))
                link(nc.vector.tensor_reduce(den[:, :], sc[:, :, :], AX.X, ALU.add))
                link(nc.vector.reciprocal(gap[:, :], den[:, :]))
                link(ts(gap[:, :], gap[:, :], 2.5, None, ALU.mult))
                dve.wait_ge(wT_mm, n - 1)
                tt(wtm[:, :, :], sc[:, :, :], gap[:, :].unsqueeze(2).to_broadcast([P, TI, E1]), ALU.mult).then_inc(w_tm, 1)

            def post_add(j, _):
                c = JOBS[j][1]
                dve.wait_ge(y_turned, j + 1)
                xs = x[:, c * TI:(c + 1) * TI, :].rearrange("p t d -> p (t d)")
                nc.vector.scalar_tensor_tensor(xs, pc[:, :], 0.5, xs, ALU.mult, ALU.add).then_inc(x_added, 1)

            def rec_input(c, k):
                m = 2 * c + k
                dve.wait_ge(rec_sig, 3 * (m + 1))
                nc.vector.scalar_tensor_tensor(r_g, pb[:, :], bf_half[:, 2 * k + 1:2 * k + 2], r_g, ALU.add,
                                               ALU.max).then_inc(rec_read, 1)
                dve.wait_ge(rec_read, m + 1)
                link(tt(r_g, r_g, r_z, ALU.mult))

            def rec_scan(c, k):
                if c:
                    dve.wait_ge(rec_y, c)
                for b in range(NB):
                    s = slice(b * SEQ, (b + 1) * SEQ)
                    last = nc.vector.tensor_tensor_scan(r_h[k][:, s], r_a[:, s], r_g[:, s], 0.5, ALU.mult, ALU.add)
                last.then_inc(rec_h, 1)

            def rec_add(c, _):
                dve.wait_ge(rec_y, c + 1)
                xs = x[:, c * TI:(c + 1) * TI, :].rearrange("p t d -> p (t d)")
                tt(xs, pc[:, :], xs, ALU.add).then_inc(rec_x, 1)

            def att_qk_split(c, i):
                g, what = i // 2, i % 2
                dve.wait_ge(qk_rd, 8 * c + i + 1)
                if c:
                    dve.wait_ge(pv_mm, 8 * c)
                ml = const[:, (C_MLQ, C_MLK)[what]:(C_MLQ, C_MLK)[what] + 1]
                nc.vector.scalar_tensor_tensor((q_r, k_r)[what][:, g, :], qk_hi[:, i % 2, :].bitcast(f32), ml,
                                               (pa, pb)[what][:, :], ALU.mult, ALU.add).then_inc(qk_res, 1)

            def att_v_out(c, b):
                dve.wait_ge(v_mm, 2 * c + b + 1)
                if 2 * c + b:
                    dve.wait_ge(pv_mm, 4 * (2 * c + b))
                for t in range(SEQ // P):
                    last = tt(vpad[:, t, :, 0:HD], pc[:, t * P:(t + 1) * P].rearrange("p (h d) -> p h d", h=H),
                              bv[:, :].rearrange("p (h d) -> p h d", h=H), ALU.add)
                last.then_inc(v_out, 1)

            def att_keys(c, u):
                b, g = divmod(u, HG)
                dve.wait_ge(qk_res, 8 * c + 2 * g + 2)
                dve.wait_ge(k_zero, 1)
                if 8 * c + u >= 2:
                    dve.wait_ge(s2_mm, 3 * (8 * c + u - 1))
                for h in (2, 3):
                    r = slice(32 * h, 32 * h + 32)
                    last = nc.vector.tensor_copy(k_one[r, u % 2, h, :], k_r[r, g, b * SEQ:(b + 1) * SEQ])
                last.then_inc(k_apart2, 1)

            def att_max_out(c, u, p):
                nth = nth_part(c, u, p)
                bank = (pa, pg[1])[nth % 2]
                dve.wait_ge(s1_mm, nth + 1)
                if p == 0 and 8 * c + u:
                    dve.wait_ge(m_T, 8 * c + u)
                k, w = (4, P) if p == 0 else (2, SEQ)
                h0 = 0 if p < 2 else 2
                out = mpad[:, min(p, 1), :].rearrange("p (h r) -> p h r", r=32)[:, h0:h0 + k, MROW]
                nc.vector.tensor_reduce(out, bank[:, :].rearrange("p (h w) -> p h w", w=w), AX.X, ALU.max,
                                        negate=True).then_inc(s1_max, 1)

            def att_shift_out(c, u):
                b, g = divmod(u, HG)
                dve.wait_ge(m_T, 8 * c + u + 1)
                if 8 * c + u >= 2:
                    dve.wait_ge(s2_mm, 3 * (8 * c + u - 1))
                bank = (pb, pu[1])[nth_part(c, u, 0) % 2]
                tt(qs_r[:, u % 2, :], bank[:, 0:SEQ], q_r[:, g, b * SEQ:(b + 1) * SEQ].bitcast(f32), ALU.add).then_inc(q_shift, 1)

            def att_norm(c, b, t):
                k = 2 * (2 * c + b) + t
                dve.wait_ge(o_T, k + 1)
                heads = pc[:, :].rearrange("p (h r) -> p h r", r=32)
                link(nc.vector.reciprocal(rden[:, :], heads[:, :, HD]))
                if k:
                    dve.wait_ge(o_T2, k)
                tt(o_tm[:, :, :], heads[:, :, 0:HD], rden[:, :].unsqueeze(2).to_broadcast([P, H, HD]), ALU.mult).then_inc(o_nrm, 1)

            def att_add(c, b, t):
                k = 2 * (2 * c + b) + t
                dve.wait_ge(att_y, k + 1)
                xs = x[:, c * TI + 2 * b + t, :]
                tt(xs, pc[:, 0:P], xs, ALU.add).then_inc(att_x, 1)

            mine = dict(ln_stats=ln_stats, ln_scale=ln_scale, ln_lo=ln_lo_part, f_top=f_top, f_places=f_places,
                        f_gates=f_gates, g_sigmoid=g_sigmoid, g_groups=g_groups, g_choose=g_choose, g_top=g_top,
                        g_places=g_places, g_weights=g_weights, post_add=post_add, rec_input=rec_input,
                        rec_scan=rec_scan, rec_add=rec_add, att_qk_split=att_qk_split, att_v_out=att_v_out,
                        att_keys=att_keys, att_max_out=att_max_out, att_shift_out=att_shift_out,
                        att_norm=att_norm, att_add=att_add)

            def run(j, i, subs):
                for name, *args in pieces_at(j, i, subs):
                    if name in mine:
                        mine[name](*args)

            def split_block(k, hi, lo, width):
                dve.wait_ge(staged[k % 2], 16 * (k // 2 + 1))
                src = arena[:, k % 2, 0:width]
                link(nc.vector.tensor_copy(hi, src))
                tt(lo, src, hi.bitcast(f32), ALU.subtract).then_inc(w_split, 1)

            dve.wait_ge(consts_in, 16)
            dve.wait_ge(smalls_in, 16 * len(smalls))
            nc.vector.tensor_copy(ident_b[:, :], ident)
            nc.vector.tensor_copy(mask1_b[:, :], const[:, C_MASK1:C_MASK1 + P])
            nc.vector.tensor_copy(mask2_b[:, :], const[:, C_MASK2:C_MASK2 + P])
            ts(bf_neg[:, :], bf[:, :], -1.0, None, ALU.mult)
            ts(bf_half[:, :], bf[:, :], 0.5, None, ALU.add)
            ts(b1_half[:, :], b13[:, 0, :], 0.5, None, ALU.mult)
            nc.vector.memset(vpad[:, :, :, :], 0.0)
            nc.vector.memset(mpad[:, :, :], 0.0)
            nc.vector.memset(k_one[:, :, :, :].bitcast(f32), 0.0).then_inc(k_zero, 1)
            link(nc.vector.memset(ones_row[:, :], 1.0))
            nc.vector.memset(vpad[:, :, :, HD:HD + 1], 1.0).then_inc(setup_dve, 1)
            dve.wait_ge(staged[0], 16)
            link(nc.vector.tensor_copy(ws_hi[:, :], arena[:, 0, 0:536]))
            tt(ws_lo[:, :], arena[:, 0, 0:536], ws_hi[:, :].bitcast(f32), ALU.subtract).then_inc(ws_split, 1)
            for name, *args in route_pieces("F1", 0):
                if name in mine:
                    mine[name](*args)

            def more_weights(j, i):
                if j == 0 and i % FB == 0 and i // FB + 1 < E0:
                    e = i // FB + 1
                    split_block(e + 1, w_hi[:, e, :], w_lo[:, e, :], 3 * F0)
                if j == 7 and i in (8, 12, 16, 20):
                    q = i // 4 - 2
                    dve.wait_ge(down_mm, first_step(7) + FB * (q + 1))
                    split_block(E0 + 1 + q, w_hi[:, q, :], w_lo[:, q, :], 3 * F0)
                if j == 8 and i == 4:
                    dve.wait_ge(down_mm, first_step(8))
                    split_block(E0 + 5, wa_hi, wa_lo, 1152)
                if j == 8 and i == 8:
                    dve.wait_ge(staged[E0 % 2], 16 * ((E0 + 6) // 2 + 1))
                    src = arena[0:2, E0 % 2, :]
                    nc.vector.tensor_copy(pos_r, src[:, 1024:1536])
                    link(nc.vector.tensor_copy(aug_hi, src[:, 0:1024]))
                    tt(aug_lo, src[:, 0:1024], aug_hi.bitcast(f32), ALU.subtract).then_inc(w_split, 1)

            def rest_of_hidden(n):
                dve.wait_ge(hi_done, n + 1)
                tt(h_lo[:, n % 4, :], hid[:, n % 4, :], h_hi[:, n % 4, :].bitcast(f32), ALU.subtract).then_inc(lo_done, 1)

            split_block(1, w_hi[:, 0, :], w_lo[:, 0, :], 3 * F0)
            for j in range(len(JOBS)):
                for i in range(steps(j)):
                    n = first_step(j) + i
                    run(j, i, (0,))
                    dve.wait_ge(silu_done, n + 1)
                    if attends(j):
                        link(nc.vector.tensor_scalar(gate[:, n % 2, :], gate[:, n % 2, :], 0.5, 0.5, ALU.mult, ALU.add))
                        link(nc.vector.scalar_tensor_tensor(gate[:, n % 2, :], pg[0][:, :], b13[:, 0, i:i + 1],
                                                            gate[:, n % 2, :], ALU.add, ALU.mult))
                    dve.wait_ge(up_mm, n + 1)
                    if n >= 4:
                        dve.wait_ge(lo_done, n - 3)
                    if j < 8:
                        tt(hid[:, n % 4, :], pu[n % 2][:, :], gate[:, n % 2, :], ALU.mult).then_inc(hid_done, 1)
                    else:
                        k = 0 if attends(j) else n % 2
                        nc.vector.scalar_tensor_tensor(hid[:, n % 4, :], pu[k][:, :], b13[:, 1, i:i + 1],
                                                       gate[:, n % 2, :], ALU.add, ALU.mult).then_inc(hid_done, 1)
                    run(j, i, (1, 2))
                    if n >= 2:
                        rest_of_hidden(n - 2)
                    more_weights(j, i)
            rest_of_hidden(first_step(len(JOBS)) - 2)
            rest_of_hidden(first_step(len(JOBS)) - 1)
            post_add(len(JOBS) - 1, 0)

        @block.sync
        def _(sp):
            def load_x(c):
                sp.dma_start(x[:, c * TI:(c + 1) * TI, :],
                             x_d[c * CT:(c + 1) * CT, :].rearrange("(t p) d -> p t d", p=P)).then_inc(x_in[c], 16)

            def stage(k):
                if k == 2:
                    sp.wait_ge(ws_split, 1)
                if k >= 3:
                    sp.wait_ge(w_split, k - 2)
                if k == E0 + 1:
                    sp.wait_ge(rec_y, CH)
                src = ws_d if k == 0 else wf_d[k - 1] if k <= E0 else wg_d[k - E0 - 1] if k < E0 + 5 \
                    else wa_d if k == E0 + 5 else aug_d
                sp.dma_start(arena[0:src.shape[0], k % 2, 0:src.shape[1]], src).then_inc(staged[k % 2], 16)

            def store(j):
                c = JOBS[j][1]
                sp.wait_ge(x_added, j + 1)
                sp.dma_start(out_d[c * CT:(c + 1) * CT, :].rearrange("(t p) d -> p t d", p=P),
                             x[:, c * TI:(c + 1) * TI, :]).then_inc(stored, 16)

            sp.dma_start(const[:, :], const_d).then_inc(consts_in, 16)
            load_x(0)
            stage(0)
            for dst, src in smalls:
                sp.dma_start(dst, src).then_inc(smalls_in, 16)
            stage(1)
            stage(2)
            for c in range(1, CH):
                load_x(c)
            load = 0
            for j in range(len(JOBS)):
                sp.wait_ge(w_stored, 16 * nth_route(*JOBS[j]))
                if j >= 8:
                    if j > 8:
                        sp.wait_ge(b2_mm, j - 8)
                    sp.dma_start(wTm[:, :], w_scr[j]).then_inc(wTm_in, 16)
                for e in range(E0 if j < 8 else E1):
                    if load >= 4:
                        old = load - 4
                        done = FB * (old + 1) if old < 8 * E0 else 8 * S0N + old - 8 * E0 + 1
                        sp.wait_ge(weighted, done)
                    sp.dma_start(wbc[:, load % 4, :], w_scr[j, e:e + 1, :].to_broadcast([P, CT])).then_inc(wbc_in[load % 4], 16)
                    load += 1
                    if j == 0 and e + 3 <= E0:
                        stage(e + 3)
                    if j == 7 and e in (0, 1):
                        stage(E0 + 1 + e)
                    if j == 7 and e in (4, 5):
                        stage(E0 - 1 + e)
                    if j == 8 and e in (0, 1):
                        stage(E0 + 5 + e)
                if j >= 13:
                    store(j - 1)
            store(len(JOBS) - 1)
            sp.wait_ge(stored, 16 * CH)


def _constants():
    c = np.zeros((P, C_END), np.float32)
    c[:, C_ID:C_ID + P] = np.eye(P)
    c[:, C_IOTA:C_IOTA + E1] = np.arange(E1)
    c[:, C_TRI:C_TRI + GR * GR] = np.tril(np.ones((GR, GR)), -1).reshape(-1)
    r = np.arange(P) % 32
    c[:, C_MLQ] = -((r >= 2 * HD) & (r < 3 * HD) | (r == 25) | (r == 27)).astype(np.float32)
    c[:, C_MLK] = -((r >= HD) & (r < 2 * HD)).astype(np.float32)
    c[:, C_POW:C_POW + TI] = -0.5
    c[:, C_EPS:C_EPS + TI] = EPS
    upper = np.triu(np.full((P, P), -1e30, np.float32), 1)
    c[:, C_MASK1:C_MASK1 + P] = upper
    c[:, C_MASK2:C_MASK2 + P] = upper.T
    return c


def _by_head(w):
    lead = w.shape[:-1]
    out = np.zeros(lead + (HG, 4, 4, HD), np.float32)
    out[..., 0:3, :] = w.reshape(lead + (HG, 4, 1, HD))
    return out.reshape(lead + (HG * P,))


def _added_rows(bq, bk):
    aug = np.zeros((2, 2, HG, 4, 32), np.float32)
    aug[0, 0] = _by_head(bq).reshape(HG, 4, 32)
    aug[0, 1] = _by_head(bk).reshape(HG, 4, 32)
    slope = (np.float32(2.0 ** (-8.0 / H)) ** np.arange(1, H + 1, dtype=np.float32)).reshape(HG, 4)
    slope = slope * np.sqrt(np.float32(HD))
    aug[0, 0, :, :, 24] = aug[0, 0, :, :, 25] = slope
    aug[1, 1, :, :, 24:26] = 1.0
    aug[1, 0, :, :, 26] = aug[1, 0, :, :, 27] = -slope
    aug[0, 1, :, :, 26:MROW + 1] = 1.0
    return aug.reshape(2, -1)


def kernel(**inputs):
    import concourse.bacc as bacc
    from concourse.bass_utils import run_bass_kernel_spmd

    i = {k: np.asarray(v) for k, v in inputs.items()}
    wf = np.zeros((E0, P, 3, F0), np.float32)
    wf[:, :, 0] = i["L0_ffn_W_gate"].transpose(0, 2, 1)
    wf[:, :, 1] = i["L0_ffn_W_up"].transpose(0, 2, 1)
    wf[:, :, 2] = i["L0_ffn_W_down"].reshape(E0, D, FB, P).transpose(0, 3, 2, 1).reshape(E0, P, F0)
    wg = np.stack([i["L1_ffn_W1"].transpose(0, 2, 1), i["L1_ffn_W3"].transpose(0, 2, 1),
                   i["L1_ffn_W2"].transpose(0, 2, 1)], 2)
    wg = wg.reshape(4, 4, P, 3 * P).transpose(0, 2, 1, 3)
    wz = np.zeros((P, 4, P), np.float32)
    bf = np.zeros((P, 4), np.float32)
    wfT, b_f = i["L0_attn_W_f"].T, i["L0_attn_b_f"]
    wfd = np.zeros((P, 2, D), np.float32)
    for k, (a, b) in enumerate(((0, P), (P, EH))):
        wz[:, 2 * k, 0:b - a], wz[:, 2 * k + 1, 0:b - a] = wfT[:, a:b], wfT[:, EH + a:EH + b]
        bf[0:b - a, 2 * k], bf[0:b - a, 2 * k + 1] = b_f[a:b], b_f[EH + a:EH + b]
        wfd[0:b - a, k] = i["L0_attn_W_down"].T[a:b]
    ws = np.concatenate([wz.reshape(P, 4 * P), i["L0_ffn_W_router"].T, i["L1_ffn_Wg"].T], 1)
    wa = np.concatenate([_by_head(i["L1_attn_Wq"]), _by_head(i["L1_attn_Wk"]), i["L1_attn_Wv"]], 1)
    pos = np.stack([np.ones(CT, np.float32), np.tile(np.arange(SEQ, dtype=np.float32), NB)])
    arrays = dict(
        x=i["L0_attn_x"].reshape(TOK, D), const=_constants(), wf=wf.reshape(E0, P, 3 * F0),
        wg=wg.reshape(4, P, 12 * P), ws=ws, wa=wa, wfd=wfd, wo=i["L1_attn_Wo"], bf=bf,
        b13=np.stack([i["L1_ffn_b1"].T, i["L1_ffn_b3"].T], 1), b2=i["L1_ffn_b2"],
        aug=np.concatenate([_added_rows(i["L1_attn_bq"], i["L1_attn_bk"]), pos], 1),
        bv=i["L1_attn_bv"].reshape(1, D), bo=i["L1_attn_bo"].reshape(1, D))
    nc = bacc.Bacc("TRN2", target_bir_lowering=False, num_devices=1)
    feed, args = {}, []
    for name, a in arrays.items():
        feed[f"in_{name}"] = np.ascontiguousarray(a)
        args.append(nc.dram_tensor(f"in_{name}", a.shape, mybir.dt.from_np(a.dtype), kind="ExternalInput").ap())
    args.append(nc.dram_tensor("out_x", (TOK, D), mybir.dt.float32, kind="ExternalOutput").ap())
    build(nc, *args)
    r = run_bass_kernel_spmd(nc, [feed], core_ids=[0])
    return r.results[0]["out_x"].reshape(TOK // SEQ, SEQ, D)
```

```python
from contextlib import ExitStack

import numpy as np
import concourse.bass as bass
import concourse.mybir as mybir

P = 128
TOK = 2048
SEQ = 256
CH = 4
CT = TOK // CH
TI = CT // P
NB = CT // SEQ
D = 128
E0, F0, FB = 8, 512, 4
E1 = 16
GR = 4
H, HD = 16, 8
HG = 4
EH = 192
MROW = 28
UNITS = NB * HG
SCALE = 1.0 / float(np.sqrt(np.float32(HD)))
EPS = 1e-5
S0N, S1N = E0 * FB, E1
LAG = 4

C_ID, C_IOTA, C_TRI, C_MLQ, C_MLK, C_POW, C_EPS = 0, 128, 144, 160, 161, 162, 166
C_MASK1, C_MASK2, C_END = 170, 298, 426

JOBS = [("F1", c) for c in range(CH)] + [("F2", c) for c in range(CH)] \
     + [("G1", c) for c in range(CH)] + [("G2", c) for c in range(CH)]


def job_of(stage, c):
    return JOBS.index((stage, c))


def first_step(j):
    return S0N * min(j, 8) + S1N * max(j - 8, 0)


def steps(j):
    return S0N if j < 8 else S1N


def norm_pieces(stage, c):
    return [(n, stage, c) for n in ("ln_stats", "ln_rstd", "ln_scale", "ln_transpose", "ln_hi", "ln_lo")]


def weigh_pieces(stage, c):
    names = ["route_logits"]
    names += ["f_top", "f_gap", "f_places", "f_gates"] if stage[0] == "F" else \
        ["g_exp", "g_sigmoid", "g_groups", "g_choose", "g_top", "g_places", "g_weights"]
    return [(n, stage, c) for n in names + ["route_transpose", "route_out"]]


def route_pieces(stage, c):
    return norm_pieces(stage, c) + weigh_pieces(stage, c)


def attention_lanes():
    at = [(c, u) for c in range(CH) for u in range(UNITS)]
    ends = [(n, c, b, t) for c in range(CH) for b in range(NB) for t in range(SEQ // P)
            for n in ("att_gather", "att_norm", "att_turn", "att_turn_out", "att_out", "att_add")]
    exps = [piece for c, u in at for piece in
            [("att_exp", c, u, p) for p in range(3)] + [("att_exp_out", c, u, p) for p in range(3)]
            + [("att_pv", c, u), ("att_pv_out", c, u)]]
    tops = [piece for c, u in at for piece in
            [("att_keys", c, u)] + [("att_max", c, u, p) for p in range(3)] + [("att_max_out", c, u, p) for p in range(3)]
            + [("att_shift", c, u), ("att_shift_out", c, u)]]
    qkv = [piece for c in range(CH) for piece in
           [(n, c, i) for i in range(2 * HG) for n in ("att_qk", "att_qk_hi", "att_qk_split")]
           + [(n, c, b) for b in range(NB) for n in ("att_v", "att_v_out")]]
    return [ends, exps, tops, qkv]


def lanes():
    out = [weigh_pieces("F1", 0)]
    out += [[("post_transpose", j, 0), ("post_add", j, 0)] for j in range(len(JOBS) - 1)]
    for stage in ("F1", "A", "F2", "G1", "B", "G2"):
        for c in range(CH):
            if stage == "A":
                rec = [(n, c, k) for k in range(2) for n in ("rec_project", "rec_gates", "rec_input", "rec_scan")]
                out.append(norm_pieces("A", c) + rec + [("rec_down", c, 0), ("rec_add", c, 0)])
            elif stage == "B":
                out.append(norm_pieces("B", c))
            elif (stage, c) != ("F1", 0):
                out.append(route_pieces(stage, c))
    return out + attention_lanes()


TAKES = dict(ln_stats="N", ln_transpose="a", route_logits="Rb", route_transpose="b", post_transpose="c",
             rec_project="ab", rec_down="c", att_qk="ab", att_v="c", att_max="ag", att_shift="bu", att_exp="bu",
             att_pv="c", att_gather="c", att_turn="c", att_out="c")
GIVES = dict(ln_lo="aN", f_top="b", g_exp="b", route_out="bR", post_add="c", rec_input="ab", rec_add="c",
             att_qk_split="ab", att_v_out="c", att_max_out="ag", att_shift_out="bu", att_exp_out="bu",
             att_pv_out="c", att_norm="c", att_turn_out="c", att_add="c")


def nth_part(c, u, p):
    return 3 * (UNITS * c + u) + p


def found(table, piece):
    name = piece[0]
    out = table.get(name, "")
    if out and name in ("att_qk", "att_qk_split"):
        out = out[piece[2] % 2]
    if out and name in ("att_max", "att_max_out", "att_exp", "att_exp_out"):
        out = out[nth_part(*piece[1:]) % 2]
    if out and name in ("att_shift", "att_shift_out"):
        out = out[nth_part(*piece[1:], 0) % 2]
    if table is TAKES and name == "ln_transpose" and piece[1] in ("A", "B"):
        out += "H"
    if table is GIVES and (name == "rec_project" and piece[2] == 1 or name == "att_v" and piece[2] == NB - 1):
        out += "H"
    return out


def needs(piece, last):
    name, c = piece[0], piece[2] if len(piece) > 2 else 0
    if name == "ln_stats":
        return [{"F1": None, "A": ("post_add", c, 0), "F2": ("rec_add", c, 0), "G1": ("post_add", 4 + c, 0),
                 "B": ("post_add", 8 + c, 0), "G2": ("att_add", c, NB - 1, SEQ // P - 1)}[piece[1]]]
    if name == "route_logits":
        return [("ln_lo",) + piece[1:]]
    if name == "rec_project":
        return [("ln_lo", "A", piece[1])]
    if not name.startswith("att_"):
        return [last]
    c, u = piece[1:3]
    b, g = divmod(u, HG)
    unit = lambda name, d, *p: (name,) + divmod(UNITS * c + u - d, UNITS) + p if UNITS * c + u >= d else None
    part = lambda name, d, *p: (name,) + divmod(2 * HG * c + u - d, 2 * HG) + p if 2 * HG * c + u >= d else None
    if name in ("att_qk", "att_qk_split"):
        g, wants = u // 2, [("ln_lo", "B", c)] if name == "att_qk" else [("att_qk_hi", c, u)]
        return wants + ([(n, c - 1, UNITS - HG + g) + p for n, p in
                         (("att_keys", ()), ("att_max", (2,)), ("att_shift_out", ()))] if c else [])
    if name == "att_qk_hi":
        return [("att_qk", c, u), part("att_qk_split", 2)]
    if name in ("att_v", "att_v_out"):
        return [("ln_lo", "B", c) if name == "att_v" else ("att_v", c, u),
                ("att_pv",) + divmod(UNITS * c + HG * u - 1, UNITS) if c or u else None]
    if name == "att_keys":
        return [("att_qk_split", c, 2 * g + 1), unit("att_exp", 2, 2)]
    if name == "att_max":
        return [("att_keys", c, u)]
    if name == "att_max_out":
        return [("att_max",) + piece[1:], unit("att_shift", 1)]
    if name == "att_shift":
        return [("att_max_out", c, u, 2)]
    if name == "att_shift_out":
        return [("att_shift", c, u), unit("att_exp", 2, 2)]
    if name == "att_exp":
        return [("att_shift_out", c, u)]
    if name == "att_exp_out":
        return [("att_exp",) + piece[1:], unit("att_pv", 1)]
    if name == "att_pv":
        return [("att_exp_out", c, u, 2), ("att_v_out", c, b)]
    if name == "att_pv_out":
        return [("att_pv", c, u)] + ([("att_gather",) + divmod(NB * c + b - 1, NB) + (SEQ // P - 1,)] if g == 0 and c + b else [])
    if name == "att_gather":
        return [("att_pv_out", c, HG * u + HG - 1)]
    chain = ["att_gather", "att_norm", "att_turn", "att_turn_out", "att_out", "att_add"]
    t = piece[3]
    k = (SEQ // P) * (NB * c + u) + t - 1
    before = divmod(k // (SEQ // P), NB) + (k % (SEQ // P),)
    return [(chain[chain.index(name) - 1],) + piece[1:]] + \
        ([(chain[chain.index(name) + 1],) + before] if k >= 0 and name in ("att_norm", "att_turn_out") else [])


PE_LEN = dict(ln_transpose=.85, route_logits=1., route_transpose=.85, post_transpose=.85, rec_project=1.28,
             rec_down=1.7, att_qk=1.07, att_v=.64, att_max=.43, att_shift=.43, att_exp=.43, att_pv=2.56,
             att_gather=.85, att_turn=.21, att_out=.32)
ACT_LEN = dict(ln_hi=.55, f_gap=.3, g_exp=.3, route_out=.6, rec_gates=1.6, att_qk_hi=.55, att_exp_out=.55,
              att_pv_out=.4, att_turn_out=.3)
POOL_LEN = dict(ln_rstd=.5)
DVE_LEN = dict(ln_stats=1.6, ln_scale=.7, ln_lo=.65, f_top=1.6, f_places=.3, f_gates=1., g_sigmoid=.4, g_groups=1.,
              g_choose=1., g_top=1.3, g_places=.5, g_weights=1.2, post_add=.7, rec_input=1.4, rec_scan=1.4,
              rec_add=.7, att_qk_split=.7, att_v_out=.5, att_keys=.5, att_max_out=.65, att_shift_out=.45,
              att_norm=.4, att_add=.25)
LENGTHS = dict(PE=PE_LEN, ACT=ACT_LEN, POOL=POOL_LEN, DVE=DVE_LEN)
SPLIT_LEN = 2.9
HOP, DMA_LEN = .3, 8.
BACKLOG = 1.
KEPT = first_step(14) + 4


def place():
    engine_of = {name: e for e, table in LENGTHS.items() for name in table}
    queues = []
    for pieces in lanes():
        queue = {e: [] for e in LENGTHS}
        for last, piece in zip([("ln_lo", "F1", 0)] + pieces, pieces):
            queue[engine_of[piece[0]]].append((piece, needs(piece, last)))
        queues.append(queue)
    total = first_step(len(JOBS))
    job = [j for j in range(len(JOBS)) for _ in range(steps(j))]
    free = dict.fromkeys(LENGTHS, 0.0)
    end = {None: 0.0, ("ln_lo", "F1", 0): 0.0}
    gate, hid, weighed, low = {}, {}, {}, {}
    others = len(queues) - len(attention_lanes())
    held, given = set(), {}
    out = [{} for _ in JOBS]
    group = 0

    def run(engine, ready, length):
        free[engine] = max(free[engine], ready) + length
        return free[engine] + HOP

    def ready(piece, wants):
        if job[(group - 1) // 3] not in ATTENDS and set("gu") & set(found(TAKES, piece)):
            return None
        if piece[0] == "post_transpose":
            wants = [("sum", piece[1])]
        if piece[0] == "ln_rstd":
            wants = wants + [("route_out",) + JOBS[job[(group - 1) // 3]]]
        if any(w not in end for w in wants) or any(x in held for x in found(TAKES, piece)):
            return None
        return max([end[w] + DMA_LEN * (w is not None and w[0] == "route_out") for w in wants]
                   + [given.get(x, 0.0) for x in found(TAKES, piece)])

    def add(engine, piece, at):
        n = (group - 1) // 3
        end[piece] = run(engine, at, LENGTHS[engine][piece[0]])
        if piece[0] == "att_keys":
            run("ACT", at, .6)
        held.update(found(TAKES, piece))
        for x in found(GIVES, piece):
            held.discard(x)
            given[x] = end[piece]
        j = job[n]
        out[j].setdefault(group - 1 - 3 * first_step(j), []).append(piece)

    def group_ready():
        n, sub = divmod(group, 3)
        j = job[n]
        if sub == 0:
            wants = [("ln_lo",) + JOBS[j]]
            if n >= KEPT:
                wants.append(("att_add", CH - 1, NB - 1, SEQ // P - 1))
            if n >= first_step(j) + 2:
                wants.append(("route_out",) + JOBS[j])
            if any(w not in end for w in wants) or (j not in ATTENDS and set("gu") & held):
                return None
            at = max(end[w] + DMA_LEN * (w[0] == "route_out") for w in wants)
            last = n - 1 if j in ATTENDS else n - 2
            return max(at, gate.get(last, 0.0))
        if sub == 1:
            return hid.get(n - 1 if j in ATTENDS else n - 2, 0.0)
        return low.get(n - LAG, 0.0)

    def add_group(at):
        nonlocal group
        n, sub = divmod(group, 3)
        j = job[n]
        if sub == 0:
            if n >= 3:
                by_pool = job[n - 3] in ATTENDS
                low[n - 3] = run("POOL" if by_pool else "DVE", run("ACT", weighed[n - 3], .53), 1.25 if by_pool else .62)
            if j and n == first_step(j) + LAG:
                end["sum", j - 1] = run("ACT", free["PE"], .53)
            gate[n] = run("ACT", run("PE", at, .64), 1.25 if j in ATTENDS else .6)
            if (j == 0 and n % FB == 1) or (j == 7 and n - first_step(j) in (9, 13, 17, 21)):
                free["DVE"] += SPLIT_LEN
        elif sub == 1:
            up = run("PE", at, .64)
            if j in ATTENDS:
                gate[n] = run("DVE", gate[n], .67)
            hid[n] = run("DVE", max(up, gate[n]), .67)
            weighed[n] = run("POOL", hid[n], 1.25)
        elif n >= LAG:
            run("PE", at, .64)
        group += 1

    free["DVE"] = SPLIT_LEN
    add_group(SPLIT_LEN)
    while group < 3 * total or any(q for queue in queues for q in queue.values()):
        moved = False
        for queue in queues:
            for e in ("ACT", "POOL", "DVE"):
                while queue[e]:
                    at = ready(*queue[e][0])
                    if at is None or at > max(free["PE"], free[e]):
                        break
                    if queue[e][0][0][0][:2] in ("f_", "g_") and free[e] > free["PE"] + BACKLOG:
                        break
                    add(e, queue[e].pop(0)[0], at)
                    moved = True
        heads = [(at, n) for n, queue in enumerate(queues) if queue["PE"]
                 for at in [ready(*queue["PE"][0])] if at is not None]
        now = [h for h in heads if h[0] <= free["PE"] + .05]
        if now:
            at, n = min(now, key=lambda h: (h[1] < others, h[1]))
            add("PE", queues[n]["PE"].pop(0)[0], at)
            continue
        if moved:
            continue
        at = group_ready() if group < 3 * total else None
        if at is not None and at <= free["PE"] + .05:
            add_group(at)
            continue
        rest = [at for queue in queues for e in ("ACT", "POOL", "DVE") if queue[e]
                  for at in [ready(*queue[e][0])] if at is not None]
        times = [h[0] for h in heads] + rest + [at] * (at is not None)
        free["PE"] = max(free["PE"] + .05, min(times))
    return out


ATTENDS = range(10, 14)
PLACED = place()
NORMS = [("F1", 0)] + [(p[1], p[2]) for at in PLACED for g in sorted(at) for p in at[g] if p[0] == "ln_stats"]
ROUTES = [(p[1], p[2]) for at in PLACED for g in sorted(at) for p in at[g] if p[0] == "route_logits"]


def build(nc, x_d, const_d, wf_d, wg_d, ws_d, wa_d, wfd_d, wo_d, bf_d, b13_d, b2_d, aug_d, bv_d, bo_d, out_d):
    f32, f32r, bf16, u32 = mybir.dt.float32, mybir.dt.float32r, mybir.dt.bfloat16, mybir.dt.uint32
    ALU, ACT, AX = mybir.AluOpType, mybir.ActivationFunctionType, mybir.AxisListType
    ctx = ExitStack()
    with ctx:
        def sb(name, shape, dt=f32):
            return ctx.enter_context(nc.sbuf_tensor(name, shape, dt))

        def ps(name):
            return ctx.enter_context(nc.psum_tensor(name, [P, 512], f32))

        def sem(name):
            return ctx.enter_context(nc.semaphore(name))

        x = sb("x", [P, CH * TI, D])
        w_hi = sb("w_hi", [P, E0, 3 * F0], f32r)
        w_lo = sb("w_lo", [P, E0, 3 * F0], f32r)
        ws_hi = sb("ws_hi", [P, 536], f32r)
        ws_lo = sb("ws_lo", [P, 536], f32r)
        arena = sb("arena", [P, 2, 1536])
        n_hi = sb("n_hi", [P, TOK], f32r)
        n_lo = sb("n_lo", [P, TOK], f32r)
        a_hi = sb("a_hi", [P, CT], f32r)
        a_lo = sb("a_lo", [P, CT], f32r)
        nrm = sb("nrm", [P, TI, D])
        gate = sb("gate", [P, 2, CT])
        hid = sb("hid", [P, 4, CT])
        h_hi = sb("h_hi", [P, 4, CT], f32r)
        h_lo = sb("h_lo", [P, 4, CT], f32r)
        wbc = sb("wbc", [P, 4, CT])
        y_fm = sb("y_fm", [P, CT])
        wT = sb("wT", [E1, CT])
        wTm = sb("wTm", [E1, CT])
        vpad = sb("vpad", [P, SEQ // P, H, 32])
        k_one = sb("k_one", [P, 2, 4, SEQ], f32r)
        const = sb("const", [P, C_END])
        ident_b = sb("ident_b", [P, P], bf16)
        mask1_b = sb("mask1_b", [P, P], bf16)
        mask2_b = sb("mask2_b", [P, P], bf16)
        wfd = sb("wfd", [P, 2, D])
        wo = sb("wo", [P, D])
        bf = sb("bf", [P, 4])
        bf_2 = sb("bf_2", [P, 4])
        bf_up = sb("bf_up", [P, 4])
        b13 = sb("b13", [P, 2, E1])
        b1_half = sb("b1_half", [P, E1])
        b2 = sb("b2", [E1, D])
        bv = sb("bv", [P, D])
        bo = sb("bo", [1, D])
        ones_row = sb("ones_row", [1, P])
        stats = sb("stats", [P, TI, 6])
        mv = sb("mv", [P, TI, 2])
        rstd = sb("rstd", [P, TI])
        mpad = sb("mpad", [P, SEQ // P, P])
        rden = sb("rden", [P, H])
        o_tm = sb("o_tm", [P, H, HD])
        o_fm = sb("o_fm", [P, P])
        lg = sb("lg", [P, TI, E1])
        sc = sb("sc", [P, TI, E1])
        top = sb("top", [P, TI, 8])
        topi = sb("topi", [P, TI, 8], u32)
        topf = sb("topf", [P, TI, 8])
        hot = sb("hot", [P, TI, E1, 4])
        gmax = sb("gmax", [P, TI, GR])
        gcmp = sb("gcmp", [P, TI, GR, GR])
        gcmq = sb("gcmq", [P, TI, GR, GR])
        gsel = sb("gsel", [P, TI, GR])
        gsel1 = sb("gsel1", [P, TI, GR])
        wtm = sb("wtm", [P, TI, E1])
        gap = sb("gap", [P, TI])
        egap = sb("egap", [P, TI])
        gk = sb("gk", [P, TI, 2])
        den = sb("den", [P, TI])

        rec = arena[:, :, :].rearrange("p a n -> p (a n)")
        r_a, r_z, r_g = (rec[:, i * CT:(i + 1) * CT] for i in range(3))
        r_h = [rec[:, (3 + k) * CT:(4 + k) * CT] for k in range(2)]
        prob = rec[:, 0:3 * CT]
        o_pad = rec[:, 3 * CT:5 * CT].rearrange("p (g t) -> p g t", g=HG)
        wh = w_hi[:, 4:8, :].rearrange("p a n -> p (a n)")
        wl = w_lo[:, 4:8, :].rearrange("p a n -> p (a n)")
        q_r = wh[:, 0:2048].rearrange("p (g t) -> p g t", g=HG)
        k_r = wh[:, 2048:4096].rearrange("p (g t) -> p g t", g=HG)
        wa_hi, wa_lo = wh[:, 4096:4096 + 1152], wl[:, 4096:4096 + 1152]
        qs_r = wh[:, 5248:5248 + 512].rearrange("p (i t) -> p i t", i=2)
        qk_hi = wl[:, 0:1024].rearrange("p (i t) -> p i t", i=2)
        aug_hi, aug_lo, pos_r = wl[0:2, 1024:2048], wl[0:2, 2048:3072], wl[0:2, 3072:3584]

        ident = const[:, C_ID:C_ID + P]
        w_scr = nc.dram_tensor("w_scr", (len(JOBS), E1, CT), f32, kind="Internal").ap()

        pg = [ps(f"pg{i}") for i in range(2)]
        pu = [ps(f"pu{i}") for i in range(2)]
        pacc = ps("pacc")
        pa, pb, pc = ps("pa"), ps("pb"), ps("pc")

        table_in = sem("table_in")
        consts_in, smalls_in, x_in = sem("consts_in"), sem("smalls_in"), [sem(f"x_in{i}") for i in range(CH)]
        staged = [sem(f"staged{i}") for i in range(2)]
        w_split = sem("w_split")
        ws_split = sem("ws_split")
        setup_dve, setup_pool = sem("setup_dve"), sem("setup_pool")
        dve_chain, pool_chain = sem("dve_chain"), sem("pool_chain")
        gate_mm, up_mm, down_mm = sem("gate_mm"), sem("up_mm"), sem("down_mm")
        tanh_done, gate_read = sem("tanh_done"), sem("gate_read")
        silu_done, weighted, hid_done, hi_done, lo_done = (
            sem(n) for n in ("silu_done", "weighted", "hid_done", "hi_done", "lo_done"))
        wbc_in = [sem(f"wbc_in{i}") for i in range(4)]
        wTm_in, b2_mm = sem("wTm_in"), sem("b2_mm")
        y_out, y_turned, x_added = sem("y_out"), sem("y_turned"), sem("x_added")
        ln_mv, ln_rs, ln_nrm, ln_T, ln_hi, ln_lo = (
            sem(n) for n in ("ln_mv", "ln_rs", "ln_nrm", "ln_T", "ln_hi", "ln_lo"))
        lg_mm, lg_read, lg_act, act_exp, w_tm, wT_mm, wT_out, w_stored = (
            sem(n) for n in ("lg_mm", "lg_read", "lg_act", "act_exp", "w_tm", "wT_mm", "wT_out", "w_stored"))
        rec_mm, rec_sig, rec_read, rec_h, rec_y, rec_x = (sem(n) for n in ("rec_mm", "rec_sig", "rec_read", "rec_h", "rec_y", "rec_x"))
        qk_mm, qk_rd, qk_res = sem("qk_mm"), sem("qk_rd"), sem("qk_res")
        v_mm, v_out = sem("v_mm"), sem("v_out")
        k_apart1, k_apart2 = sem("k_apart1"), sem("k_apart2")
        s1_mm, s1_max, m_T, q_shift, s2_mm, s2_exp, pv_mm, pv_out = (
            sem(n) for n in ("s1_mm", "s1_max", "m_T", "q_shift", "s2_mm", "s2_exp", "pv_mm", "pv_out"))
        o_T, o_nrm, o_T2, o_T2out, att_y, att_x = (
            sem(n) for n in ("o_T", "o_nrm", "o_T2", "o_T2out", "att_y", "att_x"))
        stored = sem("stored")

        block = ctx.enter_context(nc.Block())

        smalls = [(wfd[:, :, :], wfd_d), (wo[:, :], wo_d), (bf[:, :], bf_d), (b13[:, :, :], b13_d), (b2[:, :], b2_d),
                  (const[:, C_MASK1:C_END], const_d[:, C_MASK1:C_END]), (bv[:, :], bv_d.to_broadcast([P, D])), (bo[:, :], bo_d)]

        def nth_norm(stage, c):
            return NORMS.index((stage, c)) + 1

        def nth_route(stage, c):
            return ROUTES.index((stage, c)) + 1

        def norm_target(stage, c):
            if stage in ("A", "B"):
                return a_hi[:, :], a_lo[:, :]
            return n_hi[:, c * CT:(c + 1) * CT], n_lo[:, c * CT:(c + 1) * CT]

        def x_ready(eng, stage, c):
            if stage == "F1":
                eng.wait_ge(x_in[c], 16)
            elif stage == "F2":
                eng.wait_ge(rec_x, c + 1)
            elif stage == "G2":
                eng.wait_ge(att_x, 4 * (c + 1))
            else:
                eng.wait_ge(x_added, {"A": 0, "G1": 4, "B": 8}[stage] + c + 1)

        def lo_by_pool(n):
            return first_step(ATTENDS[0]) <= n < first_step(ATTENDS[-1] + 1)

        def pieces_at(j, i, subs):
            return [piece for s in subs for piece in PLACED[j].get(3 * i + s, [])]

        @block.tensor
        def _(pe):
            def mm3(out, lh, ll, rh, rl, start=True, stop=True):
                nc.tensor.matmul(out, lh, rh, start=start, stop=False)
                nc.tensor.matmul(out, lh, rl, start=False, stop=False)
                return nc.tensor.matmul(out, ll, rh, start=False, stop=stop)

            reader = {bank: None for bank in ("pa", "pb", "pc", "pg0", "pg1", "pu0", "pu1")}

            def take(bank):
                if reader[bank] is not None:
                    pe.wait_ge(*reader[bank])

            def ln_transpose(stage, c):
                n = nth_norm(stage, c)
                pe.wait_ge(ln_nrm, n)
                take("pa")
                for t in range(TI):
                    last = nc.tensor.transpose(pa[:, t * P:(t + 1) * P], nrm[:, t, :], ident)
                last.then_inc(ln_T, 1)
                reader["pa"] = (ln_lo, n)

            def route_logits(stage, c):
                n = nth_norm(stage, c)
                e, off = (E0, 512) if stage[0] == "F" else (E1, 520)
                pe.wait_ge(ln_hi, n)
                pe.wait_ge(ln_lo, n)
                take("pb")
                for t in range(TI):
                    s = slice(c * CT + t * P, c * CT + (t + 1) * P)
                    last = mm3(pb[:, t * e:(t + 1) * e], n_hi[:, s], n_lo[:, s], ws_hi[:, off:off + e], ws_lo[:, off:off + e])
                last.then_inc(lg_mm, 1)
                reader["pb"] = (lg_read, nth_route(stage, c))

            def route_transpose(stage, c):
                n = nth_route(stage, c)
                e = E0 if stage[0] == "F" else E1
                pe.wait_ge(w_tm, n)
                take("pb")
                for t in range(TI):
                    last = nc.tensor.transpose(pb[0:e, t * P:(t + 1) * P], wtm[:, t, 0:e], ident)
                last.then_inc(wT_mm, 1)
                reader["pb"] = (wT_out, n)

            def post_transpose(j, _):
                pe.wait_ge(y_out, j + 1)
                take("pc")
                for t in range(TI):
                    last = nc.tensor.transpose(pc[:, t * P:(t + 1) * P], y_fm[:, t * P:(t + 1) * P], ident)
                last.then_inc(y_turned, 1)
                reader["pc"] = (x_added, j + 1)

            def rec_project(c, k):
                pe.wait_ge(setup_dve, 1)
                pe.wait_ge(ln_hi, nth_norm("A", c))
                pe.wait_ge(ln_lo, nth_norm("A", c))
                for i, (name, bank) in enumerate((("pa", pa), ("pb", pb))):
                    take(name)
                    o = (2 * k + i) * P
                    last = mm3(bank[:, :], ws_hi[:, o:o + P], ws_lo[:, o:o + P], a_hi[:, :], a_lo[:, :])
                    reader[name] = (rec_sig, 3 * (2 * c + k) + 1) if i == 0 else (rec_read, 2 * c + k + 1)
                last.then_inc(rec_mm, 1)

            def rec_down(c, _):
                pe.wait_ge(rec_h, 2 * (c + 1))
                take("pc")
                for t in range(TI):
                    s = slice(t * P, (t + 1) * P)
                    nc.tensor.matmul(pc[:, s], r_h[0][:, s], wfd[:, 0, :], start=True, stop=False)
                    last = nc.tensor.matmul(pc[:, s], r_h[1][0:EH - P, s], wfd[0:EH - P, 1, :], start=False, stop=True)
                last.then_inc(rec_y, 1)
                reader["pc"] = (rec_x, c + 1)

            def att_qk(c, i):
                if i == 0:
                    pe.wait_ge(setup_pool, 1)
                    pe.wait_ge(ln_hi, nth_norm("B", c))
                    pe.wait_ge(ln_lo, nth_norm("B", c))
                    pe.wait_ge(w_split, E0 + 6)
                g, what = i // 2, i % 2
                name, bank = (("pa", pa), ("pb", pb))[what]
                take(name)
                o = (what * HG + g) * P
                mm3(bank[:, :], wa_hi[:, o:o + P], wa_lo[:, o:o + P], a_hi[:, :], a_lo[:, :], stop=False)
                nc.tensor.matmul(bank[:, :], aug_hi[:, o:o + P], pos_r, start=False, stop=False)
                nc.tensor.matmul(bank[:, :], aug_lo[:, o:o + P], pos_r, start=False, stop=True).then_inc(qk_mm, 1)
                reader[name] = (qk_res, 8 * c + i + 1)

            def att_v(c, b):
                take("pc")
                for t in range(SEQ // P):
                    s = slice(b * SEQ + t * P, b * SEQ + (t + 1) * P)
                    last = mm3(pc[:, t * P:(t + 1) * P], a_hi[:, s], a_lo[:, s], wa_hi[:, 1024:1152], wa_lo[:, 1024:1152])
                last.then_inc(v_mm, 1)
                reader["pc"] = (v_out, 2 * c + b + 1)

            def att_max(c, u, p):
                b, g = divmod(u, HG)
                nth = nth_part(c, u, p)
                name, bank = (("pa", pa), ("pg1", pg[1]))[nth % 2]
                if p == 0:
                    pe.wait_ge(k_apart1, 8 * c + u + 1)
                    pe.wait_ge(k_apart2, 8 * c + u + 1)
                take(name)
                heads = range(4) if p == 0 else range(2 * p - 2, 2 * p)
                w = P if p == 0 else SEQ
                if w == P:
                    nc.tensor.matmul(bank[:, :], ident_b[:, :], mask1_b[:, :].unsqueeze(1).to_broadcast([P, 4, P]),
                                     start=True, stop=False)
                for i, h in enumerate(heads):
                    t0 = b * SEQ + (0 if p == 0 else P)
                    last = nc.tensor.matmul(bank[:, i * w:(i + 1) * w], q_r[:, g, t0:t0 + P], k_one[:, u % 2, h, 0:w],
                                            start=w > P, stop=w == P and h == heads[-1])
                    if w > P:
                        last = nc.tensor.matmul(bank[:, (i + 1) * w - P:(i + 1) * w], ident_b[:, :], mask1_b[:, :],
                                                start=False, stop=True)
                last.then_inc(s1_mm, 1)
                reader[name] = (s1_max, nth + 1)

            def att_shift(c, u):
                pe.wait_ge(s1_max, 3 * (8 * c + u + 1))
                name, bank = (("pb", pb), ("pu1", pu[1]))[nth_part(c, u, 0) % 2]
                take(name)
                for t in range(SEQ // P):
                    last = nc.tensor.transpose(bank[:, t * P:(t + 1) * P], mpad[:, t, :], ident)
                last.then_inc(m_T, 1)
                reader[name] = (q_shift, 8 * c + u + 1)

            def att_exp(c, u, p):
                b, g = divmod(u, HG)
                nth = nth_part(c, u, p)
                name, bank = (("pb", pb), ("pu1", pu[1]))[nth % 2]
                if p == 0:
                    pe.wait_ge(q_shift, 8 * c + u + 1)
                take(name)
                heads = range(4) if p == 2 else range(2 * p, 2 * p + 2)
                w = P if p == 2 else SEQ
                if w == P:
                    nc.tensor.matmul(bank[:, :], ident_b[:, :], mask2_b[:, :].unsqueeze(1).to_broadcast([P, 4, P]),
                                     start=True, stop=False)
                for i, h in enumerate(heads):
                    s0 = P if p == 2 else 0
                    last = nc.tensor.matmul(bank[:, i * w:(i + 1) * w], k_one[:, u % 2, h, s0:s0 + P],
                                            qs_r[:, u % 2, SEQ - w:SEQ], start=w > P, stop=w == P and h == heads[-1])
                    if w > P:
                        last = nc.tensor.matmul(bank[:, i * w:i * w + P], ident_b[:, :], mask2_b[:, :],
                                                start=False, stop=True)
                last.then_inc(s2_mm, 1)
                reader[name] = (s2_exp, nth + 1)

            def att_pv(c, u):
                b, g = divmod(u, HG)
                pe.wait_ge(s2_exp, 3 * (8 * c + u + 1))
                if g == 0:
                    pe.wait_ge(v_out, 2 * c + b + 1)
                take("pc")
                for h in range(4):
                    o = pc[32 * h:32 * h + 32, 0:SEQ]
                    hh = 4 * g + h
                    nc.tensor.matmul(o, vpad[:, 0, hh, :], prob[:, h * SEQ:(h + 1) * SEQ], start=True, stop=False)
                    last = nc.tensor.matmul(pc[32 * h:32 * h + 32, P:SEQ], vpad[:, 1, hh, :],
                                            prob[:, 4 * SEQ + h * P:4 * SEQ + (h + 1) * P], start=False, stop=True)
                last.then_inc(pv_mm, 1)
                reader["pc"] = (pv_out, 8 * c + u + 1)

            def att_gather(c, b, t):
                k = 2 * (2 * c + b) + t
                pe.wait_ge(pv_out, 4 * (2 * c + b + 1))
                take("pc")
                for g in range(HG):
                    last = nc.tensor.transpose(pc[:, g * P:(g + 1) * P], o_pad[:, g, t * P:(t + 1) * P], ident)
                last.then_inc(o_T, 1)
                reader["pc"] = (o_nrm, k + 1)

            def att_turn(c, b, t):
                k = 2 * (2 * c + b) + t
                take("pc")
                nc.tensor.transpose(pc[:, 0:P], o_tm[:, :, :].rearrange("p h d -> p (h d)"), ident).then_inc(o_T2, 1)
                reader["pc"] = (o_T2out, k + 1)

            def att_out(c, b, t):
                k = 2 * (2 * c + b) + t
                take("pc")
                nc.tensor.matmul(pc[:, 0:P], o_fm[:, :], wo[:, :], start=True, stop=False)
                nc.tensor.matmul(pc[:, 0:P], ones_row[:, :], bo[:, :], start=False, stop=True).then_inc(att_y, 1)
                reader["pc"] = (att_x, k + 1)

            mine = dict(ln_transpose=ln_transpose, route_logits=route_logits, route_transpose=route_transpose,
                        post_transpose=post_transpose, rec_project=rec_project, rec_down=rec_down, att_qk=att_qk,
                        att_v=att_v, att_max=att_max, att_shift=att_shift, att_exp=att_exp, att_pv=att_pv,
                        att_gather=att_gather, att_turn=att_turn, att_out=att_out)

            def run(j, i, sub):
                for name, *args in pieces_at(j, i, [sub]):
                    if name in mine:
                        mine[name](*args)

            def weights(j, i):
                if j < 8:
                    e, f = divmod(i, FB)
                    part = lambda w, k: w[:, e, k * F0 + f * P:k * F0 + (f + 1) * P]
                    return [(part(w_hi, k), part(w_lo, k)) for k in range(3)], e + 1
                q, r = divmod(i, 4)
                part = lambda w, k: w[:, q, r * 3 * P + k * P:r * 3 * P + (k + 1) * P]
                return [(part(w_hi, k), part(w_lo, k)) for k in range(3)], E0 + q + 1

            def down(n):
                j = n // S0N if n < 8 * S0N else 8 + (n - 8 * S0N) // S1N
                i = n - first_step(j)
                if i == 0 and j:
                    pe.wait_ge(y_out, j)
                first = i == 0
                if first and j >= 8:
                    pe.wait_ge(wTm_in, 16 * (j - 7))
                    nc.tensor.matmul(pacc[:, :], b2[:, :], wTm[:, :], start=True, stop=False).then_inc(b2_mm, 1)
                    first = False
                w, _ = weights(j, i)
                pe.wait_ge(lo_done, n + 1)
                mm3(pacc[:, :], w[2][0], w[2][1], h_hi[:, n % 4, :], h_lo[:, n % 4, :], start=first,
                    stop=i == steps(j) - 1).then_inc(down_mm, 1)

            pe.wait_ge(consts_in, 16)
            pe.wait_ge(ws_split, 1)
            for name, *args in norm_pieces("F1", 0):
                if name in mine:
                    mine[name](*args)
            for j in range(len(JOBS)):
                c = JOBS[j][1]
                s = slice(c * CT, (c + 1) * CT)
                pe.wait_ge(ln_lo, nth_norm(*JOBS[j]))
                for i in range(steps(j)):
                    n = first_step(j) + i
                    w, split = weights(j, i)
                    pe.wait_ge(w_split, split)
                    k = 0 if j in ATTENDS else n % 2
                    take(f"pg{k}")
                    mm3(pg[k][:, :], *w[0], n_hi[:, s], n_lo[:, s]).then_inc(gate_mm, 1)
                    reader[f"pg{k}"] = (gate_read, n - first_step(ATTENDS[0]) + 1) if j in ATTENDS else (silu_done, n + 1)
                    run(j, i, 0)
                    take(f"pu{k}")
                    mm3(pu[k][:, :], *w[1], n_hi[:, s], n_lo[:, s]).then_inc(up_mm, 1)
                    reader[f"pu{k}"] = (hid_done, n + 1)
                    run(j, i, 1)
                    if n >= LAG:
                        down(n - LAG)
                    run(j, i, 2)
            total = first_step(len(JOBS))
            for n in range(total - LAG, total):
                down(n)
            post_transpose(len(JOBS) - 1, 0)

        @block.scalar
        def _(act):
            def ln_hi_part(stage, c):
                n = nth_norm(stage, c)
                act.wait_ge(ln_T, n)
                nc.scalar.activation(norm_target(stage, c)[0], pa[:, :], ACT.Copy).then_inc(ln_hi, 1)

            def f_gap(stage, c):
                act.wait_ge(lg_act, nth_route(stage, c))
                nc.scalar.activation(egap[:, :], gap[:, :], ACT.Tanh, scale=0.5).then_inc(act_exp, 1)

            def g_exp(stage, c):
                act.wait_ge(lg_mm, nth_route(stage, c))
                nc.scalar.activation(lg[:, :, :], pb[:, 0:TI * E1].rearrange("p (t e) -> p t e", t=TI), ACT.Exp,
                                     scale=-1.0).then_inc(lg_read, 1)

            def route_out(stage, c):
                n = nth_route(stage, c)
                e = E0 if stage[0] == "F" else E1
                act.wait_ge(wT_mm, n)
                if n > 1:
                    act.wait_ge(w_stored, 16 * (n - 1))
                nc.scalar.activation(wT[0:e, :], pb[0:e, :], ACT.Copy).then_inc(wT_out, 1)
                act.wait_ge(wT_out, n)
                act.dma_start(w_scr[job_of(stage, c), 0:e, :], wT[0:e, :]).then_inc(w_stored, 16)

            def rec_gates(c, k):
                m = 2 * c + k
                act.wait_ge(setup_dve, 1)
                act.wait_ge(rec_mm, m + 1)
                if m:
                    act.wait_ge(rec_h, m)
                else:
                    act.wait_ge(w_split, E0)
                nc.scalar.activation(r_z, pa[:, :], ACT.Tanh, bias=bf_2[:, 2 * k:2 * k + 1], scale=0.5).then_inc(rec_sig, 1)
                nc.scalar.activation(r_g, pb[:, :], ACT.Tanh, bias=bf_2[:, 2 * k + 1:2 * k + 2],
                                     scale=0.5).then_inc(rec_sig, 1)
                act.wait_ge(rec_sig, 3 * m + 2)
                nc.scalar.activation(r_a, r_z, ACT.Copy, bias=0.5, scale=-0.5).then_inc(rec_sig, 1)

            def att_qk_hi(c, i):
                g, what = i // 2, i % 2
                act.wait_ge(qk_mm, 8 * c + i + 1)
                nth = 8 * c + i
                if nth >= 2:
                    act.wait_ge(qk_res, nth - 1)
                nc.scalar.activation(qk_hi[:, i % 2, :], (pa, pb)[what][:, :], ACT.Copy).then_inc(qk_rd, 1)

            def att_keys(c, u):
                b, g = divmod(u, HG)
                act.wait_ge(qk_res, 8 * c + 2 * g + 2)
                act.wait_ge(setup_pool, 1)
                if 8 * c + u >= 2:
                    act.wait_ge(s2_mm, 3 * (8 * c + u - 1))
                for h in (0, 1):
                    r = slice(32 * h, 32 * h + 32)
                    last = nc.scalar.activation(k_one[r, u % 2, h, :], k_r[r, g, b * SEQ:(b + 1) * SEQ].bitcast(f32), ACT.Copy)
                last.then_inc(k_apart1, 1)

            def att_exp_out(c, u, p):
                nth = nth_part(c, u, p)
                bank = (pb, pu[1])[nth % 2]
                act.wait_ge(s2_mm, nth + 1)
                if p == 0 and 8 * c + u:
                    act.wait_ge(pv_mm, 8 * c + u)
                nc.scalar.activation(prob[:, p * CT:(p + 1) * CT], bank[:, :], ACT.Exp, scale=SCALE).then_inc(s2_exp, 1)

            def att_pv_out(c, u):
                g = u % HG
                act.wait_ge(pv_mm, 8 * c + u + 1)
                if g == 0 and 8 * c + u:
                    act.wait_ge(o_T, 2 * ((8 * c + u) // HG))
                nc.scalar.activation(o_pad[:, g, :], pc[:, 0:SEQ], ACT.Copy).then_inc(pv_out, 1)

            def att_turn_out(c, b, t):
                k = 2 * (2 * c + b) + t
                act.wait_ge(o_T2, k + 1)
                if k:
                    act.wait_ge(att_y, k)
                nc.scalar.activation(o_fm[:, :], pc[:, 0:P], ACT.Copy).then_inc(o_T2out, 1)

            mine = dict(ln_hi=ln_hi_part, f_gap=f_gap, g_exp=g_exp, route_out=route_out, rec_gates=rec_gates,
                        att_qk_hi=att_qk_hi, att_keys=att_keys, att_exp_out=att_exp_out, att_pv_out=att_pv_out,
                        att_turn_out=att_turn_out)

            def round_hidden(n):
                act.wait_ge(weighted, n + 1)
                if n >= 4:
                    act.wait_ge(down_mm, n - 3)
                nc.scalar.activation(h_hi[:, n % 4, :], hid[:, n % 4, :], ACT.Copy).then_inc(hi_done, 1)

            def take_sum(j):
                act.wait_ge(down_mm, first_step(j + 1))
                if j:
                    act.wait_ge(y_turned, j)
                nc.scalar.activation(y_fm[:, :], pacc[:, :], ACT.Copy).then_inc(y_out, 1)

            act.dma_start(const[:, 0:C_MASK1], const_d[:, 0:C_MASK1]).then_inc(consts_in, 16)
            act.wait_ge(consts_in, 16)
            nc.scalar.activation(gate[:, 0, 0:1], const[:, C_EPS:C_EPS + 1], ACT.Silu).then_inc(table_in, 1)
            act.wait_ge(table_in, 1)
            for name, *args in norm_pieces("F1", 0):
                if name in mine:
                    mine[name](*args)
            for j in range(len(JOBS)):
                for i in range(steps(j)):
                    n = first_step(j) + i
                    if j and i == LAG:
                        take_sum(j - 1)
                    act.wait_ge(gate_mm, n + 1)
                    if n >= 2:
                        act.wait_ge(hid_done, n - 1)
                    bias = b13[:, 0, i:i + 1] if j >= 8 else 0.0
                    if j in ATTENDS:
                        nc.scalar.activation(gate[:, n % 2, :], pg[0][:, :], ACT.Tanh, bias=b1_half[:, i:i + 1],
                                             scale=0.5).then_inc(tanh_done, 1)
                        act.wait_ge(tanh_done, n - first_step(ATTENDS[0]) + 1)
                        nc.scalar.activation(gate[:, n % 2, :], gate[:, n % 2, :], ACT.Copy, bias=0.5,
                                             scale=0.5).then_inc(silu_done, 1)
                    else:
                        nc.scalar.activation(gate[:, n % 2, :], pg[n % 2][:, :], ACT.Silu, bias=bias).then_inc(silu_done, 1)
                    for name, *args in pieces_at(j, i, (0, 1, 2)):
                        if name in mine:
                            mine[name](*args)
                    if n >= 2:
                        round_hidden(n - 2)
            round_hidden(first_step(len(JOBS)) - 2)
            round_hidden(first_step(len(JOBS)) - 1)
            take_sum(len(JOBS) - 1)

        @block.gpsimd
        def _(pool):
            chain = [0]

            def link(ins):
                chain[0] += 1
                ins.then_inc(pool_chain, 1)
                pool.wait_ge(pool_chain, chain[0])

            def ln_rstd(stage, c):
                n = nth_norm(stage, c)
                pool.wait_ge(ln_mv, n)
                link(nc.gpsimd.tensor_tensor(rstd[:, :], mv[:, :, 1], const[:, C_EPS:C_EPS + TI], ALU.add))
                nc.gpsimd.tensor_tensor(rstd[:, :], rstd[:, :], const[:, C_POW:C_POW + TI], ALU.pow).then_inc(ln_rs, 1)

            mine = dict(ln_rstd=ln_rstd)

            def run(j, i, subs):
                for name, *args in pieces_at(j, i, subs):
                    if name in mine:
                        mine[name](*args)

            pool.wait_ge(consts_in, 16)
            ln_rstd("F1", 0)
            nc.gpsimd.memset(mpad[:, :, :], 0.0)
            nc.gpsimd.memset(k_one[:, :, :, :].bitcast(f32), 0.0)
            nc.gpsimd.memset(ones_row[:, :], 1.0)
            link(nc.gpsimd.memset(vpad[:, :, :, :], 0.0))
            nc.gpsimd.memset(vpad[:, :, :, HD:HD + 1], 1.0).then_inc(setup_pool, 1)
            for j in range(len(JOBS)):
                for i in range(steps(j)):
                    n = first_step(j) + i
                    run(j, i, (0,))
                    pool.wait_ge(hid_done, n + 1)
                    if j < 8:
                        load = n // FB
                    else:
                        load = 8 * E0 + (n - 8 * S0N)
                    pool.wait_ge(wbc_in[load % 4], 16 * (load // 4 + 1))
                    nc.gpsimd.tensor_tensor(hid[:, n % 4, :], hid[:, n % 4, :], wbc[:, load % 4, :],
                                            ALU.mult).then_inc(weighted, 1)
                    run(j, i, (1, 2))
                    if n >= 2 and lo_by_pool(n - 2):
                        k = n - 2
                        pool.wait_ge(hi_done, k + 1)
                        if not lo_by_pool(k - 1):
                            pool.wait_ge(lo_done, k)
                        nc.gpsimd.tensor_tensor(h_lo[:, k % 4, :], hid[:, k % 4, :], h_hi[:, k % 4, :].bitcast(f32),
                                                ALU.subtract).then_inc(lo_done, 1)

        @block.vector
        def _(dve):
            chain = [0]

            def link(ins):
                chain[0] += 1
                ins.then_inc(dve_chain, 1)
                dve.wait_ge(dve_chain, chain[0])

            tt, ts = nc.vector.tensor_tensor, nc.vector.tensor_scalar

            def ln_stats(stage, c):
                n = nth_norm(stage, c)
                x_ready(dve, stage, c)
                if n > 1:
                    dve.wait_ge(ln_rs, n - 1)
                for t in range(TI):
                    last = nc.vector.bn_stats(stats[:, t, :], x[:, c * TI + t, :])
                link(last)
                for t in range(TI):
                    last = nc.vector.bn_aggr(mv[:, t, :], stats[:, t, :])
                last.then_inc(ln_mv, 1)

            def ln_scale(stage, c):
                n = nth_norm(stage, c)
                dve.wait_ge(ln_rs, n)
                dve.wait_ge(ln_mv, n)
                if n > 1:
                    dve.wait_ge(ln_T, n - 1)
                for t in range(TI):
                    last = ts(nrm[:, t, :], x[:, c * TI + t, :], mv[:, t, 0:1], rstd[:, t:t + 1], ALU.subtract, ALU.mult)
                last.then_inc(ln_nrm, 1)

            def ln_lo_part(stage, c):
                n = nth_norm(stage, c)
                dve.wait_ge(ln_hi, n)
                hi, lo = norm_target(stage, c)
                tt(lo, pa[:, :], hi.bitcast(f32), ALU.subtract).then_inc(ln_lo, 1)

            def top_of(values, e):
                for t in range(TI):
                    last = nc.vector.max(top[:, t, :], values[:, t, 0:e])
                link(last)
                for t in range(TI):
                    last = nc.vector.max_index(topi[:, t, :], top[:, t, :], values[:, t, 0:e])
                link(last)
                link(nc.vector.tensor_copy(topf[:, :, :], topi[:, :, :]))

            def places(e, k):
                iota = const[:, C_IOTA:C_IOTA + e].unsqueeze(1).unsqueeze(3).to_broadcast([P, TI, e, k])
                want = topf[:, :, 0:k].unsqueeze(2).to_broadcast([P, TI, e, k])
                link(tt(hot[:, :, 0:e, 0:k], iota, want, ALU.is_equal))

            def f_top(stage, c):
                n = nth_route(stage, c)
                dve.wait_ge(lg_mm, n)
                nc.vector.tensor_copy(lg[:, :, 0:E0], pb[:, 0:TI * E0].rearrange("p (t e) -> p t e", t=TI)).then_inc(lg_read, 1)
                dve.wait_ge(lg_read, n)
                top_of(lg, E0)
                tt(gap[:, :], top[:, :, 1], top[:, :, 0], ALU.subtract).then_inc(lg_act, 1)

            def f_places(stage, c):
                places(E0, 2)

            def f_gates(stage, c):
                n = nth_route(stage, c)
                dve.wait_ge(act_exp, n)
                ts(gk[:, :, 0], egap[:, :], -0.5, 0.5, ALU.mult, ALU.add)
                link(ts(gk[:, :, 1], egap[:, :], 0.5, 0.5, ALU.mult, ALU.add))
                link(tt(hot[:, :, 0:E0, 0:2], hot[:, :, 0:E0, 0:2],
                        gk[:, :, :].unsqueeze(2).to_broadcast([P, TI, E0, 2]), ALU.mult))
                if n > 1:
                    dve.wait_ge(wT_mm, n - 1)
                nc.vector.tensor_reduce(wtm[:, :, 0:E0], hot[:, :, 0:E0, 0:2], AX.X, ALU.add).then_inc(w_tm, 1)

            def g_sigmoid(stage, c):
                n = nth_route(stage, c)
                dve.wait_ge(lg_read, n)
                link(ts(lg[:, :, :], lg[:, :, :], 1.0, None, ALU.add))
                link(nc.vector.reciprocal(sc[:, :, :], lg[:, :, :]))

            s4 = sc[:, :, :].rearrange("p t (g e) -> p t g e", g=GR)
            m4 = lg[:, :, :].rearrange("p t (g e) -> p t g e", g=GR)

            def g_groups(stage, c):
                link(nc.vector.tensor_reduce(gmax[:, :, :], s4, AX.X, ALU.max))
                other = gmax[:, :, :].unsqueeze(2).to_broadcast([P, TI, GR, GR])
                own = gmax[:, :, :].unsqueeze(3).to_broadcast([P, TI, GR, GR])
                before = const[:, C_TRI:C_TRI + GR * GR].rearrange("p (a b) -> p a b", a=GR).unsqueeze(1) \
                    .to_broadcast([P, TI, GR, GR])
                link(tt(gcmp[:, :, :, :], other, own, ALU.is_gt))
                link(tt(gcmq[:, :, :, :], other, own, ALU.is_equal))
                link(tt(gcmq[:, :, :, :], gcmq[:, :, :, :], before, ALU.mult))
                link(tt(gcmp[:, :, :, :], gcmp[:, :, :, :], gcmq[:, :, :, :], ALU.add))

            def g_choose(stage, c):
                link(nc.vector.tensor_reduce(gsel[:, :, :], gcmp[:, :, :, :], AX.X, ALU.add))
                link(ts(gsel[:, :, :], gsel[:, :, :], 1.5, None, ALU.is_lt))
                link(ts(gsel1[:, :, :], gsel[:, :, :], 1.0, None, ALU.subtract))
                link(tt(m4, s4, gsel[:, :, :].unsqueeze(3).to_broadcast([P, TI, GR, 4]), ALU.mult))
                link(tt(m4, m4, gsel1[:, :, :].unsqueeze(3).to_broadcast([P, TI, GR, 4]), ALU.add))

            def g_top(stage, c):
                top_of(lg, E1)

            def g_places(stage, c):
                places(E1, 4)

            def g_weights(stage, c):
                n = nth_route(stage, c)
                link(nc.vector.tensor_reduce(lg[:, :, :], hot[:, :, :, :], AX.X, ALU.add))
                link(tt(sc[:, :, :], sc[:, :, :], lg[:, :, :], ALU.mult))
                link(nc.vector.tensor_reduce(den[:, :], sc[:, :, :], AX.X, ALU.add))
                link(nc.vector.reciprocal(gap[:, :], den[:, :]))
                link(ts(gap[:, :], gap[:, :], 2.5, None, ALU.mult))
                dve.wait_ge(wT_mm, n - 1)
                tt(wtm[:, :, :], sc[:, :, :], gap[:, :].unsqueeze(2).to_broadcast([P, TI, E1]), ALU.mult).then_inc(w_tm, 1)

            def post_add(j, _):
                c = JOBS[j][1]
                dve.wait_ge(y_turned, j + 1)
                xs = x[:, c * TI:(c + 1) * TI, :].rearrange("p t d -> p (t d)")
                nc.vector.scalar_tensor_tensor(xs, pc[:, :], 0.5, xs, ALU.mult, ALU.add).then_inc(x_added, 1)

            def rec_input(c, k):
                m = 2 * c + k
                dve.wait_ge(rec_sig, 3 * (m + 1))
                link(ts(r_g, r_g, 0.5, 0.5, ALU.mult, ALU.add))
                nc.vector.scalar_tensor_tensor(r_g, pb[:, :], bf_up[:, 2 * k + 1:2 * k + 2], r_g, ALU.add,
                                               ALU.max).then_inc(rec_read, 1)
                dve.wait_ge(rec_read, m + 1)
                link(nc.vector.scalar_tensor_tensor(r_g, r_z, 1.0, r_g, ALU.add, ALU.mult))

            def rec_scan(c, k):
                if c:
                    dve.wait_ge(rec_y, c)
                for b in range(NB):
                    s = slice(b * SEQ, (b + 1) * SEQ)
                    last = nc.vector.tensor_tensor_scan(r_h[k][:, s], r_a[:, s], r_g[:, s], 1.0, ALU.mult, ALU.add)
                last.then_inc(rec_h, 1)

            def rec_add(c, _):
                dve.wait_ge(rec_y, c + 1)
                xs = x[:, c * TI:(c + 1) * TI, :].rearrange("p t d -> p (t d)")
                nc.vector.scalar_tensor_tensor(xs, pc[:, :], 0.5, xs, ALU.mult, ALU.add).then_inc(rec_x, 1)

            def att_qk_split(c, i):
                g, what = i // 2, i % 2
                dve.wait_ge(qk_rd, 8 * c + i + 1)
                if c:
                    unit = UNITS * (c - 1) + UNITS - HG + g + 1
                    if what:
                        dve.wait_ge(k_apart1, unit)
                        dve.wait_ge(k_apart2, unit)
                    else:
                        dve.wait_ge(s1_mm, 3 * unit)
                        dve.wait_ge(q_shift, unit)
                ml = const[:, (C_MLQ, C_MLK)[what]:(C_MLQ, C_MLK)[what] + 1]
                nc.vector.scalar_tensor_tensor((q_r, k_r)[what][:, g, :], qk_hi[:, i % 2, :].bitcast(f32), ml,
                                               (pa, pb)[what][:, :], ALU.mult, ALU.add).then_inc(qk_res, 1)

            def att_v_out(c, b):
                dve.wait_ge(v_mm, 2 * c + b + 1)
                if 2 * c + b:
                    dve.wait_ge(pv_mm, 4 * (2 * c + b))
                for t in range(SEQ // P):
                    last = tt(vpad[:, t, :, 0:HD], pc[:, t * P:(t + 1) * P].rearrange("p (h d) -> p h d", h=H),
                              bv[:, :].rearrange("p (h d) -> p h d", h=H), ALU.add)
                last.then_inc(v_out, 1)

            def att_keys(c, u):
                b, g = divmod(u, HG)
                dve.wait_ge(qk_res, 8 * c + 2 * g + 2)
                dve.wait_ge(setup_pool, 1)
                if 8 * c + u >= 2:
                    dve.wait_ge(s2_mm, 3 * (8 * c + u - 1))
                for h in (2, 3):
                    r = slice(32 * h, 32 * h + 32)
                    last = nc.vector.tensor_copy(k_one[r, u % 2, h, :], k_r[r, g, b * SEQ:(b + 1) * SEQ])
                last.then_inc(k_apart2, 1)

            def att_max_out(c, u, p):
                nth = nth_part(c, u, p)
                bank = (pa, pg[1])[nth % 2]
                dve.wait_ge(s1_mm, nth + 1)
                if p == 0 and 8 * c + u:
                    dve.wait_ge(m_T, 8 * c + u)
                k, w = (4, P) if p == 0 else (2, SEQ)
                h0 = 0 if p < 2 else 2
                out = mpad[:, min(p, 1), :].rearrange("p (h r) -> p h r", r=32)[:, h0:h0 + k, MROW]
                nc.vector.tensor_reduce(out, bank[:, :].rearrange("p (h w) -> p h w", w=w), AX.X, ALU.max,
                                        negate=True).then_inc(s1_max, 1)

            def att_shift_out(c, u):
                b, g = divmod(u, HG)
                dve.wait_ge(m_T, 8 * c + u + 1)
                if 8 * c + u >= 2:
                    dve.wait_ge(s2_mm, 3 * (8 * c + u - 1))
                bank = (pb, pu[1])[nth_part(c, u, 0) % 2]
                tt(qs_r[:, u % 2, :], bank[:, 0:SEQ], q_r[:, g, b * SEQ:(b + 1) * SEQ].bitcast(f32), ALU.add).then_inc(q_shift, 1)

            def att_norm(c, b, t):
                k = 2 * (2 * c + b) + t
                dve.wait_ge(o_T, k + 1)
                heads = pc[:, :].rearrange("p (h r) -> p h r", r=32)
                link(nc.vector.reciprocal(rden[:, :], heads[:, :, HD]))
                if k:
                    dve.wait_ge(o_T2, k)
                tt(o_tm[:, :, :], heads[:, :, 0:HD], rden[:, :].unsqueeze(2).to_broadcast([P, H, HD]), ALU.mult).then_inc(o_nrm, 1)

            def att_add(c, b, t):
                k = 2 * (2 * c + b) + t
                dve.wait_ge(att_y, k + 1)
                xs = x[:, c * TI + 2 * b + t, :]
                tt(xs, pc[:, 0:P], xs, ALU.add).then_inc(att_x, 1)

            mine = dict(ln_stats=ln_stats, ln_scale=ln_scale, ln_lo=ln_lo_part, f_top=f_top, f_places=f_places,
                        f_gates=f_gates, g_sigmoid=g_sigmoid, g_groups=g_groups, g_choose=g_choose, g_top=g_top,
                        g_places=g_places, g_weights=g_weights, post_add=post_add, rec_input=rec_input,
                        rec_scan=rec_scan, rec_add=rec_add, att_qk_split=att_qk_split, att_v_out=att_v_out,
                        att_keys=att_keys, att_max_out=att_max_out, att_shift_out=att_shift_out,
                        att_norm=att_norm, att_add=att_add)

            def run(j, i, subs):
                for name, *args in pieces_at(j, i, subs):
                    if name in mine:
                        mine[name](*args)

            def split_block(k, hi, lo, width):
                dve.wait_ge(staged[k % 2], 16 * (k // 2 + 1))
                src = arena[:, k % 2, 0:width]
                link(nc.vector.tensor_copy(hi, src))
                tt(lo, src, hi.bitcast(f32), ALU.subtract).then_inc(w_split, 1)

            def setup():
                dve.wait_ge(smalls_in, 16 * len(smalls))
                nc.vector.tensor_copy(ident_b[:, :], ident)
                nc.vector.tensor_copy(mask1_b[:, :], const[:, C_MASK1:C_MASK1 + P])
                nc.vector.tensor_copy(mask2_b[:, :], const[:, C_MASK2:C_MASK2 + P])
                ts(bf_2[:, :], bf[:, :], 0.5, None, ALU.mult)
                ts(bf_up[:, :], bf[:, :], 0.5, None, ALU.add)
                ts(b1_half[:, :], b13[:, 0, :], 0.5, None, ALU.mult).then_inc(setup_dve, 1)
                dve.wait_ge(setup_dve, 1)

            dve.wait_ge(consts_in, 16)
            ln_stats("F1", 0)
            ln_scale("F1", 0)
            dve.wait_ge(staged[0], 16)
            link(nc.vector.tensor_copy(ws_hi[:, :], arena[:, 0, 0:536]))
            tt(ws_lo[:, :], arena[:, 0, 0:536], ws_hi[:, :].bitcast(f32), ALU.subtract).then_inc(ws_split, 1)
            ln_lo_part("F1", 0)

            def more_weights(j, i):
                if j == 0 and i == 2:
                    setup()
                if j == 0 and i % FB == 0 and i // FB + 1 < E0:
                    e = i // FB + 1
                    split_block(e + 1, w_hi[:, e, :], w_lo[:, e, :], 3 * F0)
                if j == 7 and i in (8, 12, 16, 20):
                    q = i // 4 - 2
                    dve.wait_ge(down_mm, first_step(7) + FB * (q + 1))
                    split_block(E0 + 1 + q, w_hi[:, q, :], w_lo[:, q, :], 3 * F0)
                if j == 8 and i == 4:
                    dve.wait_ge(down_mm, first_step(8))
                    split_block(E0 + 5, wa_hi, wa_lo, 1152)
                if j == 8 and i == 8:
                    dve.wait_ge(staged[E0 % 2], 16 * ((E0 + 6) // 2 + 1))
                    src = arena[0:2, E0 % 2, :]
                    nc.vector.tensor_copy(pos_r, src[:, 1024:1536])
                    link(nc.vector.tensor_copy(aug_hi, src[:, 0:1024]))
                    tt(aug_lo, src[:, 0:1024], aug_hi.bitcast(f32), ALU.subtract).then_inc(w_split, 1)

            def rest_of_hidden(n):
                if lo_by_pool(n):
                    return
                dve.wait_ge(hi_done, n + 1)
                if n and lo_by_pool(n - 1):
                    dve.wait_ge(lo_done, n)
                tt(h_lo[:, n % 4, :], hid[:, n % 4, :], h_hi[:, n % 4, :].bitcast(f32), ALU.subtract).then_inc(lo_done, 1)

            split_block(1, w_hi[:, 0, :], w_lo[:, 0, :], 3 * F0)
            for j in range(len(JOBS)):
                for i in range(steps(j)):
                    n = first_step(j) + i
                    run(j, i, (0,))
                    dve.wait_ge(silu_done, n + 1)
                    if j in ATTENDS:
                        nc.vector.scalar_tensor_tensor(gate[:, n % 2, :], pg[0][:, :], b13[:, 0, i:i + 1],
                                                       gate[:, n % 2, :], ALU.add, ALU.mult).then_inc(gate_read, 1)
                        dve.wait_ge(gate_read, n - first_step(ATTENDS[0]) + 1)
                    dve.wait_ge(up_mm, n + 1)
                    if n >= 4:
                        dve.wait_ge(lo_done, n - 3)
                    if j < 8:
                        tt(hid[:, n % 4, :], pu[n % 2][:, :], gate[:, n % 2, :], ALU.mult).then_inc(hid_done, 1)
                    else:
                        k = 0 if j in ATTENDS else n % 2
                        nc.vector.scalar_tensor_tensor(hid[:, n % 4, :], pu[k][:, :], b13[:, 1, i:i + 1],
                                                       gate[:, n % 2, :], ALU.add, ALU.mult).then_inc(hid_done, 1)
                    run(j, i, (1, 2))
                    if n >= 2:
                        rest_of_hidden(n - 2)
                    more_weights(j, i)
            rest_of_hidden(first_step(len(JOBS)) - 2)
            rest_of_hidden(first_step(len(JOBS)) - 1)
            post_add(len(JOBS) - 1, 0)

        @block.sync
        def _(sp):
            def load_x(c):
                sp.dma_start(x[:, c * TI:(c + 1) * TI, :],
                             x_d[c * CT:(c + 1) * CT, :].rearrange("(t p) d -> p t d", p=P)).then_inc(x_in[c], 16)

            def stage(k):
                if k == 2:
                    sp.wait_ge(ws_split, 1)
                if k >= 3:
                    sp.wait_ge(w_split, k - 2)
                if k == E0 + 1:
                    sp.wait_ge(rec_y, CH)
                src = ws_d if k == 0 else wf_d[k - 1] if k <= E0 else wg_d[k - E0 - 1] if k < E0 + 5 \
                    else wa_d if k == E0 + 5 else aug_d
                sp.dma_start(arena[0:src.shape[0], k % 2, 0:src.shape[1]], src).then_inc(staged[k % 2], 16)

            def store(j):
                c = JOBS[j][1]
                sp.wait_ge(x_added, j + 1)
                sp.dma_start(out_d[c * CT:(c + 1) * CT, :].rearrange("(t p) d -> p t d", p=P),
                             x[:, c * TI:(c + 1) * TI, :]).then_inc(stored, 16)

            load_x(0)
            stage(0)
            stage(1)
            load_x(1)
            for dst, src in smalls:
                sp.dma_start(dst, src).then_inc(smalls_in, 16)
            stage(2)
            for c in range(2, CH):
                load_x(c)
            load = 0
            for j in range(len(JOBS)):
                sp.wait_ge(w_stored, 16 * nth_route(*JOBS[j]))
                if j >= 8:
                    if j > 8:
                        sp.wait_ge(b2_mm, j - 8)
                    sp.dma_start(wTm[:, :], w_scr[j]).then_inc(wTm_in, 16)
                for e in range(E0 if j < 8 else E1):
                    if load >= 4:
                        old = load - 4
                        done = FB * (old + 1) if old < 8 * E0 else 8 * S0N + old - 8 * E0 + 1
                        sp.wait_ge(weighted, done)
                    sp.dma_start(wbc[:, load % 4, :], w_scr[j, e:e + 1, :].to_broadcast([P, CT])).then_inc(wbc_in[load % 4], 16)
                    load += 1
                    if j == 0 and e + 3 <= E0:
                        stage(e + 3)
                    if j == 7 and e in (0, 1):
                        stage(E0 + 1 + e)
                    if j == 7 and e in (4, 5):
                        stage(E0 - 1 + e)
                    if j == 8 and e in (0, 1):
                        stage(E0 + 5 + e)
                if j >= 13:
                    store(j - 1)
            store(len(JOBS) - 1)
            sp.wait_ge(stored, 16 * CH)


def _constants():
    c = np.zeros((P, C_END), np.float32)
    c[:, C_ID:C_ID + P] = np.eye(P)
    c[:, C_IOTA:C_IOTA + E1] = np.arange(E1)
    c[:, C_TRI:C_TRI + GR * GR] = np.tril(np.ones((GR, GR)), -1).reshape(-1)
    r = np.arange(P) % 32
    c[:, C_MLQ] = -((r >= 2 * HD) & (r < 3 * HD) | (r == 25) | (r == 27)).astype(np.float32)
    c[:, C_MLK] = -((r >= HD) & (r < 2 * HD)).astype(np.float32)
    c[:, C_POW:C_POW + TI] = -0.5
    c[:, C_EPS:C_EPS + TI] = EPS
    upper = np.triu(np.full((P, P), -1e30, np.float32), 1)
    c[:, C_MASK1:C_MASK1 + P] = upper
    c[:, C_MASK2:C_MASK2 + P] = upper.T
    return c


def _by_head(w):
    lead = w.shape[:-1]
    out = np.zeros(lead + (HG, 4, 4, HD), np.float32)
    out[..., 0:3, :] = w.reshape(lead + (HG, 4, 1, HD))
    return out.reshape(lead + (HG * P,))


def _added_rows(bq, bk):
    aug = np.zeros((2, 2, HG, 4, 32), np.float32)
    aug[0, 0] = _by_head(bq).reshape(HG, 4, 32)
    aug[0, 1] = _by_head(bk).reshape(HG, 4, 32)
    slope = (np.float32(2.0 ** (-8.0 / H)) ** np.arange(1, H + 1, dtype=np.float32)).reshape(HG, 4)
    slope = slope * np.sqrt(np.float32(HD))
    aug[0, 0, :, :, 24] = aug[0, 0, :, :, 25] = slope
    aug[1, 1, :, :, 24:26] = 1.0
    aug[1, 0, :, :, 26] = aug[1, 0, :, :, 27] = -slope
    aug[0, 1, :, :, 26:MROW + 1] = 1.0
    return aug.reshape(2, -1)


def kernel(**inputs):
    import concourse.bacc as bacc
    from concourse.bass_utils import run_bass_kernel_spmd

    i = {k: np.asarray(v) for k, v in inputs.items()}
    wf = np.zeros((E0, P, 3, F0), np.float32)
    wf[:, :, 0] = i["L0_ffn_W_gate"].transpose(0, 2, 1)
    wf[:, :, 1] = i["L0_ffn_W_up"].transpose(0, 2, 1)
    wf[:, :, 2] = i["L0_ffn_W_down"].reshape(E0, D, FB, P).transpose(0, 3, 2, 1).reshape(E0, P, F0)
    wg = np.stack([i["L1_ffn_W1"].transpose(0, 2, 1), i["L1_ffn_W3"].transpose(0, 2, 1),
                   i["L1_ffn_W2"].transpose(0, 2, 1)], 2)
    wg = wg.reshape(4, 4, P, 3 * P).transpose(0, 2, 1, 3)
    wz = np.zeros((P, 4, P), np.float32)
    bf = np.zeros((P, 4), np.float32)
    wfT, b_f = i["L0_attn_W_f"].T, i["L0_attn_b_f"]
    wfd = np.zeros((P, 2, D), np.float32)
    for k, (a, b) in enumerate(((0, P), (P, EH))):
        wz[:, 2 * k, 0:b - a], wz[:, 2 * k + 1, 0:b - a] = wfT[:, a:b], wfT[:, EH + a:EH + b]
        bf[0:b - a, 2 * k], bf[0:b - a, 2 * k + 1] = b_f[a:b], b_f[EH + a:EH + b]
        wfd[0:b - a, k] = i["L0_attn_W_down"].T[a:b]
    ws = np.concatenate([wz.reshape(P, 4 * P), i["L0_ffn_W_router"].T, i["L1_ffn_Wg"].T], 1)
    wa = np.concatenate([_by_head(i["L1_attn_Wq"]), _by_head(i["L1_attn_Wk"]), i["L1_attn_Wv"]], 1)
    pos = np.stack([np.ones(CT, np.float32), np.tile(np.arange(SEQ, dtype=np.float32), NB)])
    arrays = dict(
        x=i["L0_attn_x"].reshape(TOK, D), const=_constants(), wf=wf.reshape(E0, P, 3 * F0),
        wg=wg.reshape(4, P, 12 * P), ws=ws, wa=wa, wfd=wfd, wo=i["L1_attn_Wo"], bf=bf,
        b13=np.stack([i["L1_ffn_b1"].T, i["L1_ffn_b3"].T], 1), b2=i["L1_ffn_b2"],
        aug=np.concatenate([_added_rows(i["L1_attn_bq"], i["L1_attn_bk"]), pos], 1),
        bv=i["L1_attn_bv"].reshape(1, D), bo=i["L1_attn_bo"].reshape(1, D))
    nc = bacc.Bacc("TRN2", target_bir_lowering=False, num_devices=1)
    feed, args = {}, []
    for name, a in arrays.items():
        feed[f"in_{name}"] = np.ascontiguousarray(a)
        args.append(nc.dram_tensor(f"in_{name}", a.shape, mybir.dt.from_np(a.dtype), kind="ExternalInput").ap())
    args.append(nc.dram_tensor("out_x", (TOK, D), mybir.dt.float32, kind="ExternalOutput").ap())
    build(nc, *args)
    r = run_bass_kernel_spmd(nc, [feed], core_ids=[0])
    return r.results[0]["out_x"].reshape(TOK // SEQ, SEQ, D)
```
